# Optimizing a Trainium2 kernel written in Bass

```python
import numpy as np
import jax
import jax.numpy as jnp

def _softmax(x, axis=-1):
    return jax.nn.softmax(x, axis=axis)

def _gelu(x):
    return jax.nn.gelu(x, approximate=True)

def _silu(x):
    return jax.nn.silu(x)

def _sigmoid(x):
    return jax.nn.sigmoid(x)

def _layernorm(x, axis=-1, eps=1e-05):
    m = jnp.mean(x, axis=axis, keepdims=True)
    v = jnp.var(x, axis=axis, keepdims=True)
    return (x - m) / jnp.sqrt(v + eps)

def _scatter_add(tgt, idx, src, axis=0):
    return tgt.at[idx].add(src)

def _segment_sum(src, seg, n):
    return jax.ops.segment_sum(src, seg, n)
kernel_name = 'mk_vit_tower_cls_d1_tok_img1024_r4_d35e48'

def setup_inputs(seed: int=0):
    np.random.seed(seed)
    _w = jnp.asarray

    def _rec_inputs():
        import jax
        import jax.numpy as jnp
        _rk = jax.random.key(seed)
        x = -7.10856e-05 + 0.999911 * jax.random.normal(jax.random.fold_in(_rk, 1), (4, 512, 256, 4), jnp.float32)
        cls_tok = 0.02 * jax.random.normal(jax.random.fold_in(_rk, 5), (1, 1, 256), jnp.float32)
        return (x, cls_tok)
    x, cls_tok = _rec_inputs()

    def _L0_tok_setup():
        import jax, jax.numpy as jnp
        import numpy as np
        B, S, D, E = (8, 512, 256, 4)
        DE = 512
        key = jax.random.key(seed)
        k1, k2, k3, k4 = jax.random.split(key, 4)
        scale = 1.0 / np.sqrt(D)
        return {'expert_id': 0, 'freq_features': jax.random.normal(k1, (B, S, D, E), dtype=jnp.float32), 'W0': jax.random.normal(k2, (DE, D), dtype=jnp.float32) * scale, 'W1': jax.random.normal(k3, (DE, D), dtype=jnp.float32) * scale, 'Wo': jax.random.normal(k4, (D, DE), dtype=jnp.float32) * (1.0 / np.sqrt(DE))}
    _L0_tok_all = _L0_tok_setup()
    _L0_tok_in = {k: v for k, v in _L0_tok_all.items() if k in ('W0', 'W1', 'Wo')}
    del _L0_tok_all

    def _L0_attn_setup():
        import jax, jax.numpy as jnp
        import numpy as np
        import math
        N_EMBD = 256
        N_HEAD = 16
        HEAD_SIZE = N_EMBD // N_HEAD
        LAYER_IDX = 2
        LAMBDA_INIT = 0.8 - 0.6 * math.exp(-0.3 * (LAYER_IDX - 1))
        LN_EPS = 1e-05
        B, T = (4, 256)
        key = jax.random.key(seed)
        ks = jax.random.split(key, 11)
        s = 0.02
        return {'x': jax.random.normal(ks[0], (B, T, N_EMBD), dtype=jnp.float32), 'Wq1': jax.random.normal(ks[1], (N_EMBD, N_EMBD), dtype=jnp.float32) * s, 'Wq2': jax.random.normal(ks[2], (N_EMBD, N_EMBD), dtype=jnp.float32) * s, 'Wk1': jax.random.normal(ks[3], (N_EMBD, N_EMBD), dtype=jnp.float32) * s, 'Wk2': jax.random.normal(ks[4], (N_EMBD, N_EMBD), dtype=jnp.float32) * s, 'Wv': jax.random.normal(ks[5], (N_EMBD, 2 * N_EMBD), dtype=jnp.float32) * s, 'Wc': jax.random.normal(ks[6], (2 * N_EMBD, N_EMBD), dtype=jnp.float32) * s, 'lq1': jax.random.normal(ks[7], (N_HEAD, HEAD_SIZE), dtype=jnp.float32) * 0.1, 'lk1': jax.random.normal(ks[8], (N_HEAD, HEAD_SIZE), dtype=jnp.float32) * 0.1, 'lq2': jax.random.normal(ks[9], (N_HEAD, HEAD_SIZE), dtype=jnp.float32) * 0.1, 'lk2': jax.random.normal(ks[10], (N_HEAD, HEAD_SIZE), dtype=jnp.float32) * 0.1}
    _L0_attn_all = _L0_attn_setup()
    _L0_attn_in = {k: v for k, v in _L0_attn_all.items() if k in ('Wq1', 'Wq2', 'Wk1', 'Wk2', 'Wv', 'Wc', 'lq1', 'lk1', 'lq2', 'lk2')}
    del _L0_attn_all

    def _L0_ffn_setup():
        import jax, jax.numpy as jnp
        import numpy as np
        H = 256
        E = 64
        K = 8
        G = 8
        TOPK_GROUP = 4
        I_MOE = 128
        I_SHARED = 512
        SCALE = 2.5

        def relu2(x):
            return jnp.square(jax.nn.relu(x))

        def _route(xf, router_w, correction_bias):
            T = xf.shape[0]
            logits = xf @ router_w.T
            scores = jax.nn.sigmoid(logits)
            sfc = scores + correction_bias[None, :]
            grp = sfc.reshape(T, G, E // G)
            top2, _ = jax.lax.top_k(grp, 2)
            group_scores = top2.sum(-1)
            _, gidx = jax.lax.top_k(group_scores, TOPK_GROUP)
            gmask = jnp.zeros((T, G), sfc.dtype).at[jnp.arange(T)[:, None], gidx].set(1.0)
            emask = jnp.repeat(gmask, E // G, axis=1)
            masked = jnp.where(emask > 0, sfc, 0.0)
            _, tidx = jax.lax.top_k(masked, K)
            tw = jnp.take_along_axis(scores, tidx, axis=1)
            tw = tw / (tw.sum(-1, keepdims=True) + 1e-20)
            return (tidx, tw * SCALE)
        key = jax.random.key(seed)
        ks = jax.random.split(key, 7)
        x = jax.random.normal(ks[0], (2, 256, H), dtype=jnp.float32)
        router_w = jax.random.normal(ks[1], (E, H), dtype=jnp.float32) * 0.02
        correction_bias = jax.random.normal(ks[2], (E,), dtype=jnp.float32) * 0.01
        up_w = jax.random.normal(ks[3], (E, H, I_MOE), dtype=jnp.float32) * 0.02
        down_w = jax.random.normal(ks[4], (E, I_MOE, H), dtype=jnp.float32) * 0.02
        shared_up_w = jax.random.normal(ks[5], (H, I_SHARED), dtype=jnp.float32) * 0.02
        shared_down_w = jax.random.normal(ks[6], (I_SHARED, H), dtype=jnp.float32) * 0.02
        return {'x': x, 'router_w': router_w, 'correction_bias': correction_bias, 'up_w': up_w, 'down_w': down_w, 'shared_up_w': shared_up_w, 'shared_down_w': shared_down_w}
    _L0_ffn_all = _L0_ffn_setup()
    _L0_ffn_in = {k: v for k, v in _L0_ffn_all.items() if k in ('router_w', 'correction_bias', 'up_w', 'down_w', 'shared_up_w', 'shared_down_w')}
    del _L0_ffn_all
    return {'x': x, 'cls_tok': cls_tok, 'L0_tok_W0': _L0_tok_in['W0'], 'L0_tok_W1': _L0_tok_in['W1'], 'L0_tok_Wo': _L0_tok_in['Wo'], 'L0_attn_Wq1': _L0_attn_in['Wq1'], 'L0_attn_Wq2': _L0_attn_in['Wq2'], 'L0_attn_Wk1': _L0_attn_in['Wk1'], 'L0_attn_Wk2': _L0_attn_in['Wk2'], 'L0_attn_Wv': _L0_attn_in['Wv'], 'L0_attn_Wc': _L0_attn_in['Wc'], 'L0_attn_lq1': _L0_attn_in['lq1'], 'L0_attn_lk1': _L0_attn_in['lk1'], 'L0_attn_lq2': _L0_attn_in['lq2'], 'L0_attn_lk2': _L0_attn_in['lk2'], 'L0_ffn_router_w': _L0_ffn_in['router_w'], 'L0_ffn_correction_bias': _L0_ffn_in['correction_bias'], 'L0_ffn_up_w': _L0_ffn_in['up_w'], 'L0_ffn_down_w': _L0_ffn_in['down_w'], 'L0_ffn_shared_up_w': _L0_ffn_in['shared_up_w'], 'L0_ffn_shared_down_w': _L0_ffn_in['shared_down_w']}

def reference(x, cls_tok, L0_tok_W0, L0_tok_W1, L0_tok_Wo, L0_attn_Wq1, L0_attn_Wq2, L0_attn_Wk1, L0_attn_Wk2, L0_attn_Wv, L0_attn_Wc, L0_attn_lq1, L0_attn_lk1, L0_attn_lq2, L0_attn_lk2, L0_ffn_router_w, L0_ffn_correction_bias, L0_ffn_up_w, L0_ffn_down_w, L0_ffn_shared_up_w, L0_ffn_shared_down_w):
    import jax
    import jax.numpy as jnp

    def _L0_tok_ref(expert_id, freq_features, W0, W1, Wo):
        import jax, jax.numpy as jnp
        import numpy as np
        B, S, D, E = (8, 512, 256, 4)
        DE = 512
        x = freq_features[:, :, :, expert_id]
        gate = jax.nn.relu(jnp.einsum('bsd,ed->bse', x, W0))
        up = jnp.einsum('bsd,ed->bse', x, W1)
        hidden = gate * up
        out = jnp.einsum('bse,de->bsd', hidden, Wo)
        return out

    def _L0_attn_ref(x, Wq1, Wq2, Wk1, Wk2, Wv, Wc, lq1, lk1, lq2, lk2):
        import jax, jax.numpy as jnp
        import numpy as np
        import math
        N_EMBD = 256
        N_HEAD = 16
        HEAD_SIZE = N_EMBD // N_HEAD
        LAYER_IDX = 2
        LAMBDA_INIT = 0.8 - 0.6 * math.exp(-0.3 * (LAYER_IDX - 1))
        LN_EPS = 1e-05
        B, T = (4, 256)
        Bx, Tx, C = x.shape
        H, hs = (N_HEAD, HEAD_SIZE)
        scale = 1.0 / math.sqrt(hs)
        q1 = (x @ Wq1).reshape(Bx, Tx, H, hs)
        q2 = (x @ Wq2).reshape(Bx, Tx, H, hs)
        k1 = (x @ Wk1).reshape(Bx, Tx, H, hs)
        k2 = (x @ Wk2).reshape(Bx, Tx, H, hs)
        v = (x @ Wv).reshape(Bx, Tx, H, 2 * hs)
        att1 = jnp.einsum('bqhd,bkhd->bhqk', q1, k1) * scale
        att2 = jnp.einsum('bqhd,bkhd->bhqk', q2, k2) * scale
        causal = jnp.tril(jnp.ones((Tx, Tx), dtype=bool))
        neg_inf = jnp.float32(-jnp.inf)
        att1 = jnp.where(causal, att1, neg_inf)
        att2 = jnp.where(causal, att2, neg_inf)
        a1 = jax.nn.softmax(att1, axis=-1)
        a2 = jax.nn.softmax(att2, axis=-1)
        lam1 = jnp.exp(jnp.sum(lq1 * lk1, axis=-1))
        lam2 = jnp.exp(jnp.sum(lq2 * lk2, axis=-1))
        lam_full = lam1 - lam2 + LAMBDA_INIT
        att = a1 - lam_full[None, :, None, None] * a2
        y = jnp.einsum('bhqk,bkhd->bqhd', att, v)
        mu = jnp.mean(y, axis=-1, keepdims=True)
        var = jnp.mean(jnp.square(y - mu), axis=-1, keepdims=True)
        y = (y - mu) / jnp.sqrt(var + LN_EPS)
        y = y * (1.0 - LAMBDA_INIT)
        y = y.reshape(Bx, Tx, 2 * C)
        return y @ Wc

    def _L0_ffn_ref(x, router_w, correction_bias, up_w, down_w, shared_up_w, shared_down_w):
        import jax, jax.numpy as jnp
        import numpy as np
        H = 256
        E = 64
        K = 8
        G = 8
        TOPK_GROUP = 4
        I_MOE = 128
        I_SHARED = 512
        SCALE = 2.5

        def relu2(x):
            return jnp.square(jax.nn.relu(x))

        def _route(xf, router_w, correction_bias):
            T = xf.shape[0]
            logits = xf @ router_w.T
            scores = jax.nn.sigmoid(logits)
            sfc = scores + correction_bias[None, :]
            grp = sfc.reshape(T, G, E // G)
            top2, _ = jax.lax.top_k(grp, 2)
            group_scores = top2.sum(-1)
            _, gidx = jax.lax.top_k(group_scores, TOPK_GROUP)
            gmask = jnp.zeros((T, G), sfc.dtype).at[jnp.arange(T)[:, None], gidx].set(1.0)
            emask = jnp.repeat(gmask, E // G, axis=1)
            masked = jnp.where(emask > 0, sfc, 0.0)
            _, tidx = jax.lax.top_k(masked, K)
            tw = jnp.take_along_axis(scores, tidx, axis=1)
            tw = tw / (tw.sum(-1, keepdims=True) + 1e-20)
            return (tidx, tw * SCALE)
        B, S, Hd = x.shape
        xf = x.reshape(-1, Hd)
        T = xf.shape[0]
        tidx, tw = _route(xf.astype(jnp.float32), router_w, correction_bias)
        combine = jnp.zeros((T, E), xf.dtype).at[jnp.arange(T)[:, None], tidx].add(tw.astype(xf.dtype))

        def body(acc, ew):
            wu, wd, c = ew
            return (acc + c[:, None] * (relu2(xf @ wu) @ wd), None)
        routed, _ = jax.lax.scan(body, jnp.zeros_like(xf), (up_w, down_w, combine.T))
        shared = relu2(xf @ shared_up_w) @ shared_down_w
        return (routed + shared).reshape(B, S, Hd)
    h = _L0_tok_ref(0, x, L0_tok_W0, L0_tok_W1, L0_tok_Wo)
    h = jnp.concatenate([jnp.broadcast_to(cls_tok, (h.shape[0], 1, h.shape[2])), h], axis=1)
    h = h + _L0_attn_ref(_layernorm(h, axis=-1), L0_attn_Wq1, L0_attn_Wq2, L0_attn_Wk1, L0_attn_Wk2, L0_attn_Wv, L0_attn_Wc, L0_attn_lq1, L0_attn_lk1, L0_attn_lq2, L0_attn_lk2)
    h = h + _L0_ffn_ref(_layernorm(h, axis=-1), L0_ffn_router_w, L0_ffn_correction_bias, L0_ffn_up_w, L0_ffn_down_w, L0_ffn_shared_up_w, L0_ffn_shared_down_w)
    return h

_drawn_inputs = setup_inputs


def setup_inputs(seed=0):
    import zlib

    import numpy as np

    out = dict(_drawn_inputs(seed))
    spreads = {}
    factors = {'L0_attn_lq1': 7.348,
     'L0_attn_lk1': 6.875,
     'L0_attn_lq2': 7.63,
     'L0_attn_lk2': 7.619,
     'L0_ffn_correction_bias': 4.652}
    for name, (base, spread) in spreads.items():
        noise = np.random.default_rng([zlib.crc32(name.encode()), seed]).standard_normal(out[name].shape)
        drawn = base * np.exp(spread * noise) if base else spread * noise
        out[name] = jnp.asarray(drawn.astype(out[name].dtype))
    for name, factor in factors.items():
        out[name] = (out[name] * factor).astype(out[name].dtype)
    return out
```

```python
from contextlib import ExitStack
import math

import concourse.bass as bass
from concourse import mybir

ALU = mybir.AluOpType
ACT = mybir.ActivationFunctionType
F32 = mybir.dt.float32
BF16 = mybir.dt.bfloat16
AX_X = mybir.AxisListType.X

LN_EPS = 1e-05
LAMBDA_INIT = 0.8 - 0.6 * math.exp(-0.3 * (2 - 1))
ROUTE_SCALE = 2.5
MASKED = -1.0e30


def wait(eng, sem, value):
    if not (isinstance(value, int) and value <= 0):
        eng.wait_ge(sem, value)


def vit_layer(nc, x, cls_tok, W0, W1, Wo, Wq1, Wq2, Wk1, Wk2, Wv, Wc, lq1, lk1, lq2, lk2,
              router_w, correction_bias, up_w, down_w, shared_up_w, shared_down_w, out):
    B, S, D, E = x.shape
    P = 128
    T = S + 1
    DC = D // P
    DE = W0.shape[0]
    EC = DE // P
    H = lq1.shape[0]
    HS = lq1.shape[1]
    VD = 2 * HS
    HG = 4
    NG = H // HG
    XT = S // P

    NQ = 5
    QR = -(-T // NQ)
    q0 = [QR * i for i in range(NQ)]
    qn = [min(QR, T - QR * i) for i in range(NQ)]
    TA = T // 2 + 1

    N = B * T
    NT = -(-N // P)
    tn = [min(P, N - P * t) for t in range(NT)]
    NX = up_w.shape[0]
    I = up_w.shape[2]
    NS = shared_up_w.shape[1] // I
    NE = NX + NS
    G = 8
    GE = NX // G
    TOPG = 4
    NU = 5
    u0 = [N * u // NU for u in range(NU + 1)]
    NP = -(-NT // 2)
    upto = [min(u for u in range(NU) if u0[u + 1] >= min(P * (t + 1), N)) for t in range(NT)]

    h2_dram = nc.dram_tensor("h2_scratch", [N, D], F32, kind="Internal").ap()
    out_rows = out.rearrange("b t d -> (b t) d")

    with ExitStack() as ctx:
        def sb(name, shape, dt=F32):
            return ctx.enter_context(nc.sbuf_tensor(name, shape, dt))

        def sem(name):
            return ctx.enter_context(nc.semaphore(name))

        ps = ctx.enter_context(nc.psum_tensor("ps", [P, 8, 512], F32))

        ident = sb("ident", [P, P])
        identb = sb("identb", [P, P], BF16)
        causal = sb("causal", [P, P], BF16)
        first_row = sb("first_row", [P, P])
        cls_row = sb("cls_row", [P, D])
        even_mask = sb("even_mask", [P, 2])
        neg_half = sb("neg_half", [P, H])
        eps = sb("eps", [P, NQ])
        unused = sb("unused", [P, 1])
        lam_in = sb("lam_in", [P, 4, H, HS])
        lam_pr = sb("lam_pr", [P, 2, H, HS])
        lam_s = sb("lam_s", [P, 2, H])
        neg_lam = sb("neg_lam", [P, H])
        w0_raw = sb("w0_raw", [P, EC, D])
        w1_raw = sb("w1_raw", [P, EC, D])
        wo_raw = sb("wo_raw", [P, DC, DE])
        w0t = sb("w0t", [P, DC, DE])
        w1t = sb("w1t", [P, DC, DE])
        wot = sb("wot", [P, EC, D])
        wq = sb("wq", [P, DC, NG * P])
        wk = sb("wk", [P, DC, NG * P])
        wv = sb("wv", [P, DC, H * VD])
        wc = sb("wc", [P, H * VD // P, D])
        xraw = sb("xraw", [P, XT, D * E])
        xt_tok = sb("xt_tok", [P, DC, S])
        gate = sb("gate", [P, 2, S])
        hid_tok = sb("hid_tok", [P, EC, T])
        h = sb("h", [P, NQ, D])
        st6 = sb("st6", [P, NQ, 6])
        mv = sb("mv", [P, NQ, 2])
        rs = sb("rs", [P, NQ])
        xh = sb("xh", [P, NQ, D])
        xt = sb("xt", [P, DC, T])
        qe = sb("qe", [P, NG, T])
        qo = sb("qo", [P, NG, T])
        kt = sb("kt", [P, NG, T])
        v = sb("v", [P, NQ, H * VD])
        pr = sb("pr", [P, 2, HG, 2, T])
        negm = sb("negm", [P, 2, HG, 2])
        lsum = sb("lsum", [P, 2, 2, H])
        coef = sb("coef", [P, 2, 2, HG])
        att_t = sb("att_t", [P, HG, NQ * QR])
        rl = sb("rl", [P, H])
        y = sb("y", [P, H, VD])
        ysum = sb("ysum", [P, 2, H])
        ysq = sb("ysq", [P, H, VD])
        yrs = sb("yrs", [P, H])
        yn = sb("yn", [P, H, VD])
        yt = sb("yt", [P, H * VD // P, QR])

        consts_in = sem("consts_in")
        wtok_in = sem("wtok_in")
        wattn_in = sem("wattn_in")
        x_in = sem("x_in")
        pool_const = sem("pool_const")
        dve_const = sem("dve_const")
        lam_exp = sem("lam_exp")
        wt_ps = sem("wt_ps")
        wt_even = sem("wt_even")
        wt_odd = sem("wt_odd")
        xt_ps = sem("xt_ps")
        xt_sb = sem("xt_sb")
        gu_ps = sem("gu_ps")
        gate_sb = sem("gate_sb")
        hid_sb = sem("hid_sb")
        tok_ps = sem("tok_ps")
        h_sb = sem("h_sb")
        st_sb = sem("st_sb")
        mv_sb = sem("mv_sb")
        veps_sb = sem("veps_sb")
        rs_sb = sem("rs_sb")
        xh_sb = sem("xh_sb")
        xht_ps = sem("xht_ps")
        xht_sb = sem("xht_sb")
        q_ps = sem("q_ps")
        k_ps = sem("k_ps")
        q_sb = sem("q_sb")
        k_sb = sem("k_sb")
        v_ps = sem("v_ps")
        v_sb = sem("v_sb")
        s_ps = sem("s_ps")
        max_sb = sem("max_sb")
        exp_sb = sem("exp_sb")
        coef_sb = sem("coef_sb")
        att_sb = sem("att_sb")
        att_ps = sem("att_ps")
        attt_even = sem("attt_even")
        attt_odd = sem("attt_odd")
        pv_ps = sem("pv_ps")
        rl_sb = sem("rl_sb")
        y_sb = sem("y_sb")
        ystep = sem("ystep")
        ysq_sb = sem("ysq_sb")
        yvar_sb = sem("yvar_sb")
        yrs_sb = sem("yrs_sb")
        yrs_scaled = sem("yrs_scaled")
        yn_sb = sem("yn_sb")
        yt_ps = sem("yt_ps")
        yt_sb = sem("yt_sb")
        wc_ps = sem("wc_ps")
        h2_sb = sem("h2_sb")
        h2_out = sem("h2_out")

        TP = 4
        OUT = 6
        HPB = NQ * H
        N_WT = 2 * EC * DC + DC * EC
        wt_jobs = []
        for raw, dst in ((w0_raw, w0t), (w1_raw, w1t)):
            for d in range(DC):
                for e in range(EC):
                    wt_jobs.append((raw[:, e, d * P:(d + 1) * P], dst[:, d, e * P:(e + 1) * P]))
        for e in range(EC):
            for d in range(DC):
                wt_jobs.append((wo_raw[:, d, e * P:(e + 1) * P], wot[:, e, d * P:(d + 1) * P]))

        block = ctx.enter_context(nc.Block())

        def load_x(sp, b):
            sp.dma_start(xraw[:, :, :], x[b].rearrange("(t p) d e -> p t (d e)", p=P)).then_inc(x_in, 16)

        @block.sync
        def _(sp):
            for k, w in enumerate((lq1, lk1, lq2, lk2)):
                sp.dma_start(lam_in[:, k, :, :], w.partition_broadcast(P)).then_inc(consts_in, 16)
            sp.dma_start(cls_row[0:1, :], cls_tok.rearrange("a b d -> (a b) d")).then_inc(consts_in, 16)
            load_x(sp, 0)
            sp.dma_start(w0_raw[:, :, :], W0.rearrange("(c p) d -> p c d", p=P)).then_inc(wtok_in, 16)
            sp.dma_start(w1_raw[:, :, :], W1.rearrange("(c p) d -> p c d", p=P)).then_inc(wtok_in, 16)
            sp.dma_start(wo_raw[:, :, :], Wo.rearrange("(c p) d -> p c d", p=P)).then_inc(wtok_in, 16)
            for w, dst in (((Wq1, Wq2), wq), ((Wk1, Wk2), wk)):
                for m in range(2):
                    for c in range(DC):
                        sp.dma_start(dst[:, c, :].rearrange("p (j m k) -> p j m k", m=2, k=2 * HS)[:, :, m, :],
                                     w[m][c * P:(c + 1) * P, :].rearrange("p (j k) -> p j k", k=2 * HS)
                                     ).then_inc(wattn_in, 16)
            sp.dma_start(wv[:, :, :], Wv.rearrange("(c p) d -> p c d", p=P)).then_inc(wattn_in, 16)
            sp.dma_start(wc[:, :, :], Wc.rearrange("(c p) d -> p c d", p=P)).then_inc(wattn_in, 16)

            def store_h2(b):
                for i in range(NQ):
                    sp.wait_ge(h2_sb, b * NQ + i + 1)
                    sp.dma_start(h2_dram[bass.ds(b * T + q0[i], qn[i]), :], h[0:qn[i], i, :]).then_inc(h2_out, 16)

            with sp.Fori(1, B) as b:
                sp.wait_ge(xt_ps, b * DC)
                load_x(sp, b)
                store_h2(b - 1)
            store_h2(B - 1)
            sp.wait_ge(h2_out, 16 * NQ * B)

        @block.gpsimd
        def _(pool):
            nc.gpsimd.memset(ident[:, :], 0.0).then_inc(pool_const, 1)
            nc.gpsimd.memset(causal[:, :], 0.0).then_inc(pool_const, 1)
            nc.gpsimd.memset(first_row[:, :], 0.0).then_inc(pool_const, 1)
            nc.gpsimd.memset(even_mask[:, :], 0.0).then_inc(pool_const, 1)
            nc.gpsimd.memset(neg_half[:, :], -0.5).then_inc(pool_const, 1)
            nc.gpsimd.memset(eps[:, :], LN_EPS).then_inc(pool_const, 1)
            pool.wait_ge(pool_const, 6)
            nc.gpsimd.affine_select(out=ident[:, :], in_=ident[:, :], compare_op=ALU.not_equal, fill=1.0,
                                    base=0, pattern=[[-1, P]], channel_multiplier=1).then_inc(pool_const, 1)
            nc.gpsimd.affine_select(out=causal[:, :], in_=causal[:, :], compare_op=ALU.is_ge, fill=MASKED,
                                    base=0, pattern=[[-1, P]], channel_multiplier=1).then_inc(pool_const, 1)
            pool.wait_ge(pool_const, 8)
            nc.gpsimd.tensor_copy(identb[:, :], ident[:, :]).then_inc(pool_const, 1)
            nc.gpsimd.memset(first_row[0:1, 0:1], 1.0).then_inc(pool_const, 1)

            def batch(b):
                pool.wait_ge(mv_sb, (b + 1) * NQ)
                nc.gpsimd.tensor_tensor(rs[:, :], mv[:, :, 1], eps[:, 0:NQ], ALU.add).then_inc(veps_sb, 1)
                pool.wait_ge(veps_sb, b + 1)
                nc.gpsimd.tensor_tensor(rs[:, :], rs[:, :], neg_half[:, 0:NQ], ALU.pow).then_inc(rs_sb, 1)
                for i in range(NQ):
                    n = qn[i]
                    wait(pool, y_sb, b * NQ + i + 1)
                    nc.gpsimd.tensor_tensor(ysq[0:n, :, :], y[0:n, :, :], y[0:n, :, :], ALU.mult).then_inc(ysq_sb, 1)
                    wait(pool, yvar_sb, b * NQ + i + 1)
                    nc.gpsimd.tensor_tensor(yrs[0:n, :], ysum[0:n, 1, :], neg_half[0:n, 0:H], ALU.pow
                                            ).then_inc(yrs_sb, 1)

            batch(0)
            with pool.Fori(1, B) as b:
                batch(b)

        @block.scalar
        def _(act):
            act.wait_ge(dve_const, 4)
            nc.scalar.activation(lam_s[:, :, :], lam_s[:, :, :], ACT.Exp).then_inc(lam_exp, 1)
            for n, (_, dst) in enumerate(wt_jobs):
                if n % 2 == 0:
                    act.wait_ge(wt_ps, n + 1)
                    nc.scalar.copy(dst, ps[:, n % 8, 0:P]).then_inc(wt_even, 1)
            def batch(b):
                for c in range(DC):
                    wait(act, xt_ps, b * DC + c + 1)
                    wait(act, gu_ps, b * EC)
                    nc.scalar.copy(xt_tok[:, c, :], ps[:, TP + c, :]).then_inc(xt_sb, 1)
                for c in range(EC):
                    wait(act, gu_ps, b * EC + c + 1)
                    wait(act, hid_sb, b * EC + max(c - 1, 0))
                    nc.scalar.activation(gate[:, c % 2, :], ps[:, 2 * (c % 2), :], ACT.Relu).then_inc(gate_sb, 1)
                for i in range(NQ):
                    wait(act, xht_ps, b * NQ + i + 1)
                    wait(act, v_ps, b * NQ)
                    nc.scalar.copy(xt[:, :, q0[i]:q0[i] + qn[i]],
                                   ps[:, TP + i % 2, 0:DC * qn[i]].rearrange("p (c n) -> p c n", c=DC)
                                   ).then_inc(xht_sb, 1)
                for g in range(NG):
                    wait(act, k_ps, b * NG + g + 1)
                    nc.scalar.copy(kt[:, g, :], ps[:, 2:4, :].rearrange("p k n -> p (k n)")[:, 512 - TA:512 - TA + T]
                                   ).then_inc(k_sb, 1)
                for i in range(NQ):
                    wait(act, v_ps, b * NQ + i + 1)
                    nc.scalar.copy(v[0:qn[i], i, :], ps[0:qn[i], OUT + i % 2, :]).then_inc(v_sb, 1)

                def evac(n, hh):
                    i = n // NG
                    if hh % 2 == 1:
                        wait(act, att_ps, b * HPB + n * HG + hh + 1)
                        wait(act, pv_ps, b * HPB + max(n - 1, 0) * HG + (hh + 1 if n else 0))
                        m = (i + 1) * qn[i]
                        nc.scalar.copy(att_t[0:QR, hh, 0:m], ps[0:QR, TP + 1, 0:m]).then_inc(attt_odd, 1)

                def evac_y(i):
                    wait(act, yt_ps, b * NQ + i + 1)
                    wait(act, wc_ps, b * NQ + i)
                    nc.scalar.copy(yt[:, :, 0:qn[i]],
                                   ps[:, TP, 0:H * VD // P * qn[i]].rearrange("p (c n) -> p c n", n=qn[i])
                                   ).then_inc(yt_sb, 1)

                for n in range(NQ * NG):
                    i, g = divmod(n, NG)
                    nk = q0[i] + qn[i]
                    for hh in range(HG):
                        c = b * HPB + n * HG + hh
                        act.wait_ge(max_sb, c + 1)
                        wait(act, att_ps, b * HPB + (max(n - 2, 0) * HG + (hh + 1 if n >= 2 else 0)))
                        for m in range(2):
                            bank = 2 * (hh % 2) + m if i < NQ - 1 else 2 * m
                            src = ps[0:qn[i], bank:bank + 2, :].rearrange("p k n -> p (k n)")[:, 0:nk] \
                                if i == NQ - 1 else ps[0:qn[i], bank, 0:nk]
                            e = nc.scalar.activation(pr[0:qn[i], n % 2, hh, m, 0:nk], src, ACT.Exp,
                                                     bias=negm[0:qn[i], n % 2, hh, m:m + 1],
                                                     accum_out=lsum[0:qn[i], i % 2, m, HG * g + hh:HG * g + hh + 1])
                        e.then_inc(exp_sb, 1)
                        if n >= 1:
                            evac(n - 1, hh)
                    if n >= NG + 1 and n % NG == 1:
                        evac_y(i - 1)
                for hh in range(HG):
                    evac(NQ * NG - 1, hh)
                evac_y(NQ - 1)

            batch(0)
            with act.Fori(1, B) as b:
                batch(b)

        @block.vector
        def _(dve):
            nc.vector.memset(mv[:, :, :], 1.0).then_inc(dve_const, 1)
            nc.vector.memset(ps[:, TP:TP + 2, :], 0.0).then_inc(dve_const, 1)
            nc.vector.memset(hid_tok[:, :, 0:1], 0.0).then_inc(dve_const, 1)
            dve.wait_ge(consts_in, 5 * 16)
            nc.vector.tensor_tensor(lam_pr[:, :, :, :], lam_in[:, 0:4:2, :, :], lam_in[:, 1:4:2, :, :], ALU.mult
                                    ).then_inc(ystep, 1)
            dve.wait_ge(ystep, 1)
            nc.vector.tensor_reduce(lam_s[:, :, :], lam_pr[:, :, :, :], AX_X, ALU.add).then_inc(dve_const, 1)
            dve.wait_ge(pool_const, 10)
            for k in range(2):
                idv = ident[:, :].rearrange("p (j k d) -> p k j d", k=2, d=HS)[:, k]
                nc.vector.tensor_reduce(even_mask[:, k:k + 1], idv, mybir.AxisListType.XY, ALU.add).then_inc(ystep, 1)
            dve.wait_ge(ystep, 3)
            nc.vector.tensor_scalar(even_mask[:, :], even_mask[:, :], HS ** -0.5, None, ALU.mult).then_inc(ystep, 1)
            dve.wait_ge(lam_exp, 1)
            nc.vector.tensor_tensor(neg_lam[:, :], lam_s[:, 1, :], lam_s[:, 0, :], ALU.subtract).then_inc(ystep, 1)
            dve.wait_ge(ystep, 5)
            nc.vector.tensor_scalar(neg_lam[:, :], neg_lam[:, :], -LAMBDA_INIT, None, ALU.add).then_inc(ystep, 1)
            for n, (_, dst) in enumerate(wt_jobs):
                if n % 2 == 1:
                    dve.wait_ge(wt_ps, n + 1)
                    nc.vector.tensor_copy(dst, ps[:, n % 8, 0:P]).then_inc(wt_odd, 1)
            dve.wait_ge(ystep, 6)

            def batch(b):
                for c in range(EC):
                    wait(dve, gate_sb, b * EC + c + 1)
                    wait(dve, tok_ps, b * NQ)
                    nc.vector.tensor_tensor(hid_tok[:, c, 1:T], gate[:, c % 2, :], ps[:, 2 * (c % 2) + 1, :], ALU.mult
                                            ).then_inc(hid_sb, 1)
                for i in range(NQ):
                    n = qn[i]
                    wait(dve, tok_ps, b * NQ + i + 1)
                    wait(dve, h2_out, b * (NQ * 16))
                    nc.vector.tensor_copy(h[0:n, i, :], ps[0:n, OUT + i % 2, 0:D]).then_inc(h_sb, 1)
                    wait(dve, h_sb, b * NQ + i + 1)
                    nc.vector.bn_stats(st6[0:n, i, :], h[0:n, i, :]).then_inc(st_sb, 1)
                dve.wait_ge(st_sb, (b + 1) * NQ)
                nc.vector.memset(unused[:, :], 0.0)
                for i in range(NQ):
                    nc.vector.bn_aggr(mv[0:qn[i], i, :], st6[0:qn[i], i, :]).then_inc(mv_sb, 1)
                dve.wait_ge(rs_sb, b + 1)
                for i in range(NQ):
                    n = qn[i]
                    wait(dve, xht_ps, b * NQ)
                    nc.vector.tensor_scalar(xh[0:n, i, :], h[0:n, i, :], mv[0:n, i, 0:1], rs[0:n, i:i + 1],
                                            ALU.subtract, ALU.mult).then_inc(xh_sb, 1)
                for g in range(NG):
                    wait(dve, q_ps, b * NG + g + 1)
                    qps = ps[:, 0:2, :].rearrange("p k n -> p (k n)")[:, 512 - TA:512 - TA + T]
                    nc.vector.tensor_scalar(qe[:, g, :], qps, even_mask[:, 0:1], None, ALU.mult)
                    nc.vector.tensor_scalar(qo[:, g, :], qps, even_mask[:, 1:2], None, ALU.mult).then_inc(q_sb, 1)

                def coefs(n):
                    i, g = divmod(n, NG)
                    m = qn[i]
                    hs = slice(HG * g, HG * g + HG)
                    done = b * (3 * NQ * NG) + 3 * n
                    wait(dve, exp_sb, b * HPB + (n + 1) * HG)
                    nc.vector.reciprocal(coef[0:m, n % 2, 0, :], lsum[0:m, i % 2, 1, hs]).then_inc(coef_sb, 1)
                    nc.vector.tensor_tensor(coef[0:m, n % 2, 1, :], lsum[0:m, i % 2, 0, hs], neg_lam[0:m, hs], ALU.mult
                                            ).then_inc(coef_sb, 1)
                    dve.wait_ge(coef_sb, done + 2)
                    nc.vector.tensor_tensor(coef[0:m, n % 2, 0, :], coef[0:m, n % 2, 0, :], coef[0:m, n % 2, 1, :],
                                            ALU.mult).then_inc(coef_sb, 1)
                    dve.wait_ge(coef_sb, done + 3)

                def combine(n, hh):
                    i = n // NG
                    m = qn[i]
                    nk = q0[i] + m
                    nc.vector.scalar_tensor_tensor(
                        out=pr[0:m, n % 2, hh, 0, 0:nk], in0=pr[0:m, n % 2, hh, 1, 0:nk],
                        scalar=coef[0:m, n % 2, 0, hh:hh + 1], in1=pr[0:m, n % 2, hh, 0, 0:nk],
                        op0=ALU.mult, op1=ALU.add).then_inc(att_sb, 1)

                def evac(n, hh):
                    i = n // NG
                    if hh % 2 == 0:
                        wait(dve, att_ps, b * HPB + n * HG + hh + 1)
                        wait(dve, pv_ps, b * HPB + max(n - 1, 0) * HG + (hh + 1 if n else 0))
                        m = (i + 1) * qn[i]
                        nc.vector.tensor_copy(att_t[0:QR, hh, 0:m], ps[0:QR, TP, 0:m]).then_inc(attt_even, 1)

                def head_norm(i):
                    m = qn[i]
                    k = b * (5 * NQ) + 5 * i + 6
                    bank = ps[0:m, OUT + i % 2, :].rearrange("p (h d) -> p h d", h=H)
                    nc.vector.reciprocal(rl[0:m, :], lsum[0:m, i % 2, 0, :]).then_inc(ystep, 1)
                    wait(dve, pv_ps, b * HPB + (i + 1) * H)
                    dve.wait_ge(ystep, k + 1)
                    wait(dve, yt_ps, b * NQ + i)
                    nc.vector.tensor_tensor(yn[0:m, :, :], bank, rl[0:m, :].unsqueeze(2).to_broadcast([m, H, VD]),
                                            ALU.mult).then_inc(ystep, 1)
                    dve.wait_ge(ystep, k + 2)
                    nc.vector.tensor_reduce(ysum[0:m, 0, :], yn[0:m, :, :], AX_X, ALU.add).then_inc(ystep, 1)
                    dve.wait_ge(ystep, k + 3)
                    nc.vector.tensor_scalar(ysum[0:m, 0, :], ysum[0:m, 0, :], 1.0 / VD, None, ALU.mult
                                            ).then_inc(ystep, 1)
                    dve.wait_ge(ystep, k + 4)
                    nc.vector.tensor_tensor(y[0:m, :, :], yn[0:m, :, :],
                                            ysum[0:m, 0, :].unsqueeze(2).to_broadcast([m, H, VD]), ALU.subtract
                                            ).then_inc(y_sb, 1)
                    wait(dve, ysq_sb, b * NQ + i + 1)
                    nc.vector.tensor_reduce(ysum[0:m, 1, :], ysq[0:m, :, :], AX_X, ALU.add).then_inc(ystep, 1)
                    dve.wait_ge(ystep, k + 5)
                    nc.vector.tensor_scalar(ysum[0:m, 1, :], ysum[0:m, 1, :], 1.0 / VD, LN_EPS, ALU.mult, ALU.add
                                            ).then_inc(yvar_sb, 1)
                    wait(dve, yrs_sb, b * NQ + i + 1)
                    nc.vector.tensor_scalar(yrs[0:m, :], yrs[0:m, :], 1.0 - LAMBDA_INIT, None, ALU.mult
                                            ).then_inc(yrs_scaled, 1)
                    wait(dve, yrs_scaled, b * NQ + i + 1)
                    nc.vector.tensor_tensor(yn[0:m, :, :], y[0:m, :, :],
                                            yrs[0:m, :].unsqueeze(2).to_broadcast([m, H, VD]), ALU.mult
                                            ).then_inc(yn_sb, 1)

                def residual(i):
                    m = qn[i]
                    wait(dve, wc_ps, b * NQ + i + 1)
                    nc.vector.tensor_tensor(h[0:m, i, :], h[0:m, i, :], ps[0:m, OUT + i % 2, 0:D], ALU.add
                                            ).then_inc(h2_sb, 1)

                for n in range(NQ * NG):
                    i, g = divmod(n, NG)
                    m = qn[i]
                    nk = q0[i] + qn[i]
                    for hh in range(HG):
                        c = b * HPB + n * HG + hh
                        dve.wait_ge(s_ps, c + 1)
                        if i < NQ - 1:
                            src = ps[0:m, 2 * (hh % 2):2 * (hh % 2) + 2, 0:nk]
                        else:
                            src = ps[0:m, 0:4, :].rearrange("p (m k) n -> p m (k n)", m=2)[:, :, 0:nk]
                        nc.vector.tensor_reduce(negm[0:m, n % 2, hh, :], src, AX_X, ALU.max, negate=True
                                                ).then_inc(max_sb, 1)
                        if n >= 1:
                            if hh == 0:
                                coefs(n - 1)
                            combine(n - 1, hh)
                            if hh == 1:
                                evac(n - 1, 0)
                    if n >= 1:
                        evac(n - 1, 2)
                    if n >= NG and n % NG == 0:
                        head_norm(i - 1)
                    if n >= NG and n % NG == 2:
                        residual(i - 1)
                coefs(NQ * NG - 1)
                for hh in range(HG):
                    combine(NQ * NG - 1, hh)
                evac(NQ * NG - 1, 0)
                evac(NQ * NG - 1, 2)
                head_norm(NQ - 1)
                residual(NQ - 1)

            batch(0)
            with dve.Fori(1, B) as b:
                batch(b)

        @block.tensor
        def _(pe):
            pe.wait_ge(pool_const, 10)
            pe.wait_ge(wtok_in, 3 * 16)
            pe.wait_ge(dve_const, 3)
            for n, (raw, _) in enumerate(wt_jobs):
                if n >= 8:
                    pe.wait_ge(wt_even if n % 2 == 0 else wt_odd, n // 2 - 3)
                nc.tensor.transpose(ps[:, n % 8, 0:P], raw, ident[:, :]).then_inc(wt_ps, 1)
            pe.wait_ge(wt_even, len(wt_jobs) // 2)
            pe.wait_ge(wt_odd, len(wt_jobs) // 2)
            pe.wait_ge(consts_in, 5 * 16)
            pe.wait_ge(wattn_in, (2 * 2 * DC + 2) * 16)

            def batch(b):
                pe.wait_ge(x_in, (b + 1) * 16)
                wait(pe, yt_sb, b * NQ)
                for c in range(DC):
                    for t in range(XT):
                        xv = xraw[:, t, :].rearrange("p (d e) -> p d e", e=E)[:, c * P:(c + 1) * P, 0]
                        last = nc.tensor.transpose(ps[:, TP + c, t * P:(t + 1) * P], xv, ident[:, :])
                    last.then_inc(xt_ps, 1)
                pe.wait_ge(xt_sb, (b + 1) * DC)
                for c in range(EC):
                    if c >= 2:
                        wait(pe, hid_sb, b * EC + c - 1)
                    for w, bank in ((w0t, 2 * (c % 2)), (w1t, 2 * (c % 2) + 1)):
                        for d in range(DC):
                            last = nc.tensor.matmul(ps[:, bank, :], w[:, d, c * P:(c + 1) * P], xt_tok[:, d, :],
                                                    start=(d == 0), stop=(d == DC - 1))
                    last.then_inc(gu_ps, 1)
                pe.wait_ge(hid_sb, (b + 1) * EC)
                for i in range(NQ):
                    n = qn[i]
                    if i >= 2:
                        wait(pe, h_sb, b * NQ + i - 1)
                    else:
                        wait(pe, h2_sb, b * NQ)
                    bank = ps[0:n, OUT + i % 2, 0:D]
                    for c in range(EC):
                        last = nc.tensor.matmul(bank, hid_tok[:, c, q0[i]:q0[i] + n], wot[:, c, :],
                                                start=(c == 0), stop=(c == EC - 1 and i > 0))
                    if i == 0:
                        last = nc.tensor.matmul(bank, first_row[0:1, 0:n], cls_row[0:1, :], start=False, stop=True)
                    last.then_inc(tok_ps, 1)
                for i in range(NQ):
                    n = qn[i]
                    wait(pe, xh_sb, b * NQ + i + 1)
                    if i >= 2:
                        wait(pe, xht_sb, b * NQ + i - 1)
                    for c in range(DC):
                        last = nc.tensor.transpose(ps[:, TP + i % 2, c * n:(c + 1) * n],
                                                   xh[0:n, i, c * P:(c + 1) * P], ident[0:n, 0:n])
                    last.then_inc(xht_ps, 1)
                pe.wait_ge(xht_sb, (b + 1) * NQ)
                for g in range(NG):
                    for w, bank, free, done in ((wq, 0, q_sb, q_ps), (wk, 2, k_sb, k_ps)):
                        if g >= 1:
                            wait(pe, free, b * NG + g)
                        for k, (a, z) in enumerate(((0, TA), (TA, T))):
                            dst = ps[:, bank, 512 - TA:512] if k == 0 else ps[:, bank + 1, 0:T - TA]
                            for d in range(DC):
                                last = nc.tensor.matmul(dst, w[:, d, g * P:(g + 1) * P], xt[:, d, a:z],
                                                        start=(d == 0), stop=(d == DC - 1))
                        last.then_inc(done, 1)
                for i in range(NQ):
                    n = qn[i]
                    if i >= 2:
                        wait(pe, v_sb, b * NQ + i - 1)
                    for d in range(DC):
                        last = nc.tensor.matmul(ps[0:n, OUT + i % 2, :], xt[:, d, q0[i]:q0[i] + n], wv[:, d, :],
                                                start=(d == 0), stop=(d == DC - 1))
                    last.then_inc(v_ps, 1)
                pe.wait_ge(v_sb, (b + 1) * NQ)
                pe.wait_ge(q_sb, (b + 1) * NG)
                pe.wait_ge(k_sb, (b + 1) * NG)

                def scores(n, hh):
                    i, g = divmod(n, NG)
                    m = qn[i]
                    nk = q0[i] + m
                    c = n * HG + hh
                    if i == NQ - 1:
                        wait(pe, exp_sb, b * HPB + c)
                    elif c >= 2:
                        wait(pe, exp_sb, b * HPB + c - 1)
                    qt = qe if hh % 2 == 0 else qo
                    for k in range(2):
                        r = 32 * (2 * (hh // 2) + k)
                        bank = 2 * (hh % 2) + k if i < NQ - 1 else 2 * k
                        parts = [(0, nk, ps[0:m, bank, 0:nk])] if nk <= 512 else \
                            [(0, 512, ps[0:m, bank, 0:512]), (512, nk, ps[0:m, bank + 1, 0:nk - 512])]
                        for a, z, dst in parts:
                            nc.tensor.matmul(dst, qt[r:r + 32, g, q0[i]:q0[i] + m], kt[r:r + 32, g, a:z],
                                             start=True, stop=False, skip_group_check=True)
                            lo = max(a, q0[i])
                            if lo < z:
                                last = nc.tensor.matmul(dst[:, lo - a:z - a], identb[0:m, 0:m],
                                                        causal[0:m, lo - q0[i]:z - q0[i]],
                                                        start=False, stop=True, skip_group_check=True)
                    last.then_inc(s_ps, 1)

                def turn(n, hh):
                    i = n // NG
                    m = qn[i]
                    c = n * HG + hh
                    wait(pe, att_sb, b * HPB + c + 1)
                    if c >= 2:
                        wait(pe, attt_even if hh % 2 == 0 else attt_odd, b * (HPB // 2) + c // 2)
                    for j in range(i + 1):
                        last = nc.tensor.transpose(ps[0:qn[j], TP + hh % 2, j * m:(j + 1) * m],
                                                   pr[0:m, n % 2, hh, 0, q0[j]:q0[j] + qn[j]], ident[0:m, 0:m])
                    last.then_inc(att_ps, 1)

                def values(n, hh):
                    i, g = divmod(n, NG)
                    m = qn[i]
                    c = n * HG + hh
                    hd = HG * g + hh
                    wait(pe, attt_even if hh % 2 == 0 else attt_odd, b * (HPB // 2) + c // 2 + 1)
                    if hd == 0 and i >= 2:
                        wait(pe, h2_sb, b * NQ + i - 1)
                    for j in range(i + 1):
                        last = nc.tensor.matmul(ps[0:m, OUT + i % 2, VD * hd:VD * (hd + 1)],
                                                att_t[0:qn[j], hh, j * m:(j + 1) * m],
                                                v[0:qn[j], j, VD * hd:VD * (hd + 1)],
                                                start=(j == 0), stop=(j == i))
                    last.then_inc(pv_ps, 1)

                def project(i):
                    m = qn[i]
                    wait(pe, yn_sb, b * NQ + i + 1)
                    ended = (i + 1) * H + (HG if i < NQ - 1 else 0)
                    wait(pe, attt_even, b * (HPB // 2) + ended // 2)
                    for c in range(H * VD // P):
                        last = nc.tensor.transpose(ps[:, TP, c * m:(c + 1) * m],
                                                   yn[0:m, :, :].rearrange("p h d -> p (h d)")[:, c * P:(c + 1) * P],
                                                   ident[0:m, 0:m])
                    last.then_inc(yt_ps, 1)
                    wait(pe, yt_sb, b * NQ + i + 1)
                    for c in range(H * VD // P):
                        last = nc.tensor.matmul(ps[0:m, OUT + i % 2, 0:D], yt[:, c, 0:m], wc[:, c, :],
                                                start=(c == 0), stop=(c == H * VD // P - 1))
                    last.then_inc(wc_ps, 1)

                U = NQ * NG
                for n in range(U + 1):
                    for hh in range(HG):
                        if n < U:
                            scores(n, hh)
                        if n >= 1:
                            turn(n - 1, hh)
                            if hh >= 1:
                                values(n - 1, hh - 1)
                    if n >= 1:
                        values(n - 1, HG - 1)
                    if n >= NG + 1 and n % NG == 1:
                        project((n - 2) // NG)
                project(NQ - 1)


            batch(0)
            with pe.Fori(1, B) as b:
                batch(b)

    with ExitStack() as ctx:
        def sb(name, shape, dt=F32):
            return ctx.enter_context(nc.sbuf_tensor(name, shape, dt))

        def sem(name):
            return ctx.enter_context(nc.semaphore(name))

        ps = ctx.enter_context(nc.psum_tensor("ps2", [P, 8, 512], F32))

        ident = sb("ident2", [P, P])
        half = sb("half", [P, NT])
        lower = sb("lower", [P, G, G])
        bias = sb("bias", [P, NX])
        rw_raw = sb("rw_raw", [P, D])
        rw_t = sb("rw_t", [P, DC, NX])
        acc = sb("acc", [P, NT, D])
        st6 = sb("st62", [P, NT, 6])
        mv = sb("mv2", [P, NT, 2])
        rs = sb("rs2", [P, NT])
        x2 = sb("x2", [P, 2, D])
        x2t = sb("x2t", [P, DC, N])
        score = sb("score", [P, NT, NX])
        sfc = sb("sfc", [P, NT, NX])
        eq = sb("eq", [P, NT, NX])
        rest = sb("rest", [P, NT, NX])
        g1 = sb("g1", [P, NT, G])
        g2 = sb("g2", [P, NT, G])
        gc = sb("gc", [P, NT, G])
        top8 = sb("top8", [P, NT, 8])
        wsum = sb("wsum", [P, NT])
        comb = sb("comb", [P, NX, NT])
        cur = sb("cur", [P, 2, NT])
        wu = sb("wu", [P, 2, DC, I])
        wd = sb("wd", [P, 2, D])
        wus = sb("wus", [P, DC, NS * I])
        wds = sb("wds", [P, NS, D])
        r = sb("r", [P, 2, N // NU + 1])
        hid = sb("hid", [P, 2, N])

        w_in = sem("w_in")
        h2_in = [sem(f"h2_in{k}") for k in range(5)]
        wu_in = [sem(f"wu_in{k}") for k in range(2)]
        wd_in = [sem(f"wd_in{k}") for k in range(2)]
        pool_c2 = sem("pool_c2")
        clear_sb = sem("clear_sb")
        st_sb = sem("st_sb2")
        mv_sb = sem("mv_sb2")
        veps_sb = sem("veps_sb2")
        rs_sb = sem("rs_sb2")
        x2_sb = sem("x2_sb")
        x2_ps = sem("x2_ps")
        x2t_sb = sem("x2t_sb")
        rw_ps = sem("rw_ps")
        rw_sb = sem("rw_sb")
        logit_ps = sem("logit_ps")
        sig_sb = sem("sig_sb")
        route = sem("route")
        cur_sb = sem("cur_sb")
        up_ps = sem("up_ps")
        relu_sb = sem("relu_sb")
        hid_sb = sem("hid_sb2")
        down_ps = sem("down_ps")
        acc_sb = sem("acc_sb")
        out_done = sem("out_done")

        UP = 0
        DN = 5
        LG = 5
        full = N // P
        chunks = [(a, min(a + 4, full)) for a in range(0, full, 4)]
        piece_of = [min(t // 4, 4) for t in range(NT)]

        block = ctx.enter_context(nc.Block())

        @block.sync
        def _(sp):
            sp.dma_start(rw_raw[0:NX, :], router_w).then_inc(w_in, 16)
            sp.dma_start(bias[:, :], correction_bias.partition_broadcast(P)).then_inc(w_in, 16)
            sp.wait_ge(clear_sb, 1)
            for k, (a, z) in enumerate(chunks):
                sp.dma_start(acc[:, a:z, :], h2_dram[P * a:P * z, :].rearrange("(t p) d -> p t d", p=P)
                             ).then_inc(h2_in[k], 16)
            if full < NT:
                sp.dma_start(acc[0:tn[full], full, :], h2_dram[P * full:N, :]).then_inc(h2_in[4], 16)
            sp.dma_start(wus[:, :, :], shared_up_w.rearrange("(c p) i -> p c i", p=P)).then_inc(w_in, 16)
            sp.dma_start(wds[:, :, :], shared_down_w.rearrange("(c p) d -> p c d", p=P)).then_inc(w_in, 16)

            def load(e, k):
                sp.dma_start(wu[:, k, :, :], up_w[bass.ds(e, 1)].rearrange("a (c p) i -> p (a c) i", p=P)
                             ).then_inc(wu_in[k], 16)
                sp.dma_start(wd[:, k, :], down_w[bass.ds(e, 1)].rearrange("a i d -> i (a d)")
                             ).then_inc(wd_in[k], 16)

            for k in range(2):
                load(k, k)
            with sp.Fori(0, NX // 2 - 1) as j:
                e = j * 2
                for k in range(2):
                    sp.wait_ge(down_ps, (e + (NS + k + 1)) * NP)
                    load(e + (2 + k), k)
            for k, (a, z) in enumerate(chunks):
                sp.wait_ge(acc_sb, NE * NP)
                sp.dma_start(out_rows[P * a:P * z, :].rearrange("(t p) d -> p t d", p=P), acc[:, a:z, :]
                             ).then_inc(out_done, 16)
            if full < NT:
                sp.dma_start(out_rows[P * full:N, :], acc[0:tn[full], full, :]).then_inc(out_done, 16)
            sp.wait_ge(out_done, 16 * (len(chunks) + (full < NT)))

        @block.gpsimd
        def _(pool):
            nc.gpsimd.memset(ident[:, :], 0.0).then_inc(pool_c2, 1)
            nc.gpsimd.memset(half[:, :], -0.5).then_inc(pool_c2, 1)
            nc.gpsimd.memset(lower[:, :, :], 0.0).then_inc(pool_c2, 1)
            pool.wait_ge(pool_c2, 3)
            nc.gpsimd.affine_select(out=ident[:, :], in_=ident[:, :], compare_op=ALU.not_equal, fill=1.0,
                                    base=0, pattern=[[-1, P]], channel_multiplier=1).then_inc(pool_c2, 1)
            nc.gpsimd.affine_select(out=lower[:, :, :], in_=lower[:, :, :], compare_op=ALU.is_ge, fill=1.0,
                                    base=0, pattern=[[-1, G], [1, G]], channel_multiplier=0).then_inc(pool_c2, 1)
            for k in range(5):
                ts = [t for t in range(NT) if piece_of[t] == k]
                if not ts:
                    continue
                a, z = ts[0], ts[-1] + 1
                pool.wait_ge(mv_sb, z)
                nc.gpsimd.tensor_scalar(rs[:, a:z], mv[:, a:z, 1], LN_EPS, None, ALU.add).then_inc(veps_sb, 1)
                pool.wait_ge(veps_sb, k + 1)
                nc.gpsimd.tensor_tensor(rs[:, a:z], rs[:, a:z], half[:, a:z], ALU.pow).then_inc(rs_sb, 1)

        @block.scalar
        def _(act):
            act.wait_ge(rw_ps, 1)
            nc.scalar.copy(rw_t[:, :, :], ps[:, 7, 0:DC * NX].rearrange("p (c n) -> p c n", c=DC)).then_inc(rw_sb, 1)
            for t in range(NT):
                n = tn[t]
                act.wait_ge(x2_ps, t + 1)
                nc.scalar.copy(x2t[:, :, P * t:P * t + n],
                               ps[:, UP + t % 2, 0:DC * n].rearrange("p (c n) -> p c n", c=DC)).then_inc(x2t_sb, 1)
            for t in range(NT):
                act.wait_ge(logit_ps, t + 1)
                act.wait_ge(clear_sb, 2)
                nc.scalar.activation(score[0:tn[t], t, :], ps[0:tn[t], LG + t % 2, 0:NX], ACT.Exp, scale=-1.0
                                     ).then_inc(sig_sb, 1)

            def expert(n, k):
                def square(u):
                    act.wait_ge(relu_sb, n * NU + (u + 1))
                    nc.scalar.activation(hid[:, k, u0[u]:u0[u + 1]], r[:, u % 2, 0:u0[u + 1] - u0[u]], ACT.Square
                                         ).then_inc(hid_sb, 1)

                for u in range(NU):
                    act.wait_ge(up_ps, n * NU + (u + 1))
                    if u >= 2:
                        act.wait_ge(hid_sb, n * NU + (u - 1))
                    else:
                        act.wait_ge(hid_sb, n * NU)
                    nc.scalar.activation(r[:, u % 2, 0:u0[u + 1] - u0[u]], ps[:, UP + u, 0:u0[u + 1] - u0[u]], ACT.Relu
                                         ).then_inc(relu_sb, 1)
                    if u >= 1:
                        square(u - 1)
                square(NU - 1)

            def free_hid(n):
                act.wait_ge(down_ps, n * NP)

            for n in range(NS):
                if n >= 2:
                    free_hid(n - 1)
                expert(n, n % 2)
            with act.Fori(0, NX // 2) as j:
                n = j * 2 + NS
                for k in range(2):
                    free_hid(n + (k - 1))
                    expert(n + k, k)

        @block.vector
        def _(dve):
            nc.vector.memset(mv[:, :, :], 1.0)
            nc.vector.memset(acc[:, full:NT, :], 0.0).then_inc(clear_sb, 1)
            nc.vector.memset(score[:, :, :], 0.0).then_inc(clear_sb, 1)
            for k in range(5):
                ts = [t for t in range(NT) if piece_of[t] == k]
                if not ts:
                    continue
                dve.wait_ge(h2_in[k], 16)
                for t in ts:
                    nc.vector.bn_stats(st6[0:tn[t], t, :], acc[0:tn[t], t, :]).then_inc(st_sb, 1)
                for t in ts:
                    dve.wait_ge(st_sb, t + 1)
                    nc.vector.bn_aggr(mv[0:tn[t], t, :], st6[0:tn[t], t, :]).then_inc(mv_sb, 1)
                dve.wait_ge(mv_sb, ts[-1] + 1)
                dve.wait_ge(rs_sb, k + 1)
                for t in ts:
                    if t >= 2:
                        dve.wait_ge(x2_ps, t - 1)
                    n = tn[t]
                    nc.vector.tensor_scalar(x2[0:n, t % 2, :], acc[0:n, t, :], mv[0:n, t, 0:1], rs[0:n, t:t + 1],
                                            ALU.subtract, ALU.mult).then_inc(x2_sb, 1)

            step = [0]

            def link(ins):
                step[0] += 1
                ins.then_inc(route, 1)
                dve.wait_ge(route, step[0])

            def over(ap, n):
                return ap.unsqueeze(3).to_broadcast([P, NT, G, n])

            def routing():
                dve.wait_ge(sig_sb, NT)
                dve.wait_ge(w_in, 4 * 16)
                dve.wait_ge(pool_c2, 5)
                link(nc.vector.tensor_scalar(score[:, :, :], score[:, :, :], 1.0, None, ALU.add))
                link(nc.vector.reciprocal(score[:, :, :], score[:, :, :]))
                link(nc.vector.tensor_tensor(sfc[:, :, :], score[:, :, :],
                                             bias[:, :].unsqueeze(1).to_broadcast([P, NT, NX]), ALU.add))
                grp = sfc[:, :, :].rearrange("p t (g k) -> p t g k", g=G)
                eqg = eq[:, :, :].rearrange("p t (g k) -> p t g k", g=G)
                resg = rest[:, :, :].rearrange("p t (g k) -> p t g k", g=G)
                link(nc.vector.tensor_reduce(g1[:, :, :], grp, AX_X, ALU.max))
                link(nc.vector.tensor_tensor(eqg, grp, over(g1[:, :, :], GE), ALU.is_equal))
                link(nc.vector.tensor_reduce(gc[:, :, :], eqg, AX_X, ALU.add))
                link(nc.vector.scalar_tensor_tensor(out=rest[:, :, :].rearrange("p t e -> p (t e)"),
                                                    in0=eq[:, :, :].rearrange("p t e -> p (t e)"), scalar=MASKED,
                                                    in1=sfc[:, :, :].rearrange("p t e -> p (t e)"),
                                                    op0=ALU.mult, op1=ALU.add))
                link(nc.vector.tensor_reduce(g2[:, :, :], resg, AX_X, ALU.max))
                link(nc.vector.tensor_scalar(gc[:, :, :], gc[:, :, :], 1.5, MASKED, ALU.is_lt, ALU.mult))
                link(nc.vector.tensor_tensor(gc[:, :, :], gc[:, :, :], g1[:, :, :], ALU.add))
                link(nc.vector.tensor_tensor(g2[:, :, :], g2[:, :, :], gc[:, :, :], ALU.max))
                link(nc.vector.tensor_tensor(g1[:, :, :], g1[:, :, :], g2[:, :, :], ALU.add))
                ga = over(g1[:, :, :], G)
                gb = g1[:, :, :].unsqueeze(2).to_broadcast([P, NT, G, G])
                link(nc.vector.tensor_tensor(eqg, gb, ga, ALU.is_equal))
                link(nc.vector.tensor_tensor(eqg, eqg, lower[:, :, :].unsqueeze(1).to_broadcast([P, NT, G, G]), ALU.mult))
                link(nc.vector.tensor_tensor(resg, gb, ga, ALU.is_gt))
                link(nc.vector.tensor_tensor(eq[:, :, :], eq[:, :, :], rest[:, :, :], ALU.add))
                link(nc.vector.tensor_reduce(gc[:, :, :], eqg, AX_X, ALU.add))
                link(nc.vector.tensor_scalar(gc[:, :, :], gc[:, :, :], TOPG - 0.5, None, ALU.is_lt))
                link(nc.vector.tensor_tensor(grp, grp, over(gc[:, :, :], GE), ALU.mult))
                link(nc.vector.tensor_scalar(sfc[:, :, :], sfc[:, :, :], 0.0, None, ALU.add))
                for t in range(NT):
                    top = nc.vector.max(top8[:, t, :], sfc[:, t, :])
                link(top)
                for t in range(NT):
                    rep = nc.vector.match_replace(rest[:, t, :], top8[:, t, :], sfc[:, t, :], MASKED)
                link(rep)
                link(nc.vector.tensor_tensor(eq[:, :, :], rest[:, :, :], sfc[:, :, :], ALU.not_equal))
                link(nc.vector.tensor_tensor(eq[:, :, :], eq[:, :, :], score[:, :, :], ALU.mult))
                link(nc.vector.tensor_reduce(wsum[:, :], eq[:, :, :], AX_X, ALU.add))
                link(nc.vector.tensor_scalar(wsum[:, :], wsum[:, :], 1e-20, None, ALU.add))
                link(nc.vector.reciprocal(wsum[:, :], wsum[:, :]))
                link(nc.vector.tensor_tensor(rest[:, :, :], eq[:, :, :],
                                             wsum[:, :].unsqueeze(2).to_broadcast([P, NT, NX]), ALU.mult))
                link(nc.vector.tensor_scalar(comb[:, :, :].rearrange("p e t -> p t e"), rest[:, :, :], ROUTE_SCALE,
                                             None, ALU.mult))

            def add(n, k):
                for q in range(NP):
                    dve.wait_ge(down_ps, n * NP + (q + 1))
                    for t in range(2 * q, min(2 * q + 2, NT)):
                        m = tn[t]
                        w = 1.0 if k is None else cur[0:m, k, t:t + 1]
                        last = nc.vector.scalar_tensor_tensor(
                            out=acc[0:m, t, :], in0=ps[0:m, DN + q % 3, D * (t % 2):D * (t % 2 + 1)], scalar=w,
                            in1=acc[0:m, t, :], op0=ALU.mult, op1=ALU.add)
                    last.then_inc(acc_sb, 1)

            add(0, None)
            routing()
            for n in range(1, NS):
                dve.wait_ge(acc_sb, n * NP)
                add(n, None)
            with dve.Fori(0, NX // 2) as j:
                e = j * 2
                for k in range(2):
                    nc.vector.tensor_copy(cur[:, k, :], comb[:, bass.ds(e + k, 1), :].rearrange("p a t -> p (a t)")
                                          ).then_inc(cur_sb, 1)
                    dve.wait_ge(cur_sb, e + (k + 1))
                    dve.wait_ge(acc_sb, (e + (NS + k)) * NP)
                    add(e + (NS + k), k)

        @block.tensor
        def _(pe):
            pe.wait_ge(pool_c2, 4)
            pe.wait_ge(w_in, 4 * 16)
            for c in range(DC):
                last = nc.tensor.transpose(ps[:, 7, c * NX:(c + 1) * NX], rw_raw[0:NX, c * P:(c + 1) * P],
                                           ident[0:NX, 0:NX])
            last.then_inc(rw_ps, 1)
            for t in range(NT):
                n = tn[t]
                pe.wait_ge(x2_sb, t + 1)
                if t >= 2:
                    pe.wait_ge(x2t_sb, t - 1)
                for c in range(DC):
                    last = nc.tensor.transpose(ps[:, UP + t % 2, c * n:(c + 1) * n], x2[0:n, t % 2, c * P:(c + 1) * P],
                                               ident[0:n, 0:n])
                last.then_inc(x2_ps, 1)
            pe.wait_ge(rw_sb, 1)
            pe.wait_ge(x2t_sb, NT)
            for t in range(NT):
                n = tn[t]
                if t >= 2:
                    pe.wait_ge(sig_sb, t - 1)
                for c in range(DC):
                    last = nc.tensor.matmul(ps[0:n, LG + t % 2, 0:NX], x2t[:, c, P * t:P * t + n], rw_t[:, c, :],
                                            start=(c == 0), stop=(c == DC - 1))
                last.then_inc(logit_ps, 1)
            pe.wait_ge(sig_sb, NT)

            def up(n, w):
                for u in range(NU):
                    if not (isinstance(n, int) and n == 0):
                        pe.wait_ge(relu_sb, (n - 1) * NU + (u + 1))
                    for c in range(DC):
                        last = nc.tensor.matmul(ps[:, UP + u, 0:u0[u + 1] - u0[u]], w(c), x2t[:, c, u0[u]:u0[u + 1]],
                                                start=(c == 0), stop=(c == DC - 1))
                    last.then_inc(up_ps, 1)

            def down(n, k, w):
                for q in range(NP):
                    if isinstance(n, int) and n == 0:
                        if q >= 3:
                            pe.wait_ge(acc_sb, q - 2)
                    else:
                        pe.wait_ge(acc_sb, (n - 1) * NP + (NP + q - 2))
                    for t in range(2 * q, min(2 * q + 2, NT)):
                        pe.wait_ge(hid_sb, n * NU + (upto[t] + 1))
                        last = nc.tensor.matmul(ps[0:tn[t], DN + q % 3, D * (t % 2):D * (t % 2 + 1)],
                                                hid[:, k, P * t:P * t + tn[t]], w, start=True, stop=True)
                    last.then_inc(down_ps, 1)

            def shared_up(n):
                up(n, lambda c: wus[:, c, n * I:(n + 1) * I])

            def routed_up(e, k, loads):
                pe.wait_ge(wu_in[k], loads)
                up(e + NS, lambda c: wu[:, k, c, :])

            def routed_down(e, k, loads):
                pe.wait_ge(wd_in[k], loads)
                down(e + NS, k, wd[:, k, :])

            shared_up(0)
            for n in range(NS - 1):
                shared_up(n + 1)
                down(n, n % 2, wds[:, n, :])
            routed_up(0, 0, 16)
            down(NS - 1, (NS - 1) % 2, wds[:, NS - 1, :])
            with pe.Fori(0, NX // 2 - 1) as j:
                e = j * 2
                routed_up(e + 1, 1, e * 8 + 16)
                routed_down(e, 0, e * 8 + 16)
                routed_up(e + 2, 0, e * 8 + 32)
                routed_down(e + 1, 1, e * 8 + 16)
            routed_up(NX - 1, 1, (NX // 2) * 16)
            routed_down(NX - 2, 0, (NX // 2) * 16)
            routed_down(NX - 1, 1, (NX // 2) * 16)


_INS = ['x', 'cls_tok', 'L0_tok_W0', 'L0_tok_W1', 'L0_tok_Wo', 'L0_attn_Wq1', 'L0_attn_Wq2', 'L0_attn_Wk1',
        'L0_attn_Wk2', 'L0_attn_Wv', 'L0_attn_Wc', 'L0_attn_lq1', 'L0_attn_lk1', 'L0_attn_lq2', 'L0_attn_lk2',
        'L0_ffn_router_w', 'L0_ffn_correction_bias', 'L0_ffn_up_w', 'L0_ffn_down_w', 'L0_ffn_shared_up_w',
        'L0_ffn_shared_down_w']
_OUTS = [((4, 513, 256), 'float32')]


def kernel(**inputs):
    import numpy as _np
    import concourse.bacc as _bacc
    from concourse import mybir as _mybir
    from concourse.bass_utils import run_bass_kernel_spmd as _run

    nc = _bacc.Bacc("TRN2", target_bir_lowering=False, num_devices=1)
    arrays, args = {}, []
    for name in _INS:
        a = _np.ascontiguousarray(inputs[name])
        arrays[f"in_{name}_dram"] = a
        args.append(nc.dram_tensor(f"in_{name}_dram", a.shape, _mybir.dt.from_np(a.dtype), kind="ExternalInput").ap())
    for i, (shape, dtype) in enumerate(_OUTS):
        dt = _mybir.dt.from_np(_np.dtype(dtype))
        args.append(nc.dram_tensor(f"out_{i}_dram", shape, dt, kind="ExternalOutput").ap())
    vit_layer(nc, *args)
    r = _run(nc, [arrays], core_ids=[0])
    got = tuple(r.results[0][f"out_{i}_dram"] for i in range(len(_OUTS)))
    return got[0]
```

```python
from contextlib import ExitStack
import math

import concourse.bass as bass
from concourse import mybir

ALU = mybir.AluOpType
ACT = mybir.ActivationFunctionType
F32 = mybir.dt.float32
BF16 = mybir.dt.bfloat16
F32R = mybir.dt.float32r
AX_X = mybir.AxisListType.X

LN_EPS = 1e-05
LAMBDA_INIT = 0.8 - 0.6 * math.exp(-0.3 * (2 - 1))
ROUTE_SCALE = 2.5
MASKED = -1.0e30


def wait(eng, sem, value):
    if not (isinstance(value, int) and value <= 0):
        eng.wait_ge(sem, value)


def vit_layer(nc, x, cls_tok, W0, W1, Wo, Wq1, Wq2, Wk1, Wk2, Wv, Wc, lq1, lk1, lq2, lk2,
              router_w, correction_bias, up_w, down_w, shared_up_w, shared_down_w, out):
    B, S, D, E = x.shape
    P = 128
    T = S + 1
    DC = D // P
    DE = W0.shape[0]
    EC = DE // P
    H = lq1.shape[0]
    HS = lq1.shape[1]
    VD = 2 * HS
    HG = P // (2 * HS)
    NG = H // HG
    XT = S // P
    NQ = S // P
    NR = NQ + 1
    rn = [P] * NQ + [T - S]

    N = B * T
    NT = -(-N // P)
    tn = [min(P, N - P * t) for t in range(NT)]
    NX = up_w.shape[0]
    I = up_w.shape[2]
    NS = shared_up_w.shape[1] // I
    NE = NX + NS
    G = 8
    GE = NX // G
    TOPG = 4
    NU = 5
    u0 = [2 * (N * u // (2 * NU)) for u in range(NU + 1)]
    NP = -(-NT // 2)
    upto = [min(u for u in range(NU) if u0[u + 1] >= min(P * (t + 1), N)) for t in range(NT)]

    h_dram = nc.dram_tensor("h_scratch", [N, D], F32, kind="Internal").ap()
    o_dram = nc.dram_tensor("o_scratch", [N, D], F32, kind="Internal").ap()
    out_rows = out.rearrange("b t d -> (b t) d")

    with ExitStack() as ctx:
        def sb(name, shape, dt=F32):
            return ctx.enter_context(nc.sbuf_tensor(name, shape, dt))

        def sem(name):
            return ctx.enter_context(nc.semaphore(name))

        ps = ctx.enter_context(nc.psum_tensor("ps", [P, 8, 512], F32))

        TC = 3 * HS
        ident = sb("ident", [P, P])
        identb = sb("identb", [P, P], BF16)
        causal = sb("causal", [P, P], BF16)
        sel = sb("sel", [P, 2, 2, HG, P], F32R)
        which = sb("which", [P, HG, 2])
        blk = sb("blk", [P, NG, TC])
        qblk = sb("qblk", [P, 2, NG * TC + P - TC], F32R)
        own_head = sb("own_head", [H, H * VD])
        ones = sb("ones", [P, 1])
        first_row = sb("first_row", [1, P])
        cls_row = sb("cls_row", [1, D])
        neg_half = sb("neg_half", [P, HG * NQ])
        eps = sb("eps", [P, NR])
        unused = sb("unused", [P, 1])
        lam_in = sb("lam_in", [P, 4, H, HS])
        lam_s = sb("lam_s", [P, 2, H])
        neg_lam = sb("neg_lam", [P, H])
        lam_diag = sb("lam_diag", [H, H])
        neg_lam_col = sb("neg_lam_col", [H, 1])
        w0t = sb("w0t", [P, DC, DE])
        w1t = sb("w1t", [P, DC, DE])
        wot = sb("wot", [P, EC, D])
        wq = sb("wq", [P, DC, NG * P])
        wk = sb("wk", [P, DC, NG * P])
        wv = sb("wv", [P, DC, H * VD])
        wc = sb("wc", [P, H * VD // P, D])
        xraw = sb("xraw", [P, XT, D * E])
        xt_tok = sb("xt_tok", [P, DC, S])
        gate = sb("gate", [P, 2, S // 2])
        hid_tok = sb("hid_tok", [P, EC, T])
        h = sb("h", [P, NR, D])
        st6 = sb("st6", [P, NR, 6])
        mv = sb("mv", [P, NR, 2])
        rs = sb("rs", [P, NR])
        xh = sb("xh", [P, 2, D])
        xt = sb("xt", [P, DC, T])
        qs = sb("qs", [P, 2, NG, T + 1], F32R)
        ks = sb("ks", [P, 2, NG, T + 1], F32R)
        q4 = sb("q4", [P, 2, 2, S], F32R)
        k4 = sb("k4", [P, 2, S], F32R)
        v = sb("v", [P, NR, H * VD])
        po = [P * i * (i + 1) // 2 for i in range(NQ + 1)]
        pr = sb("pr", [P, 2, 2, po[NQ]])
        negm = sb("negm", [P, 2, NQ, 2])
        lsum = sb("lsum", [P, 2, 2, NQ])
        rc = sb("rc", [P, 2, 2, NQ])
        coef = sb("coef", [P, 2, NQ])
        att_t = sb("att_t", [P, po[NQ]])
        yraw = sb("yraw", [P, HG * NQ, VD])
        ytail = sb("ytail", [1, H, VD])
        y = sb("y", [P, HG * NQ, VD])
        ysum = sb("ysum", [P, 2, HG * NQ])
        ysq = sb("ysq", [P, HG * NQ, VD])
        yrs = sb("yrs", [P, HG * NQ])
        yn = sb("yn", [P, NR, H * VD])
        yt = sb("yt", [P, H * VD // P, P])
        o = sb("o", [P, NR, D])
        pt = sb("pt", [TC, T])
        pt2 = sb("pt2", [H, T])
        negt = sb("negt", [TC, 1])
        lt = sb("lt", [TC, 1])
        lt2 = sb("lt2", [H, 1])
        rt = sb("rt", [H, 2])
        ct = sb("ct", [H, 1])
        att_tail = sb("att_tail", [P, NR * H])
        tm = sb("tm", [H, H * VD])

        names = """consts_in wtok_in wattn_in x_in pool_const dve_const setup lam_exp wt_ps wt_even wt_odd
            x_ps x_sb gu_ps gate_sb hid_sb to_ps h_sb st_sb mv_sb veps_sb rs_sb xh_sb xht_ps xht_sb
            qk_ps hi_sb lo_sb qkt_ps qkt_hi qkt_lo qblk_sb v_ps v_sb rp_ps rpq_sb rpk_sb
            ts_ps tmax_sb texp_sb tcopy_sb tstep tatt_sb tt_ps tt_sb tv_ps tm_sb ty_ps ty_sb
            s_ps max_sb exp_sb coef_sb att_sb att_ps attt_even attt_odd pv_ps y_sb
            nstep yc_sb ysq_sb yvar_sb yrs_sb yrs_scaled yn_sb yt_ps yt_sb pc_ps pc_sb h_out o_out""".split()
        sems = {n: sem(n) for n in names}
        (consts_in, wtok_in, wattn_in, x_in, pool_const, dve_const, setup, lam_exp, wt_ps, wt_even, wt_odd,
         x_ps, x_sb, gu_ps, gate_sb, hid_sb, to_ps, h_sb, st_sb, mv_sb, veps_sb, rs_sb, xh_sb, xht_ps, xht_sb,
         qk_ps, hi_sb, lo_sb, qkt_ps, qkt_hi, qkt_lo, qblk_sb, v_ps, v_sb, rp_ps, rpq_sb, rpk_sb,
         ts_ps, tmax_sb, texp_sb, tcopy_sb, tstep, tatt_sb, tt_ps, tt_sb, tv_ps, tm_sb, ty_ps, ty_sb,
         s_ps, max_sb, exp_sb, coef_sb, att_sb, att_ps, attt_even, attt_odd, pv_ps, y_sb,
         nstep, yc_sb, ysq_sb, yvar_sb, yrs_sb, yrs_scaled, yn_sb, yt_ps, yt_sb, pc_ps, pc_sb, h_out, o_out
         ) = (sems[n] for n in names)

        TP = 4
        YB = 6
        BG = 7
        SLOTS = H * NQ
        GU = 2 * EC
        NN = NG + 1
        L_ATT, L_TURN, L_PV = NQ, NQ + 1, NQ + 3
        last_slot = SLOTS - 1 + L_PV
        V_ORDER = (0, NQ, 1, 2, 3)
        NORM_Y = 3

        flat = pr[:, :, :, :].rearrange("p a b n -> p (a b n)")
        w0_raw = flat[:, 0:EC * D].rearrange("p (c d) -> p c d", c=EC)
        w1_raw = flat[:, EC * D:2 * EC * D].rearrange("p (c d) -> p c d", c=EC)
        wo_raw = flat[:, 2 * EC * D:2 * EC * D + DC * DE].rearrange("p (c d) -> p c d", c=DC)
        wt_jobs = []
        for raw, dst in ((w0_raw, w0t), (w1_raw, w1t)):
            for d in range(DC):
                for e in range(EC):
                    wt_jobs.append((raw[:, e, d * P:(d + 1) * P], dst[:, d, e * P:(e + 1) * P]))
        for e in range(EC):
            for d in range(DC):
                wt_jobs.append((wo_raw[:, d, e * P:(e + 1) * P], wot[:, e, d * P:(d + 1) * P]))

        def token_pieces():
            return ([("x", c) for c in range(DC)] + [("gu", k) for k in range(GU)] + [("to", i) for i in range(NR)]
                    + [("xh", i) for i in range(NR)] + [("qkt", 0)])

        def schedule(first, last):
            at = [[] for _ in range(2 * (last_slot + 1))]
            for n in range(1, H):
                at[2 * (NQ * n - 3) + 1].append(("rp", 2 * n, 0))
                at[2 * (NQ * n - 2)].append(("rp", 2 * n + 1, 0))
            free = []
            for sl in range(SLOTS):
                i = sl % NQ
                free += {0: [2 * sl, 2 * sl + 1], 1: [2 * sl], 2: [2 * sl + 1],
                         3: [2 * sl] if sl < 2 * NQ else []}[i]

            def place(kind, i, t, not_before=0):
                while free[0] < not_before:
                    free.pop(0)
                if not (first and t < 0) and not (last and t > 0):
                    at[free[0]].append((kind, i, t))
                free.pop(0)

            for i in V_ORDER:
                place("v", i, 0)
            for i in range(NR):
                place("yt", i, -1, 2 * NORM_Y)
                place("pc", i, -1)
            for kind in ("tt", "tv", "ty"):
                place(kind, 0, 0)
            for kind, i in token_pieces():
                if kind == "xh" and i == 0:
                    place(kind, i, 1, free[0] + 2 * NQ)
                else:
                    place(kind, i, 1)
            for j in range(2 * NG):
                place("qk", j, 1, 2 * (NQ * (HG * (j // 2 + 1) - 1) - 1))
            if not last:
                at[2 * SLOTS].append(("rp", 0, 1))
                at[2 * SLOTS + 2].append(("rp", 1, 1))
            return at

        prologue = ([(k, i, 0) for k, i in token_pieces()] + [("qk", j, 0) for j in range(2 * NG)]
                    + [("rp", 0, 0), ("rp", 1, 0)])

        plan = schedule(False, False)
        slot_of = {piece: k // 2 for k, at_k in enumerate(plan) for piece in at_k}
        last_piece = [piece for at_k in plan for piece in at_k][-1]
        centre_slot = [slot_of[("ty", 0, 0)] + 1] + [NQ * HG * k + L_PV for k in range(1, NG)]
        norm_rows = [slot_of[("xh", i, 1)] - 1 for i in range(NR)]

        def bank_of(k):
            return {(0, 1): 1, (1, 1): 3}.get((k // 2 % NQ, k % 2), BG) if k < 2 * SLOTS else BG

        def score_view(i):
            nk, k = P * (i + 1), 2 * (i % 2)
            if 2 * nk <= 512:
                return ps[:, k, :].rearrange("p (m n) -> p m n", m=2)[:, :, 0:nk]
            return ps[:, k:k + 2, 0:nk]

        def left(kind, i, t):
            return {"x": (x_sb, t * DC + (i + 1)), "gu": (hid_sb, t * GU + (i + 1)), "to": (h_sb, t * NR + (i + 1)),
                    "xh": (xht_sb, t * NR + (i + 1)), "qk": (lo_sb, t * (2 * NG) + (i + 1)), "qkt": (qkt_lo, t + 1),
                    "v": (v_sb, t * NR + (i + 1)), "tt": (tt_sb, t + 1), "tv": (tm_sb, t + 1), "ty": (ty_sb, t + 1),
                    "rp": ((rpq_sb, rpk_sb)[i % 2], t * H + (i // 2 + 1)),
                    "yt": (yt_sb, t * NR + (i + 1)), "pc": (pc_sb, t * NR + (i + 1))}[kind]

        block = ctx.enter_context(nc.Block())

        def load_x(sp, b):
            sp.dma_start(xraw[:, :, :], x[b].rearrange("(t p) d e -> p t (d e)", p=P)).then_inc(x_in, 16)

        @block.sync
        def _(sp):
            load_x(sp, 0)
            sp.dma_start(w0_raw, W0.rearrange("(c p) d -> p c d", p=P)).then_inc(wtok_in, 16)
            sp.dma_start(w1_raw, W1.rearrange("(c p) d -> p c d", p=P)).then_inc(wtok_in, 16)
            sp.dma_start(wo_raw, Wo.rearrange("(c p) d -> p c d", p=P)).then_inc(wtok_in, 16)
            for k, w in enumerate((lq1, lk1, lq2, lk2)):
                sp.dma_start(lam_in[:, k, :, :], w.partition_broadcast(P)).then_inc(consts_in, 16)
            sp.dma_start(cls_row[0:1, :], cls_tok.rearrange("a b d -> (a b) d")).then_inc(consts_in, 16)
            for w, dst in (((Wq1, Wq2), wq), ((Wk1, Wk2), wk)):
                for m in range(2):
                    for c in range(DC):
                        sp.dma_start(dst[:, c, :].rearrange("p (j m k) -> p j m k", m=2, k=HS)[:, :, m, :],
                                     w[m][c * P:(c + 1) * P, :].rearrange("p (j k) -> p j k", k=HS)
                                     ).then_inc(wattn_in, 16)
            sp.dma_start(wv[:, :, :], Wv.rearrange("(c p) d -> p c d", p=P)).then_inc(wattn_in, 16)
            sp.dma_start(wc[:, :, :], Wc.rearrange("(c p) d -> p c d", p=P)).then_inc(wattn_in, 16)

            def store(b, ready, src, dst, done):
                for i in range(NR):
                    sp.wait_ge(ready, b * NR + (i + 1))
                    sp.dma_start(dst[bass.ds(b * T + P * i, rn[i]), :], src[0:rn[i], i, :]).then_inc(done, 16)

            sp.wait_ge(x_ps, DC)
            load_x(sp, 1)
            store(0, h_sb, h, h_dram, h_out)
            sp.wait_ge(x_ps, 2 * DC)
            load_x(sp, 2)
            store(1, h_sb, h, h_dram, h_out)
            with sp.Fori(1, B - 2) as b:
                sp.wait_ge(x_ps, b * DC + 2 * DC)
                load_x(sp, b + 2)
                store(b - 1, pc_sb, o, o_dram, o_out)
                store(b + 1, h_sb, h, h_dram, h_out)
            store(B - 3, pc_sb, o, o_dram, o_out)
            store(B - 1, h_sb, h, h_dram, h_out)
            store(B - 2, pc_sb, o, o_dram, o_out)
            store(B - 1, pc_sb, o, o_dram, o_out)
            sp.wait_ge(h_out, 16 * NR * B)
            sp.wait_ge(o_out, 16 * NR * B)

        @block.gpsimd
        def _(pool):
            nc.gpsimd.memset(ident[:, :], 0.0).then_inc(pool_const, 1)
            nc.gpsimd.memset(causal[:, :], 0.0).then_inc(pool_const, 1)
            nc.gpsimd.memset(first_row[:, :], 0.0).then_inc(pool_const, 1)
            nc.gpsimd.memset(own_head[:, :], 1.0).then_inc(pool_const, 1)
            nc.gpsimd.memset(neg_half[:, :], -0.5).then_inc(pool_const, 1)
            nc.gpsimd.memset(eps[:, :], LN_EPS).then_inc(pool_const, 1)
            nc.gpsimd.memset(ones[:, :], 1.0).then_inc(pool_const, 1)
            pool.wait_ge(pool_const, 7)
            nc.gpsimd.affine_select(out=ident[:, :], in_=ident[:, :], compare_op=ALU.not_equal, fill=1.0,
                                    base=0, pattern=[[-1, P]], channel_multiplier=1).then_inc(pool_const, 1)
            nc.gpsimd.affine_select(out=causal[:, :], in_=causal[:, :], compare_op=ALU.is_ge, fill=MASKED,
                                    base=0, pattern=[[-1, P]], channel_multiplier=1).then_inc(pool_const, 1)
            nc.gpsimd.affine_select(out=own_head[:, :], in_=own_head[:, :], compare_op=ALU.is_ge, fill=0.0,
                                    base=0, pattern=[[1, H * VD]], channel_multiplier=-VD).then_inc(pool_const, 1)
            pool.wait_ge(pool_const, 10)
            nc.gpsimd.affine_select(out=own_head[:, :], in_=own_head[:, :], compare_op=ALU.is_ge, fill=0.0,
                                    base=VD - 1, pattern=[[-1, H * VD]], channel_multiplier=VD
                                    ).then_inc(pool_const, 1)
            nc.gpsimd.tensor_copy(identb[:, :], ident[:, :]).then_inc(pool_const, 1)
            nc.gpsimd.memset(first_row[0:1, 0:1], 1.0).then_inc(pool_const, 1)

            def norm_scale(t):
                wait(pool, mv_sb, t * NR + NR)
                nc.gpsimd.tensor_tensor(rs[:, :], mv[:, :, 1], eps[:, :], ALU.add).then_inc(veps_sb, 1)
                pool.wait_ge(veps_sb, t + 1)
                nc.gpsimd.tensor_tensor(rs[:, :], rs[:, :], neg_half[:, 0:NR], ALU.pow).then_inc(rs_sb, 1)

            def head_scale(b, k):
                m = 1 if k == 0 else P
                pool.wait_ge(yc_sb, b * NN + (k + 1))
                nc.gpsimd.tensor_tensor(ysq[0:m, :, :], y[0:m, :, :], y[0:m, :, :], ALU.mult).then_inc(ysq_sb, 1)
                pool.wait_ge(yvar_sb, b * NN + (k + 1))
                nc.gpsimd.tensor_tensor(yrs[0:m, :], ysum[0:m, 1, :], neg_half[0:m, :], ALU.pow).then_inc(yrs_sb, 1)

            def batch(b, first, last):
                if not first:
                    head_scale(b - 1, NG)
                todo = [(centre_slot[k], k) for k in range(NG)]
                if not last:
                    todo.append((slot_of[("to", NR - 1, 1)], None))
                for _, k in sorted(todo, key=lambda e: e[0]):
                    if k is None:
                        norm_scale(b + 1)
                    else:
                        head_scale(b, k)

            norm_scale(0)
            batch(0, True, False)
            with pool.Fori(1, B - 1) as b:
                batch(b, False, False)
            batch(B - 1, False, True)
            head_scale(B - 1, NG)

        @block.scalar
        def _(act):
            act.wait_ge(dve_const, 6)
            nc.scalar.activation(lam_s[:, :, :], lam_s[:, :, :], ACT.Exp).then_inc(lam_exp, 1)
            for n, (_, dst) in enumerate(wt_jobs):
                if n % 2 == 0:
                    act.wait_ge(wt_ps, n + 1)
                    nc.scalar.copy(dst, ps[:, n % 8, 0:P]).then_inc(wt_even, 1)

            def piece(kind, i, t, bank):
                src = ps[:, bank, :]
                if kind == "x":
                    act.wait_ge(x_ps, t * DC + (i + 1))
                    wait(act, gu_ps, t * GU)
                    nc.scalar.copy(xt_tok[:, i, :], src).then_inc(x_sb, 1)
                elif kind == "gu":
                    act.wait_ge(gu_ps, t * GU + (i + 1))
                    wait(act, hid_sb, t * GU + max(i - 1, 0))
                    nc.scalar.activation(gate[:, i % 2, :], src[:, 0:S // 2], ACT.Relu).then_inc(gate_sb, 1)
                elif kind == "xh":
                    act.wait_ge(xht_ps, t * NR + (i + 1))
                    wait(act, v_ps, t * NR)
                    nc.scalar.copy(xt[:, :, P * i:P * i + rn[i]],
                                   src[:, 0:DC * rn[i]].rearrange("p (c n) -> p c n", c=DC)).then_inc(xht_sb, 1)
                elif kind == "qk":
                    g = i // 2
                    act.wait_ge(qk_ps, t * (2 * NG) + (i + 1))
                    wait(act, rp_ps, t * (2 * H) - 2 * H + 2 * HG * (g + 1))
                    dst = (qs, ks)[i % 2]
                    nc.scalar.activation(dst[:, 0, g, 0:S], src, ACT.Copy, scale=(HS ** -0.5, 1.0)[i % 2]
                                         ).then_inc(hi_sb, 1)
                elif kind == "qkt":
                    act.wait_ge(qkt_ps, t + 1)
                    wait(act, ts_ps, t)
                    nc.scalar.activation(qs[:, 0, :, S:T].rearrange("p g n -> p (g n)"), src[:, 0:NG], ACT.Copy,
                                         scale=HS ** -0.5)
                    nc.scalar.activation(ks[:, 0, :, S:T].rearrange("p g n -> p (g n)"), src[:, NG:2 * NG], ACT.Copy
                                         ).then_inc(qkt_hi, 1)
                elif kind == "v":
                    m = rn[i]
                    act.wait_ge(v_ps, t * NR + (V_ORDER.index(i) + 1))
                    wait(act, pv_ps, t * SLOTS)
                    wait(act, tv_ps, t)
                    nc.scalar.copy(v[0:m, i, :], src[0:m, :]).then_inc(v_sb, 1)
                elif kind == "rp" and i % 2 == 0:
                    n = i // 2
                    act.wait_ge(rp_ps, t * (2 * H) + (i + 1))
                    wait(act, s_ps, t * SLOTS + NQ * (n - 1))
                    for m in range(2):
                        rows = slice(4 * HS * m, 4 * HS * (m + 1))
                        q = nc.scalar.copy(q4[rows, n % 2, m, :], src[rows, :])
                    q.then_inc(rpq_sb, 1)
                elif kind == "yt":
                    act.wait_ge(yt_ps, t * NR + (i + 1))
                    nc.scalar.copy(yt[:, :, 0:rn[i]],
                                   src[:, 0:H * VD // P * rn[i]].rearrange("p (c n) -> p c n", n=rn[i])
                                   ).then_inc(yt_sb, 1)
                elif kind == "pc":
                    act.wait_ge(pc_ps, t * NR + (i + 1))
                    nc.scalar.copy(o[0:rn[i], i, :], src[0:rn[i], 0:D]).then_inc(pc_sb, 1)

            def tail_exp(b):
                act.wait_ge(tmax_sb, b + 1)
                wait(act, tatt_sb, b)
                nc.scalar.activation(pt[:, :], ps[0:TC, 0:2, :].rearrange("p k n -> p (k n)")[:, 0:T], ACT.Exp,
                                     bias=negt[:, 0:1], accum_out=lt[:, 0:1]).then_inc(texp_sb, 1)
                act.wait_ge(texp_sb, b + 1)
                wait(act, tt_ps, b)
                nc.scalar.copy(pt2[:, :], pt[2 * HS:3 * HS, :])
                nc.scalar.copy(lt2[:, :], lt[2 * HS:3 * HS, :]).then_inc(tcopy_sb, 1)

            def batch(b, first, last):
                at = schedule(first, last)
                for s in range(last_slot + 1):
                    c = s - L_TURN - 1
                    if c >= 0 and c < SLOTS and c % 2 == 1:
                        i = c % NQ
                        act.wait_ge(att_ps, b * SLOTS + (c + 1))
                        wait(act, pv_ps, b * SLOTS + max(c - NQ + 1, 0))
                        nc.scalar.copy(att_t[:, po[i]:po[i + 1]], ps[:, TP + 1, 0:P * (i + 1)]).then_inc(attt_odd, 1)
                    for kind, i, dt in at[2 * s]:
                        piece(kind, i, b + dt, bank_of(2 * s))
                    if s == SLOTS // 2 and not first:
                        act.wait_ge(o_out, b * (NR * 16))
                    if s < SLOTS:
                        n, i = divmod(s, NQ)
                        nk = P * (i + 1)
                        act.wait_ge(max_sb, b * SLOTS + (s + 1))
                        wait(act, att_ps, b * SLOTS + (s - 2 * NQ + 1 if n >= 2 else 0))
                        for m in range(2):
                            e = nc.scalar.activation(pr[:, n % 2, m, po[i]:po[i] + nk], score_view(i)[:, m, :],
                                                     ACT.Exp, bias=negm[:, n % 2, i, m:m + 1],
                                                     accum_out=lsum[:, n % 2, m, i:i + 1])
                        e.then_inc(exp_sb, 1)
                    if s == SLOTS + 1 and not last:
                        tail_exp(b + 1)
                    for kind, i, dt in at[2 * s + 1]:
                        piece(kind, i, b + dt, bank_of(2 * s + 1))

            for k, (kind, i, t) in enumerate(prologue):
                piece(kind, i, t, k % 4)
            tail_exp(0)
            batch(0, True, False)
            with act.Fori(1, B - 1) as b:
                batch(b, False, False)
            batch(B - 1, False, True)
            for k in range(2 * NR):
                piece(("yt", "pc")[k % 2], k // 2, B - 1, BG)

        @block.vector
        def _(dve):
            nc.vector.memset(mv[:, :, :], 1.0).then_inc(dve_const, 1)
            nc.vector.memset(hid_tok[:, :, 0:1], 0.0).then_inc(dve_const, 1)
            nc.vector.memset(sel[:, :, :, :, :].bitcast(F32), 0.0).then_inc(setup, 1)
            nc.vector.memset(blk[:, :, :], 0.0).then_inc(setup, 1)
            nc.vector.memset(q4[:, :, :, :].bitcast(F32), 0.0).then_inc(dve_const, 1)
            nc.vector.memset(qblk[:, :, :].bitcast(F32), 0.0).then_inc(setup, 1)
            nc.vector.memset(qs[:, :, :, T:T + 1].bitcast(F32), 0.0).then_inc(dve_const, 1)
            nc.vector.memset(ks[:, :, :, T:T + 1].bitcast(F32), 0.0).then_inc(dve_const, 1)
            dve.wait_ge(consts_in, 5 * 16)
            nc.vector.tensor_tensor(lam_in[:, 0:2, :, :], lam_in[:, 0:4:2, :, :], lam_in[:, 1:4:2, :, :], ALU.mult
                                    ).then_inc(setup, 1)
            dve.wait_ge(setup, 4)
            nc.vector.tensor_reduce(lam_s[:, :, :], lam_in[:, 0:2, :, :], AX_X, ALU.add).then_inc(dve_const, 1)
            dve.wait_ge(pool_const, 13)
            nc.vector.tensor_reduce(which[:, :, :], ident[:, :].rearrange("p (j m d) -> p j m d", m=2, d=HS), AX_X,
                                    ALU.add).then_inc(setup, 1)
            for qk, places in enumerate((((0, 1), (2, 3)), ((0, 2), (1, 3)))):
                for part in range(2):
                    for j in range(HG):
                        for c in places[part]:
                            cp = nc.vector.tensor_copy(
                                sel[:, qk, part, j, :].rearrange("p (m c d) -> p m c d", m=2, d=HS)[:, :, c, :],
                                ident[:, 2 * HS * j:2 * HS * (j + 1)].rearrange("p (m d) -> p m d", m=2))
            cp.then_inc(setup, 1)
            dve.wait_ge(setup, 6)
            for g in range(NG):
                for m in range(2):
                    cp = nc.vector.tensor_copy(blk[:, g, 2 * HS * m + HG * g:2 * HS * m + HG * (g + 1)],
                                               which[:, :, m])
            cp.then_inc(setup, 1)
            dve.wait_ge(lam_exp, 1)
            nc.vector.tensor_tensor(neg_lam[:, :], lam_s[:, 1, :], lam_s[:, 0, :], ALU.subtract).then_inc(setup, 1)
            dve.wait_ge(setup, 8)
            nc.vector.tensor_scalar(neg_lam[:, :], neg_lam[:, :], -LAMBDA_INIT, None, ALU.add).then_inc(setup, 1)
            dve.wait_ge(setup, 9)
            nc.vector.tensor_tensor(lam_diag[:, :], neg_lam[0:H, :], ident[0:H, 0:H], ALU.mult).then_inc(setup, 1)
            dve.wait_ge(setup, 10)
            nc.vector.tensor_reduce(neg_lam_col[:, :], lam_diag[:, :], AX_X, ALU.add).then_inc(setup, 1)
            for n, (_, dst) in enumerate(wt_jobs):
                if n % 2 == 1:
                    dve.wait_ge(wt_ps, n + 1)
                    nc.vector.tensor_copy(dst, ps[:, n % 8, 0:P]).then_inc(wt_odd, 1)
            dve.wait_ge(setup, 11)

            def piece(kind, i, t, bank):
                src = ps[:, bank, :]
                if kind == "gu":
                    c, half = divmod(i, 2)
                    dve.wait_ge(gate_sb, t * GU + (i + 1))
                    wait(dve, to_ps, t * NR)
                    nc.vector.tensor_tensor(hid_tok[:, c, 1 + S // 2 * half:1 + S // 2 * (half + 1)], gate[:, i % 2, :],
                                            src[:, S // 2:S], ALU.mult).then_inc(hid_sb, 1)
                elif kind == "to":
                    m = rn[i]
                    dve.wait_ge(to_ps, t * NR + (i + 1))
                    wait(dve, h_out, t * (NR * 16))
                    nc.vector.tensor_copy(h[0:m, i, :], src[0:m, 0:D]).then_inc(h_sb, 1)
                    dve.wait_ge(h_sb, t * NR + (i + 1))
                    nc.vector.bn_stats(st6[0:m, i, :], h[0:m, i, :]).then_inc(st_sb, 1)
                    if i == NR - 1:
                        dve.wait_ge(st_sb, t * NR + NR)
                        nc.vector.memset(unused[:, :], 0.0)
                        for j in range(NR):
                            nc.vector.bn_aggr(mv[0:rn[j], j, :], st6[0:rn[j], j, :]).then_inc(mv_sb, 1)
                elif kind == "qk":
                    g = i // 2
                    dst = (qs, ks)[i % 2]
                    dve.wait_ge(hi_sb, t * (2 * NG) + (i + 1))
                    nc.vector.scalar_tensor_tensor(out=dst[:, 1, g, 0:S], in0=src, scalar=(HS ** -0.5, 1.0)[i % 2],
                                                   in1=dst[:, 0, g, 0:S].bitcast(F32), op0=ALU.mult,
                                                   op1=ALU.subtract).then_inc(lo_sb, 1)
                elif kind == "qkt":
                    dve.wait_ge(qkt_hi, t + 1)
                    for dst, a, sc in ((qs, 0, HS ** -0.5), (ks, NG, 1.0)):
                        lo = nc.vector.scalar_tensor_tensor(
                            out=dst[:, 1, :, S:T].rearrange("p g n -> p (g n)"), in0=src[:, a:a + NG], scalar=sc,
                            in1=dst[:, 0, :, S:T].bitcast(F32).rearrange("p g n -> p (g n)"), op0=ALU.mult,
                            op1=ALU.subtract)
                    lo.then_inc(qkt_lo, 1)
                    dve.wait_ge(qkt_lo, t + 1)
                    for part in range(2):
                        for g in range(NG):
                            q = nc.vector.tensor_scalar(qblk[:, part, TC * g:TC * (g + 1)], blk[:, g, :],
                                                        qs[:, part, g, S:T].bitcast(F32), None, ALU.mult)
                    q.then_inc(qblk_sb, 1)
                elif kind == "rp" and i % 2 == 1:
                    n = i // 2
                    dve.wait_ge(rp_ps, t * (2 * H) + (i + 1))
                    wait(dve, s_ps, t * SLOTS + NQ * (n - 1))
                    nc.vector.tensor_copy(k4[:, n % 2, :], src).then_inc(rpk_sb, 1)
                elif kind == "tt":
                    dve.wait_ge(tt_ps, t + 1)
                    nc.vector.tensor_copy(att_tail[:, 0:NQ * H], src[:, 0:NQ * H])
                    nc.vector.tensor_copy(att_tail[0:1, NQ * H:NR * H], src[0:1, NQ * H:NR * H]).then_inc(tt_sb, 1)
                elif kind == "tv":
                    dve.wait_ge(tv_ps, t + 1)
                    nc.vector.tensor_tensor(tm[:, :], own_head[:, :], src[0:H, :], ALU.mult).then_inc(tm_sb, 1)
                elif kind == "ty":
                    dve.wait_ge(ty_ps, t + 1)
                    nc.vector.tensor_copy(ytail[:, :, :].rearrange("p h d -> p (h d)"), src[0:1, :]
                                          ).then_inc(ty_sb, 1)

            def normalise(t, i):
                m = rn[i]
                dve.wait_ge(rs_sb, t + 1)
                wait(dve, xht_ps, t * NR + max(i - 1, 0))
                nc.vector.tensor_scalar(xh[0:m, i % 2, :], h[0:m, i, :], mv[0:m, i, 0:1], rs[0:m, i:i + 1],
                                        ALU.subtract, ALU.mult).then_inc(xh_sb, 1)

            def tail_max(b):
                dve.wait_ge(ts_ps, b + 1)
                nc.vector.tensor_reduce(negt[:, :], ps[0:TC, 0:2, :].rearrange("p k n -> p (k n)")[:, 0:T], AX_X,
                                        ALU.max, negate=True).then_inc(tmax_sb, 1)

            def tail_combine(b):
                dve.wait_ge(tcopy_sb, b + 1)
                nc.vector.reciprocal(rt[:, 0:1], lt[0:H, :]).then_inc(tstep, 1)
                nc.vector.reciprocal(rt[:, 1:2], lt2[:, :]).then_inc(tstep, 1)
                dve.wait_ge(tstep, b * 4 + 2)
                nc.vector.tensor_tensor(ct[:, :], rt[:, 1:2], neg_lam_col[:, :], ALU.mult).then_inc(tstep, 1)
                dve.wait_ge(tstep, b * 4 + 3)
                nc.vector.tensor_scalar(pt2[:, :], pt2[:, :], ct[:, 0:1], None, ALU.mult).then_inc(tstep, 1)
                dve.wait_ge(tstep, b * 4 + 4)
                nc.vector.scalar_tensor_tensor(out=pt2[:, :], in0=pt[0:H, :], scalar=rt[:, 0:1], in1=pt2[:, :],
                                               op0=ALU.mult, op1=ALU.add).then_inc(tatt_sb, 1)

            def coefs(b, n):
                dve.wait_ge(exp_sb, b * SLOTS + NQ * (n + 1))
                nc.vector.reciprocal(rc[:, n % 2, :, :], lsum[:, n % 2, :, :]).then_inc(coef_sb, 1)
                dve.wait_ge(coef_sb, b * (2 * H) + (2 * n + 1))
                nc.vector.scalar_tensor_tensor(out=coef[:, n % 2, :], in0=lsum[:, n % 2, 0, :],
                                               scalar=neg_lam[:, n:n + 1], in1=rc[:, n % 2, 1, :], op0=ALU.mult,
                                               op1=ALU.mult).then_inc(coef_sb, 1)
                dve.wait_ge(coef_sb, b * (2 * H) + (2 * n + 2))

            def take_y(b, n):
                dve.wait_ge(pv_ps, b * SLOTS + NQ * (n + 1))
                nc.vector.tensor_tensor(yraw[:, NQ * (n % HG):NQ * (n % HG + 1), :],
                                        ps[:, YB, 0:NQ * VD].rearrange("p (i d) -> p i d", d=VD),
                                        rc[:, n % 2, 0, :].unsqueeze(2).to_broadcast([P, NQ, VD]), ALU.mult
                                        ).then_inc(y_sb, 1)

            def centre(b, k):
                m = 1 if k == 0 else P
                c = b * (3 * NN) + 3 * k
                if k:
                    dve.wait_ge(y_sb, b * H + HG * k)
                else:
                    dve.wait_ge(ty_sb, b + 1)
                src = yraw if k else ytail
                nc.vector.tensor_reduce(ysum[0:m, 0, :], src[0:m, :, :], AX_X, ALU.add).then_inc(nstep, 1)
                dve.wait_ge(nstep, c + 1)
                nc.vector.tensor_scalar(ysum[0:m, 0, :], ysum[0:m, 0, :], 1.0 / VD, None, ALU.mult).then_inc(nstep, 1)
                dve.wait_ge(nstep, c + 2)
                nc.vector.tensor_tensor(y[0:m, :, :], src[0:m, :, :],
                                        ysum[0:m, 0, :].unsqueeze(2).to_broadcast([m, HG * NQ, VD]), ALU.subtract
                                        ).then_inc(yc_sb, 1)

            def spread(b, k):
                m = 1 if k == 0 else P
                c = b * (3 * NN) + 3 * k
                dve.wait_ge(ysq_sb, b * NN + (k + 1))
                nc.vector.tensor_reduce(ysum[0:m, 1, :], ysq[0:m, :, :], AX_X, ALU.add).then_inc(nstep, 1)
                dve.wait_ge(nstep, c + 3)
                nc.vector.tensor_scalar(ysum[0:m, 1, :], ysum[0:m, 1, :], 1.0 / VD, LN_EPS, ALU.mult, ALU.add
                                        ).then_inc(yvar_sb, 1)

            def scale_y(b, k):
                m = 1 if k == 0 else P
                dve.wait_ge(yrs_sb, b * NN + (k + 1))
                nc.vector.tensor_scalar(yrs[0:m, :], yrs[0:m, :], 1.0 - LAMBDA_INIT, None, ALU.mult
                                        ).then_inc(yrs_scaled, 1)
                dve.wait_ge(yrs_scaled, b * NN + (k + 1))
                if k == 0:
                    wait(dve, yt_ps, b * NR)
                    nc.vector.tensor_tensor(yn[0:1, NQ, :].rearrange("p (h d) -> p h d", d=VD), y[0:1, :, :],
                                            yrs[0:1, :].unsqueeze(2).to_broadcast([1, HG * NQ, VD]), ALU.mult
                                            ).then_inc(yn_sb, 1)
                    return
                for j in range(HG):
                    hd = HG * (k - 1) + j
                    last = nc.vector.tensor_tensor(
                        yn[:, 0:NQ, VD * hd:VD * (hd + 1)], y[:, NQ * j:NQ * (j + 1), :],
                        yrs[:, NQ * j:NQ * (j + 1)].unsqueeze(2).to_broadcast([P, NQ, VD]), ALU.mult)
                last.then_inc(yn_sb, 1)

            def batch(b, first, last):
                at = schedule(first, last)
                for s in range(last_slot + 1):
                    c = s - L_TURN - 1
                    if c >= 0 and c < SLOTS and c % 2 == 0:
                        i = c % NQ
                        dve.wait_ge(att_ps, b * SLOTS + (c + 1))
                        wait(dve, pv_ps, b * SLOTS + max(c - NQ + 1, 0))
                        nc.vector.tensor_copy(att_t[:, po[i]:po[i + 1]], ps[:, TP, 0:P * (i + 1)]
                                              ).then_inc(attt_even, 1)
                    if s < SLOTS:
                        n, i = divmod(s, NQ)
                        dve.wait_ge(s_ps, b * SLOTS + (s + 1))
                        nc.vector.tensor_reduce(negm[:, n % 2, i, :], score_view(i), AX_X, ALU.max, negate=True
                                                ).then_inc(max_sb, 1)
                    for kind, i, dt in at[2 * s]:
                        piece(kind, i, b + dt, bank_of(2 * s))
                    c = s - L_ATT
                    if c >= 0 and c < SLOTS:
                        n, i = divmod(c, NQ)
                        if i == 0:
                            coefs(b, n)
                        cut = slice(po[i], po[i + 1])
                        nc.vector.scalar_tensor_tensor(out=pr[:, n % 2, 0, cut], in0=pr[:, n % 2, 1, cut],
                                                       scalar=coef[:, n % 2, i:i + 1], in1=pr[:, n % 2, 0, cut],
                                                       op0=ALU.mult, op1=ALU.add).then_inc(att_sb, 1)
                    if not last:
                        if s == SLOTS:
                            tail_max(b + 1)
                        if s == SLOTS + 2:
                            tail_combine(b + 1)
                    for kind, i, dt in at[2 * s + 1]:
                        piece(kind, i, b + dt, bank_of(2 * s + 1))
                    if s >= L_PV + NQ - 1 and (s - L_PV) % NQ == NQ - 1:
                        take_y(b, (s - L_PV) // NQ)
                    if not last:
                        for i in range(NR):
                            if norm_rows[i] == s:
                                normalise(b + 1, i)
                    if not first:
                        if s == 0:
                            centre(b - 1, NG)
                        if s == 1:
                            spread(b - 1, NG)
                        if s == NORM_Y - 1:
                            scale_y(b - 1, NG)
                    for k in range(NG):
                        if s == centre_slot[k]:
                            centre(b, k)
                        if s == centre_slot[k] + 1:
                            spread(b, k)
                        if s == centre_slot[k] + 3:
                            scale_y(b, k)

            for k, (kind, i, t) in enumerate(prologue):
                if kind == "xh":
                    normalise(t, i)
                piece(kind, i, t, k % 4)
            tail_max(0)
            tail_combine(0)
            batch(0, True, False)
            with dve.Fori(1, B - 1) as b:
                batch(b, False, False)
            batch(B - 1, False, True)
            centre(B - 1, NG)
            spread(B - 1, NG)
            scale_y(B - 1, NG)

        @block.tensor
        def _(pe):
            pe.wait_ge(pool_const, 13)
            pe.wait_ge(wtok_in, 3 * 16)
            pe.wait_ge(dve_const, 6)
            for n, (raw, _) in enumerate(wt_jobs):
                if n >= 8:
                    pe.wait_ge(wt_even if n % 2 == 0 else wt_odd, n // 2 - 3)
                nc.tensor.transpose(ps[:, n % 8, 0:P], raw, ident[:, :]).then_inc(wt_ps, 1)
            pe.wait_ge(wt_even, len(wt_jobs) // 2)
            pe.wait_ge(wt_odd, len(wt_jobs) // 2)
            pe.wait_ge(consts_in, 5 * 16)
            pe.wait_ge(setup, 7)

            def take_waits(dst):
                nc.tensor.matmul(dst[0:32, 0:2], ident[:, 0:32], ident[:, 0:2], start=True, stop=True)

            def piece(kind, i, t, bank):
                dst = ps[:, bank, :]
                if kind == "x":
                    pe.wait_ge(x_in, t * 16 + 16)
                    for q in range(XT):
                        xv = xraw[:, q, :].rearrange("p (d e) -> p d e", e=E)[:, i * P:(i + 1) * P, 0]
                        last = nc.tensor.transpose(dst[:, q * P:(q + 1) * P], xv, ident[:, :])
                    last.then_inc(x_ps, 1)
                elif kind == "gu":
                    c, half = divmod(i, 2)
                    cols = slice(S // 2 * half, S // 2 * (half + 1))
                    pe.wait_ge(x_sb, t * DC + DC)
                    for k, w in enumerate((w0t, w1t)):
                        for d in range(DC):
                            last = nc.tensor.matmul(dst[:, S // 2 * k:S // 2 * (k + 1)], w[:, d, c * P:(c + 1) * P],
                                                    xt_tok[:, d, cols], start=(d == 0), stop=(d == DC - 1))
                    last.then_inc(gu_ps, 1)
                elif kind == "to":
                    m = rn[i]
                    pe.wait_ge(hid_sb, t * GU + GU)
                    for c in range(EC):
                        last = nc.tensor.matmul(dst[0:m, 0:D], hid_tok[:, c, P * i:P * i + m], wot[:, c, :],
                                                start=(c == 0), stop=(c == EC - 1 and i > 0))
                    if i == 0:
                        last = nc.tensor.matmul(dst[0:m, 0:D], first_row[0:1, 0:m], cls_row[0:1, :], start=False,
                                                stop=True)
                    last.then_inc(to_ps, 1)
                elif kind == "xh":
                    m = rn[i]
                    pe.wait_ge(xh_sb, t * NR + (i + 1))
                    if m < P:
                        take_waits(dst)
                    for c in range(DC):
                        last = nc.tensor.transpose(dst[:, c * m:(c + 1) * m], xh[0:m, i % 2, c * P:(c + 1) * P],
                                                   ident[0:m, 0:m])
                    last.then_inc(xht_ps, 1)
                elif kind == "qk":
                    g = i // 2
                    w = (wq, wk)[i % 2]
                    pe.wait_ge(xht_sb, t * NR + NR)
                    for d in range(DC):
                        last = nc.tensor.matmul(dst, w[:, d, g * P:(g + 1) * P], xt[:, d, 0:S],
                                                start=(d == 0), stop=(d == DC - 1))
                    last.then_inc(qk_ps, 1)
                elif kind == "qkt":
                    pe.wait_ge(xht_sb, t * NR + NR)
                    for j in range(2 * NG):
                        w, g = ((wq, wk)[j // NG], j % NG)
                        for d in range(DC):
                            last = nc.tensor.matmul(dst[:, j:j + 1], w[:, d, g * P:(g + 1) * P], xt[:, d, S:T],
                                                    start=(d == 0), stop=(d == DC - 1))
                    last.then_inc(qkt_ps, 1)
                elif kind == "v":
                    m = rn[i]
                    for d in range(DC):
                        last = nc.tensor.matmul(dst[0:m, :], xt[:, d, P * i:P * i + m], wv[:, d, :],
                                                start=(d == 0), stop=(d == DC - 1))
                    last.then_inc(v_ps, 1)
                elif kind == "rp":
                    n, qk = divmod(i, 2)
                    g, j = divmod(n, HG)
                    src = (qs, ks)[qk]
                    pe.wait_ge(lo_sb, t * (2 * NG) + (2 * g + qk + 1))
                    for part in range(2):
                        last = nc.tensor.matmul(dst, sel[:, qk, part, j, :], src[:, part, g, 0:S],
                                                start=(part == 0), stop=(part == 1))
                    last.then_inc(rp_ps, 1)
                elif kind == "tt":
                    pe.wait_ge(tatt_sb, t + 1)
                    take_waits(dst)
                    for j in range(NR):
                        last = nc.tensor.transpose(dst[0:rn[j], H * j:H * (j + 1)], pt2[:, P * j:P * j + rn[j]],
                                                   ident[0:H, 0:H])
                    last.then_inc(tt_ps, 1)
                elif kind == "tv":
                    pe.wait_ge(tt_sb, t + 1)
                    pe.wait_ge(v_sb, t * NR + NR)
                    for j in range(NR):
                        last = nc.tensor.matmul(dst[0:H, :], att_tail[0:rn[j], H * j:H * (j + 1)], v[0:rn[j], j, :],
                                                start=(j == 0), stop=(j == NR - 1))
                    last.then_inc(tv_ps, 1)
                elif kind == "ty":
                    pe.wait_ge(tm_sb, t + 1)
                    take_waits(dst)
                    nc.tensor.matmul(dst[0:1, :], ones[0:H, :], tm[:, :], start=True, stop=True).then_inc(ty_ps, 1)
                elif kind == "yt":
                    m = rn[i]
                    pe.wait_ge(yn_sb, t * NN + NN)
                    if m < P:
                        take_waits(dst)
                    for c in range(H * VD // P):
                        last = nc.tensor.transpose(dst[:, c * m:(c + 1) * m], yn[0:m, i, c * P:(c + 1) * P],
                                                   ident[0:m, 0:m])
                    last.then_inc(yt_ps, 1)
                elif kind == "pc":
                    m = rn[i]
                    pe.wait_ge(yt_sb, t * NR + (i + 1))
                    for c in range(H * VD // P):
                        last = nc.tensor.matmul(dst[0:m, 0:D], yt[:, c, 0:m], wc[:, c, :],
                                                start=(c == 0), stop=(c == H * VD // P - 1))
                    last.then_inc(pc_ps, 1)

            def tail_scores(b):
                wait(pe, exp_sb, b * SLOTS)
                pe.wait_ge(qblk_sb, b + 1)
                pe.wait_ge(lo_sb, b * (2 * NG) + 2 * NG)
                for a, z, bank in ((0, S, 0), (S, T + 1, 1)):
                    for g in range(NG):
                        for k in range(4):
                            last = nc.tensor.matmul(ps[:, bank, 0:z - a], qblk[:, k // 2, TC * g:TC * g + P],
                                                    ks[:, k % 2, g, a:z], start=(g == 0 and k == 0),
                                                    stop=(g == NG - 1 and k == 3))
                last.then_inc(ts_ps, 1)

            before = {}

            def bank_free(b, bank):
                if before.get(bank) is not None:
                    kind, i, dt = before[bank]
                    ready, value = left(kind, V_ORDER.index(i) if kind == "v" else i, b + dt)
                    pe.wait_ge(ready, value)
                    before[bank] = None

            def scores(b, s):
                n, i = divmod(s, NQ)
                nk = P * (i + 1)
                if s >= 2:
                    pe.wait_ge(exp_sb, b * SLOTS + (s - 1))
                else:
                    pe.wait_ge(texp_sb, b + 1)
                if i == 0:
                    pe.wait_ge(rpq_sb, b * H + (n + 1))
                    pe.wait_ge(rpk_sb, b * H + (n + 1))
                bank_free(b, {2: 1, 3: 3}.get(i))
                dst = score_view(i)
                for m in range(2):
                    nc.tensor.matmul(dst[:, m, :], q4[:, n % 2, m, P * i:P * (i + 1)], k4[:, n % 2, 0:nk],
                                     start=True, stop=False)
                    last = nc.tensor.matmul(dst[:, m, P * i:nk], identb[:, :], causal[:, :], start=False, stop=True)
                last.then_inc(s_ps, 1)

            def turn(b, c):
                n, i = divmod(c, NQ)
                pe.wait_ge(att_sb, b * SLOTS + (c + 1))
                wait(pe, attt_even if c % 2 == 0 else attt_odd, b * (SLOTS // 2) + c // 2)
                for j in range(i + 1):
                    last = nc.tensor.transpose(ps[:, TP + c % 2, P * j:P * (j + 1)],
                                               pr[:, n % 2, 0, po[i] + P * j:po[i] + P * (j + 1)], ident[:, :])
                last.then_inc(att_ps, 1)

            def values(b, c):
                n, i = divmod(c, NQ)
                pe.wait_ge(attt_even if c % 2 == 0 else attt_odd, b * (SLOTS // 2) + (c // 2 + 1))
                if c == 0:
                    pe.wait_ge(v_sb, b * NR + NR)
                if i == 0:
                    wait(pe, y_sb, b * H + n)
                for j in range(i + 1):
                    last = nc.tensor.matmul(ps[:, YB, VD * i:VD * (i + 1)], att_t[:, po[i] + P * j:po[i] + P * (j + 1)],
                                            v[:, j, VD * n:VD * (n + 1)], start=(j == 0), stop=(j == i))
                last.then_inc(pv_ps, 1)

            def run(kind, i, b, dt, bank):
                bank_free(b, bank)
                before[bank] = (kind, i, dt)
                piece(kind, i, b + dt, bank)

            def batch(b, first, last):
                at = schedule(first, last)
                for s in range(last_slot + 1):
                    if s < SLOTS:
                        scores(b, s)
                    if s == SLOTS and not last:
                        tail_scores(b + 1)
                    for kind, i, dt in at[2 * s]:
                        run(kind, i, b, dt, bank_of(2 * s))
                    if s >= L_PV:
                        values(b, s - L_PV)
                    if s >= L_TURN and s - L_TURN < SLOTS:
                        turn(b, s - L_TURN)
                    for kind, i, dt in at[2 * s + 1]:
                        run(kind, i, b, dt, bank_of(2 * s + 1))

            for k, (kind, i, t) in enumerate(prologue):
                if k >= 4:
                    k2, i2, t2 = prologue[k - 4]
                    s2, v2 = left(k2, i2, t2)
                    pe.wait_ge(s2, v2)
                if kind == "qkt" and k:
                    pe.wait_ge(wattn_in, (2 * 2 * DC + 2) * 16)
                piece(kind, i, t, k % 4)
            for k2, i2, t2 in prologue[-4:]:
                s2, v2 = left(k2, i2, t2)
                pe.wait_ge(s2, v2)
            tail_scores(0)
            batch(0, True, False)
            kind, i, dt = last_piece
            with pe.Fori(1, B - 1) as b:
                before[BG] = (kind, i, dt - 1)
                batch(b, False, False)
            before[BG] = (kind, i, dt - 1)
            batch(B - 1, False, True)
            for k in range(2 * NR):
                run(("yt", "pc")[k % 2], k // 2, B - 1, 0, BG)

    with ExitStack() as ctx:
        def sb(name, shape, dt=F32):
            return ctx.enter_context(nc.sbuf_tensor(name, shape, dt))

        def sem(name):
            return ctx.enter_context(nc.semaphore(name))

        ps = ctx.enter_context(nc.psum_tensor("ps2", [P, 8, 512], F32))

        ident = sb("ident2", [P, P])
        half = sb("half", [P, NT])
        zeros = sb("zeros", [P, DC * I + D])
        lower = sb("lower", [P, G, G])
        bias = sb("bias", [P, NX])
        rw_raw = sb("rw_raw", [P, D])
        rw_t = sb("rw_t", [P, DC, NX])
        acc = sb("acc", [P, NT, D])
        oacc = sb("oacc", [P, NT, D])
        st6 = sb("st62", [P, NT, 6])
        mv = sb("mv2", [P, NT, 2])
        rs = sb("rs2", [P, NT])
        x2 = sb("x2", [P, 2, D])
        x2t = sb("x2t", [P, DC, N])
        score = sb("score", [P, NT, NX])
        sfc = sb("sfc", [P, NT, NX])
        eq = sb("eq", [P, NT, NX])
        rest = sb("rest", [P, NT, NX])
        g1 = sb("g1", [P, NT, G])
        g2 = sb("g2", [P, NT, G])
        gc = sb("gc", [P, NT, G])
        top8 = sb("top8", [P, NT, 8])
        wsum = sb("wsum", [P, NT])
        comb = sb("comb", [P, NX, NT])
        cur = sb("cur", [P, 2, NT])
        WC = DC * I + D
        UPW = slice(0, DC * I)
        DNW = slice(DC * I, WC)
        wr = sb("wr", [P, NS + 2, WC])
        wh = sb("wh", [P, NS + 2, WC], F32R)
        wl = sb("wl", [P, NS + 2, WC], F32R)
        x2h = sb("x2h", [P, DC, N], F32R)
        x2l = sb("x2l", [P, DC, N], F32R)
        r = sb("r", [P, 2, u0[NU] - u0[NU - 1]])
        hid = sb("hid", [P, 2, N])
        hid_h = sb("hid_h", [P, 2, P * NT], F32R)
        hid_l = sb("hid_l", [P, 2, P * NT], F32R)

        w_in = sem("w_in")
        h2_in = [sem(f"h2_in{k}") for k in range(5)]
        shared_in = sem("shared_in")
        up_in = [sem(f"up_in{k}") for k in range(2)]
        down_in = [sem(f"down_in{k}") for k in range(2)]
        uph_sb = sem("uph_sb")
        upl_sb = sem("upl_sb")
        downh_sb = sem("downh_sb")
        downl_sb = sem("downl_sb")
        x2h_sb = sem("x2h_sb")
        x2l_sb = sem("x2l_sb")
        sq_sb = sem("sq_sb")
        hidh_sb = sem("hidh_sb")
        hidl_sb = sem("hidl_sb")
        pad_sb = sem("pad_sb")
        pool_c2 = sem("pool_c2")
        clear_sb = sem("clear_sb")
        sum_sb = sem("sum_sb")
        st_sb = sem("st_sb2")
        mv_sb = sem("mv_sb2")
        veps_sb = sem("veps_sb2")
        rs_sb = sem("rs_sb2")
        x2_sb = sem("x2_sb")
        x2_ps = sem("x2_ps")
        rw_ps = sem("rw_ps")
        rw_sb = sem("rw_sb")
        logit_ps = sem("logit_ps")
        sig_sb = sem("sig_sb")
        route = sem("route")
        cur_sb = sem("cur_sb")
        up_ps = sem("up_ps")
        relu_sb = sem("relu_sb")
        down_ps = sem("down_ps")
        acc_sb = sem("acc_sb")
        out_done = sem("out_done")

        UP = 0
        DN = 5
        LG = 5
        full = N // P
        chunks = [(a, min(a + 4, full)) for a in range(0, full, 4)]
        piece_of = [min(t // 4, 4) for t in range(NT)]

        block = ctx.enter_context(nc.Block())

        @block.sync
        def _(sp):
            sp.dma_start(rw_raw[0:NX, :], router_w).then_inc(w_in, 16)
            sp.dma_start(bias[:, :], correction_bias.partition_broadcast(P)).then_inc(w_in, 16)
            sp.wait_ge(clear_sb, 1)
            for k, (a, z) in enumerate(chunks):
                for src, dst in ((h_dram, acc), (o_dram, oacc)):
                    sp.dma_start(dst[:, a:z, :], src[P * a:P * z, :].rearrange("(t p) d -> p t d", p=P)
                                 ).then_inc(h2_in[k], 16)
            if full < NT:
                for src, dst in ((h_dram, acc), (o_dram, oacc)):
                    sp.dma_start(dst[0:tn[full], full, :], src[P * full:N, :]).then_inc(h2_in[4], 16)
            for c in range(DC):
                sp.dma_start(wr[:, 0:NS, I * c:I * (c + 1)],
                             shared_up_w[P * c:P * (c + 1), :].rearrange("p (n i) -> p n i", i=I)
                             ).then_inc(shared_in, 16)
            sp.dma_start(wr[:, 0:NS, DC * I:WC], shared_down_w.rearrange("(n p) d -> p n d", p=P)
                         ).then_inc(shared_in, 16)

            def load_up(e, k):
                sp.dma_start(wr[:, NS + k, UPW].rearrange("p (c i) -> p c i", c=DC),
                             up_w[bass.ds(e, 1)].rearrange("a (c p) i -> p (a c) i", p=P)
                             ).then_inc(up_in[k], 16)

            def load_down(e, k):
                sp.dma_start(wr[:, NS + k, DNW], down_w[bass.ds(e, 1)].rearrange("a i d -> i (a d)")
                             ).then_inc(down_in[k], 16)

            for k in range(2):
                load_up(k, k)
                load_down(k, k)
            with sp.Fori(0, NX // 2 - 1) as j:
                e = j * 2
                for k in range(2):
                    sp.wait_ge(upl_sb, e + (NS + k + 1))
                    load_up(e + (2 + k), k)
                    sp.wait_ge(downl_sb, e + (NS + k + 1))
                    load_down(e + (2 + k), k)
            for k, (a, z) in enumerate(chunks):
                sp.wait_ge(acc_sb, NE * NP)
                sp.dma_start(out_rows[P * a:P * z, :].rearrange("(t p) d -> p t d", p=P), acc[:, a:z, :]
                             ).then_inc(out_done, 16)
            if full < NT:
                sp.dma_start(out_rows[P * full:N, :], acc[0:tn[full], full, :]).then_inc(out_done, 16)
            sp.wait_ge(out_done, 16 * (len(chunks) + (full < NT)))

        @block.gpsimd
        def _(pool):
            nc.gpsimd.memset(ident[:, :], 0.0).then_inc(pool_c2, 1)
            nc.gpsimd.memset(half[:, :], -0.5).then_inc(pool_c2, 1)
            nc.gpsimd.memset(lower[:, :, :], 0.0).then_inc(pool_c2, 1)
            nc.gpsimd.memset(zeros[:, :], 0.0).then_inc(pool_c2, 1)
            pool.wait_ge(pool_c2, 4)
            nc.gpsimd.affine_select(out=ident[:, :], in_=ident[:, :], compare_op=ALU.not_equal, fill=1.0,
                                    base=0, pattern=[[-1, P]], channel_multiplier=1).then_inc(pool_c2, 1)
            nc.gpsimd.affine_select(out=lower[:, :, :], in_=lower[:, :, :], compare_op=ALU.is_ge, fill=1.0,
                                    base=0, pattern=[[-1, G], [1, G]], channel_multiplier=0).then_inc(pool_c2, 1)
            for k in range(5):
                ts = [t for t in range(NT) if piece_of[t] == k]
                if not ts:
                    continue
                a, z = ts[0], ts[-1] + 1
                pool.wait_ge(mv_sb, z)
                nc.gpsimd.tensor_scalar(rs[:, a:z], mv[:, a:z, 1], LN_EPS, None, ALU.add).then_inc(veps_sb, 1)
                pool.wait_ge(veps_sb, k + 1)
                nc.gpsimd.tensor_tensor(rs[:, a:z], rs[:, a:z], half[:, a:z], ALU.pow).then_inc(rs_sb, 1)

            def split_up(n, slot):
                nc.gpsimd.tensor_tensor(wh[:, slot, UPW], wr[:, slot, UPW], zeros[:, UPW], ALU.add
                                        ).then_inc(uph_sb, 1)
                pool.wait_ge(uph_sb, n + 1)
                nc.gpsimd.tensor_tensor(wl[:, slot, UPW], wr[:, slot, UPW], wh[:, slot, UPW].bitcast(F32),
                                        ALU.subtract).then_inc(upl_sb, 1)

            def split_down(n, slot):
                nc.gpsimd.tensor_tensor(wh[:, slot, DNW], wr[:, slot, DNW], zeros[:, 0:D], ALU.add
                                        ).then_inc(downh_sb, 1)
                pool.wait_ge(downh_sb, n + 1)
                nc.gpsimd.tensor_tensor(wl[:, slot, DNW], wr[:, slot, DNW], wh[:, slot, DNW].bitcast(F32),
                                        ALU.subtract).then_inc(downl_sb, 1)

            pool.wait_ge(shared_in, (DC + 1) * 16)
            split_up(0, 0)
            for t in range(NT):
                cols = slice(P * t, P * t + tn[t])
                pool.wait_ge(x2h_sb, t + 1)
                nc.gpsimd.tensor_tensor(x2l[:, :, cols], x2t[:, :, cols], x2h[:, :, cols].bitcast(F32), ALU.subtract
                                        ).then_inc(x2l_sb, 1)
            for n in range(1, NS):
                split_up(n, n)
                split_down(n - 1, n - 1)
            split_down(NS - 1, NS - 1)
            for k in range(2):
                pool.wait_ge(up_in[k], 16)
                split_up(NS + k, NS + k)
                pool.wait_ge(down_in[k], 16)
                split_down(NS + k, NS + k)
            with pool.Fori(0, NX // 2 - 1) as j:
                e = j * 2 + 2
                for k in range(2):
                    pool.wait_ge(up_in[k], e * 8 + 16)
                    pool.wait_ge(up_ps, (e + (NS - 1 + k)) * NU)
                    split_up(e + (NS + k), NS + k)
                    pool.wait_ge(down_in[k], e * 8 + 16)
                    pool.wait_ge(down_ps, (e + (NS - 1 + k)) * NP)
                    split_down(e + (NS + k), NS + k)

        @block.scalar
        def _(act):
            act.wait_ge(rw_ps, 1)
            nc.scalar.copy(rw_t[:, :, :], ps[:, 7, 0:DC * NX].rearrange("p (c n) -> p c n", c=DC)).then_inc(rw_sb, 1)
            for t in range(NT):
                n = tn[t]
                act.wait_ge(x2_ps, t + 1)
                nc.scalar.copy(x2t[:, :, P * t:P * t + n],
                               ps[:, UP + t % 2, 0:DC * n].rearrange("p (c n) -> p c n", c=DC))
                nc.scalar.copy(x2h[:, :, P * t:P * t + n],
                               ps[:, UP + t % 2, 0:DC * n].rearrange("p (c n) -> p c n", c=DC)).then_inc(x2h_sb, 1)
            for t in range(NT):
                act.wait_ge(logit_ps, t + 1)
                act.wait_ge(clear_sb, 2)
                nc.scalar.activation(score[0:tn[t], t, :], ps[0:tn[t], LG + t % 2, 0:NX], ACT.Exp, scale=-1.0
                                     ).then_inc(sig_sb, 1)

            def expert(n, k):
                def square(u):
                    act.wait_ge(relu_sb, n * NU + (u + 1))
                    nc.scalar.activation(hid[:, k, u0[u]:u0[u + 1]], r[:, u % 2, 0:u0[u + 1] - u0[u]], ACT.Square
                                         ).then_inc(sq_sb, 1)

                def high(u):
                    act.wait_ge(sq_sb, n * NU + (u + 1))
                    nc.scalar.copy(hid_h[:, k, u0[u]:u0[u + 1]], hid[:, k, u0[u]:u0[u + 1]]).then_inc(hidh_sb, 1)

                for u in range(NU):
                    act.wait_ge(up_ps, n * NU + (u + 1))
                    wait(act, sq_sb, n * NU + max(u - 1, 0))
                    nc.scalar.activation(r[:, u % 2, 0:u0[u + 1] - u0[u]], ps[:, UP + u, 0:u0[u + 1] - u0[u]], ACT.Relu
                                         ).then_inc(relu_sb, 1)
                    if u >= 1:
                        square(u - 1)
                    if u >= 2:
                        high(u - 2)
                square(NU - 1)
                high(NU - 2)
                high(NU - 1)

            def free_hid(n):
                act.wait_ge(hidl_sb, n * NU)
                act.wait_ge(down_ps, n * NP)

            act.wait_ge(pad_sb, 2)
            for n in range(NS):
                if n >= 2:
                    free_hid(n - 1)
                expert(n, n % 2)
            with act.Fori(0, NX // 2) as j:
                n = j * 2 + NS
                for k in range(2):
                    free_hid(n + (k - 1))
                    expert(n + k, k)

        @block.vector
        def _(dve):
            nc.vector.memset(mv[:, :, :], 1.0)
            nc.vector.memset(acc[:, full:NT, :], 0.0).then_inc(clear_sb, 1)
            nc.vector.memset(score[:, :, :], 0.0).then_inc(clear_sb, 1)
            for part in (hid_h, hid_l):
                nc.vector.memset(part[:, :, N:P * NT].bitcast(F32), 0.0).then_inc(pad_sb, 1)
            for k in range(5):
                ts = [t for t in range(NT) if piece_of[t] == k]
                if not ts:
                    continue
                dve.wait_ge(h2_in[k], 2 * 16)
                for t in ts:
                    nc.vector.tensor_tensor(acc[0:tn[t], t, :], acc[0:tn[t], t, :], oacc[0:tn[t], t, :], ALU.add
                                            ).then_inc(sum_sb, 1)
                for t in ts:
                    dve.wait_ge(sum_sb, t + 1)
                    nc.vector.bn_stats(st6[0:tn[t], t, :], acc[0:tn[t], t, :]).then_inc(st_sb, 1)
                for t in ts:
                    dve.wait_ge(st_sb, t + 1)
                    nc.vector.bn_aggr(mv[0:tn[t], t, :], st6[0:tn[t], t, :]).then_inc(mv_sb, 1)
                dve.wait_ge(mv_sb, ts[-1] + 1)
                dve.wait_ge(rs_sb, k + 1)
                for t in ts:
                    if t >= 2:
                        dve.wait_ge(x2_ps, t - 1)
                    n = tn[t]
                    nc.vector.tensor_scalar(x2[0:n, t % 2, :], acc[0:n, t, :], mv[0:n, t, 0:1], rs[0:n, t:t + 1],
                                            ALU.subtract, ALU.mult).then_inc(x2_sb, 1)

            step = [0]

            def link(ins):
                step[0] += 1
                ins.then_inc(route, 1)
                dve.wait_ge(route, step[0])

            def over(ap, n):
                return ap.unsqueeze(3).to_broadcast([P, NT, G, n])

            grp = sfc[:, :, :].rearrange("p t (g k) -> p t g k", g=G)
            eqg = eq[:, :, :].rearrange("p t (g k) -> p t g k", g=G)
            resg = rest[:, :, :].rearrange("p t (g k) -> p t g k", g=G)

            def group_scores():
                dve.wait_ge(sig_sb, NT)
                dve.wait_ge(w_in, 2 * 16)
                dve.wait_ge(pool_c2, 6)
                link(nc.vector.tensor_scalar(score[:, :, :], score[:, :, :], 1.0, None, ALU.add))
                link(nc.vector.reciprocal(score[:, :, :], score[:, :, :]))
                link(nc.vector.tensor_tensor(sfc[:, :, :], score[:, :, :],
                                             bias[:, :].unsqueeze(1).to_broadcast([P, NT, NX]), ALU.add))
                link(nc.vector.tensor_reduce(g1[:, :, :], grp, AX_X, ALU.max))
                link(nc.vector.tensor_tensor(eqg, grp, over(g1[:, :, :], GE), ALU.is_equal))
                link(nc.vector.tensor_reduce(gc[:, :, :], eqg, AX_X, ALU.add))
                link(nc.vector.scalar_tensor_tensor(out=rest[:, :, :].rearrange("p t e -> p (t e)"),
                                                    in0=eq[:, :, :].rearrange("p t e -> p (t e)"), scalar=MASKED,
                                                    in1=sfc[:, :, :].rearrange("p t e -> p (t e)"),
                                                    op0=ALU.mult, op1=ALU.add))
                link(nc.vector.tensor_reduce(g2[:, :, :], resg, AX_X, ALU.max))
                link(nc.vector.tensor_scalar(gc[:, :, :], gc[:, :, :], 1.5, MASKED, ALU.is_lt, ALU.mult))
                link(nc.vector.tensor_tensor(gc[:, :, :], gc[:, :, :], g1[:, :, :], ALU.add))
                link(nc.vector.tensor_tensor(g2[:, :, :], g2[:, :, :], gc[:, :, :], ALU.max))
                link(nc.vector.tensor_tensor(g1[:, :, :], g1[:, :, :], g2[:, :, :], ALU.add))
            def pick_groups():
                ga = over(g1[:, :, :], G)
                gb = g1[:, :, :].unsqueeze(2).to_broadcast([P, NT, G, G])
                link(nc.vector.tensor_tensor(eqg, gb, ga, ALU.is_equal))
                link(nc.vector.tensor_tensor(eqg, eqg, lower[:, :, :].unsqueeze(1).to_broadcast([P, NT, G, G]), ALU.mult))
                link(nc.vector.tensor_tensor(resg, gb, ga, ALU.is_gt))
                link(nc.vector.tensor_tensor(eq[:, :, :], eq[:, :, :], rest[:, :, :], ALU.add))
                link(nc.vector.tensor_reduce(gc[:, :, :], eqg, AX_X, ALU.add))
                link(nc.vector.tensor_scalar(gc[:, :, :], gc[:, :, :], TOPG - 0.5, None, ALU.is_lt))
                link(nc.vector.tensor_tensor(grp, grp, over(gc[:, :, :], GE), ALU.mult))
                link(nc.vector.tensor_scalar(sfc[:, :, :], sfc[:, :, :], 0.0, None, ALU.add))

            def pick_experts():
                for t in range(NT):
                    top = nc.vector.max(top8[:, t, :], sfc[:, t, :])
                link(top)
                for t in range(NT):
                    rep = nc.vector.match_replace(rest[:, t, :], top8[:, t, :], sfc[:, t, :], MASKED)
                link(rep)
                link(nc.vector.tensor_tensor(eq[:, :, :], rest[:, :, :], sfc[:, :, :], ALU.not_equal))
                link(nc.vector.tensor_tensor(eq[:, :, :], eq[:, :, :], score[:, :, :], ALU.mult))
                link(nc.vector.tensor_reduce(wsum[:, :], eq[:, :, :], AX_X, ALU.add))
                link(nc.vector.tensor_scalar(wsum[:, :], wsum[:, :], 1e-20, None, ALU.add))
                link(nc.vector.reciprocal(wsum[:, :], wsum[:, :]))
                link(nc.vector.tensor_tensor(rest[:, :, :], eq[:, :, :],
                                             wsum[:, :].unsqueeze(2).to_broadcast([P, NT, NX]), ALU.mult))
                link(nc.vector.tensor_scalar(comb[:, :, :].rearrange("p e t -> p t e"), rest[:, :, :], ROUTE_SCALE,
                                             None, ALU.mult))

            def low(n, k):
                for u in range(NU):
                    cols = slice(u0[u], u0[u + 1])
                    dve.wait_ge(hidh_sb, n * NU + (u + 1))
                    nc.vector.tensor_tensor(hid_l[:, k, cols], hid[:, k, cols], hid_h[:, k, cols].bitcast(F32),
                                            ALU.subtract).then_inc(hidl_sb, 1)

            def add(n, k):
                for q in range(NP):
                    dve.wait_ge(down_ps, n * NP + (q + 1))
                    for t in range(2 * q, min(2 * q + 2, NT)):
                        m = tn[t]
                        w = 1.0 if k is None else cur[0:m, k, t:t + 1]
                        last = nc.vector.scalar_tensor_tensor(
                            out=acc[0:m, t, :], in0=ps[0:m, DN + q % 3, D * (t % 2):D * (t % 2 + 1)], scalar=w,
                            in1=acc[0:m, t, :], op0=ALU.mult, op1=ALU.add)
                    last.then_inc(acc_sb, 1)

            low(0, 0)
            group_scores()
            add(0, None)
            low(1, 1)
            pick_groups()
            for n in range(1, NS):
                dve.wait_ge(acc_sb, n * NP)
                add(n, None)
                low(n + 1, (n + 1) % 2)
                if n == 1:
                    pick_experts()
            with dve.Fori(0, NX // 2 - 1) as j:
                e = j * 2
                for k in range(2):
                    nc.vector.tensor_copy(cur[:, k, :], comb[:, bass.ds(e + k, 1), :].rearrange("p a t -> p (a t)")
                                          ).then_inc(cur_sb, 1)
                    dve.wait_ge(cur_sb, e + (k + 1))
                    dve.wait_ge(acc_sb, (e + (NS + k)) * NP)
                    add(e + (NS + k), k)
                    low(e + (NS + k + 1), (NS + k + 1) % 2)
            for k in range(2):
                n = NE - 2 + k
                nc.vector.tensor_copy(cur[:, k, :], comb[:, NX - 2 + k, :]).then_inc(cur_sb, 1)
                dve.wait_ge(cur_sb, NX - 2 + (k + 1))
                dve.wait_ge(acc_sb, n * NP)
                add(n, k)
                if k == 0:
                    low(n + 1, (n + 1) % 2)

        @block.tensor
        def _(pe):
            pe.wait_ge(pool_c2, 5)
            pe.wait_ge(w_in, 2 * 16)
            for c in range(DC):
                last = nc.tensor.transpose(ps[:, 7, c * NX:(c + 1) * NX], rw_raw[0:NX, c * P:(c + 1) * P],
                                           ident[0:NX, 0:NX])
            last.then_inc(rw_ps, 1)
            for t in range(NT):
                n = tn[t]
                pe.wait_ge(x2_sb, t + 1)
                if t >= 2:
                    pe.wait_ge(x2h_sb, t - 1)
                for c in range(DC):
                    last = nc.tensor.transpose(ps[:, UP + t % 2, c * n:(c + 1) * n], x2[0:n, t % 2, c * P:(c + 1) * P],
                                               ident[0:n, 0:n])
                last.then_inc(x2_ps, 1)
            pe.wait_ge(rw_sb, 1)
            pe.wait_ge(x2h_sb, NT)
            for t in range(NT):
                n = tn[t]
                if t >= 2:
                    pe.wait_ge(sig_sb, t - 1)
                for c in range(DC):
                    last = nc.tensor.matmul(ps[0:n, LG + t % 2, 0:NX], x2t[:, c, P * t:P * t + n], rw_t[:, c, :],
                                            start=(c == 0), stop=(c == DC - 1))
                last.then_inc(logit_ps, 1)
            pe.wait_ge(sig_sb, NT)

            def products(dst, pairs):
                for k, (w, x) in enumerate(pairs):
                    last = nc.tensor.matmul(dst, w, x, start=(k == 0), stop=(k == len(pairs) - 1))
                return last

            def up(n, slot):
                pe.wait_ge(upl_sb, n + 1)
                for u in range(NU):
                    cols = slice(u0[u], u0[u + 1])
                    if isinstance(n, int) and n == 0:
                        pe.wait_ge(x2l_sb, upto_x[u])
                    else:
                        pe.wait_ge(relu_sb, (n - 1) * NU + (u + 1))
                    pairs = []
                    for c in range(DC):
                        w = slice(I * c, I * (c + 1))
                        pairs += [(wh[:, slot, w], x2h[:, c, cols]), (wh[:, slot, w], x2l[:, c, cols]),
                                  (wl[:, slot, w], x2h[:, c, cols])]
                    products(ps[:, UP + u, 0:u0[u + 1] - u0[u]], pairs).then_inc(up_ps, 1)

            def down(n, k, slot):
                w = DNW
                pe.wait_ge(downl_sb, n + 1)
                for q in range(NP):
                    if isinstance(n, int) and n == 0:
                        if q >= 3:
                            pe.wait_ge(acc_sb, q - 2)
                    else:
                        pe.wait_ge(acc_sb, (n - 1) * NP + (NP + q - 2))
                    for t in range(2 * q, min(2 * q + 2, NT)):
                        rows = slice(P * t, P * (t + 1))
                        pe.wait_ge(hidl_sb, n * NU + (upto[t] + 1))
                        last = products(ps[:, DN + q % 3, D * (t % 2):D * (t % 2 + 1)],
                                        [(hid_h[:, k, rows], wh[:, slot, w]), (hid_h[:, k, rows], wl[:, slot, w]),
                                         (hid_l[:, k, rows], wh[:, slot, w])])
                    last.then_inc(down_ps, 1)

            upto_x = [-(-u0[u + 1] // P) for u in range(NU)]
            pe.wait_ge(pad_sb, 2)
            up(0, 0)
            for n in range(NS - 1):
                up(n + 1, n + 1)
                down(n, n % 2, n)
            up(NS, NS)
            down(NS - 1, (NS - 1) % 2, NS - 1)
            with pe.Fori(0, NX // 2 - 1) as j:
                n = j * 2 + NS
                up(n + 1, NS + 1)
                down(n, 0, NS)
                up(n + 2, NS)
                down(n + 1, 1, NS + 1)
            up(NE - 1, NS + 1)
            down(NE - 2, 0, NS)
            down(NE - 1, 1, NS + 1)


_INS = ['x', 'cls_tok', 'L0_tok_W0', 'L0_tok_W1', 'L0_tok_Wo', 'L0_attn_Wq1', 'L0_attn_Wq2', 'L0_attn_Wk1',
        'L0_attn_Wk2', 'L0_attn_Wv', 'L0_attn_Wc', 'L0_attn_lq1', 'L0_attn_lk1', 'L0_attn_lq2', 'L0_attn_lk2',
        'L0_ffn_router_w', 'L0_ffn_correction_bias', 'L0_ffn_up_w', 'L0_ffn_down_w', 'L0_ffn_shared_up_w',
        'L0_ffn_shared_down_w']
_OUTS = [((4, 513, 256), 'float32')]


def kernel(**inputs):
    import numpy as _np
    import concourse.bacc as _bacc
    from concourse import mybir as _mybir
    from concourse.bass_utils import run_bass_kernel_spmd as _run

    nc = _bacc.Bacc("TRN2", target_bir_lowering=False, num_devices=1)
    arrays, args = {}, []
    for name in _INS:
        a = _np.ascontiguousarray(inputs[name])
        arrays[f"in_{name}_dram"] = a
        args.append(nc.dram_tensor(f"in_{name}_dram", a.shape, _mybir.dt.from_np(a.dtype), kind="ExternalInput").ap())
    for i, (shape, dtype) in enumerate(_OUTS):
        dt = _mybir.dt.from_np(_np.dtype(dtype))
        args.append(nc.dram_tensor(f"out_{i}_dram", shape, dt, kind="ExternalOutput").ap())
    vit_layer(nc, *args)
    r = _run(nc, [arrays], core_ids=[0])
    got = tuple(r.results[0][f"out_{i}_dram"] for i in range(len(_OUTS)))
    return got[0]
```

```python
from contextlib import ExitStack
import math

import concourse.bass as bass
from concourse import mybir

ALU = mybir.AluOpType
ACT = mybir.ActivationFunctionType
F32 = mybir.dt.float32
BF16 = mybir.dt.bfloat16
F32R = mybir.dt.float32r
AX_X = mybir.AxisListType.X

LN_EPS = 1e-05
LAMBDA_INIT = 0.8 - 0.6 * math.exp(-0.3 * (2 - 1))
ROUTE_SCALE = 2.5
MASKED = -1.0e30


def wait(eng, sem, value):
    if not (isinstance(value, int) and value <= 0):
        eng.wait_ge(sem, value)


def vit_layer(nc, x, cls_tok, W0, W1, Wo, Wq1, Wq2, Wk1, Wk2, Wv, Wc, lq1, lk1, lq2, lk2,
              router_w, correction_bias, up_w, down_w, shared_up_w, shared_down_w, out):
    B, S, D, E = x.shape
    P = 128
    T = S + 1
    DC = D // P
    DE = W0.shape[0]
    EC = DE // P
    H = lq1.shape[0]
    HS = lq1.shape[1]
    VD = 2 * HS
    HG = P // (2 * HS)
    NG = H // HG
    XT = S // P
    NQ = S // P
    NR = NQ + 1
    rn = [P] * NQ + [T - S]

    N = B * T
    NT = -(-N // P)
    tn = [min(P, N - P * t) for t in range(NT)]
    NX = up_w.shape[0]
    I = up_w.shape[2]
    NS = shared_up_w.shape[1] // I
    NE = NX + NS
    G = 8
    GE = NX // G
    TOPG = 4
    NU = 5
    u0 = [2 * (N * u // (2 * NU)) for u in range(NU + 1)]
    NP = -(-NT // 2)
    upto = [min(u for u in range(NU) if u0[u + 1] >= min(P * (t + 1), N)) for t in range(NT)]

    h_dram = nc.dram_tensor("h_scratch", [N, D], F32, kind="Internal").ap()
    o_dram = nc.dram_tensor("o_scratch", [N, D], F32, kind="Internal").ap()
    out_rows = out.rearrange("b t d -> (b t) d")

    with ExitStack() as ctx:
        def sb(name, shape, dt=F32):
            return ctx.enter_context(nc.sbuf_tensor(name, shape, dt))

        def sem(name):
            return ctx.enter_context(nc.semaphore(name))

        ps = ctx.enter_context(nc.psum_tensor("ps", [P, 8, 512], F32))

        TC = 3 * HS
        ident = sb("ident", [P, P])
        identb = sb("identb", [P, P], BF16)
        causal = sb("causal", [P, P], BF16)
        sel = sb("sel", [P, 2, 2, HG, P], F32R)
        which = sb("which", [P, HG, 2])
        blk = sb("blk", [P, NG, TC])
        qblk = sb("qblk", [P, 2, NG * TC + P - TC], F32R)
        own_head = sb("own_head", [H, H * VD])
        ones = sb("ones", [P, 1])
        first_row = sb("first_row", [1, P])
        cls_row = sb("cls_row", [1, D])
        neg_half = sb("neg_half", [P, HG * NQ])
        eps = sb("eps", [P, NR])
        unused = sb("unused", [P, 1])
        lam_in = sb("lam_in", [P, 4, H, HS])
        lam_s = sb("lam_s", [P, 2, H])
        neg_lam = sb("neg_lam", [P, H])
        lam_diag = sb("lam_diag", [H, H])
        neg_lam_col = sb("neg_lam_col", [H, 1])
        w0t = sb("w0t", [P, DC, DE])
        w1t = sb("w1t", [P, DC, DE])
        wot = sb("wot", [P, EC, D])
        wq = sb("wq", [P, DC, NG * P])
        wk = sb("wk", [P, DC, NG * P])
        wv = sb("wv", [P, DC, H * VD])
        wc = sb("wc", [P, H * VD // P, D])
        xraw = sb("xraw", [P, XT, D * E])
        xt_tok = sb("xt_tok", [P, DC, S])
        gate = sb("gate", [P, 2, S // 2])
        hid_tok = sb("hid_tok", [P, EC, T])
        h = sb("h", [P, NR, D])
        st6 = sb("st6", [P, NR, 6])
        mv = sb("mv", [P, NR, 2])
        rs = sb("rs", [P, NR])
        xh = sb("xh", [P, 2, D])
        xt = sb("xt", [P, DC, T])
        qs = sb("qs", [P, 2, NG, T + 1], F32R)
        ks = sb("ks", [P, 2, NG, T + 1], F32R)
        q4 = sb("q4", [P, 2, 2, S], F32R)
        k4 = sb("k4", [P, 2, S], F32R)
        v = sb("v", [P, NR, H * VD])
        po = [P * i * (i + 1) // 2 for i in range(NQ + 1)]
        pr = sb("pr", [P, 2, 2, po[NQ]])
        negm = sb("negm", [P, 2, NQ, 2])
        lsum = sb("lsum", [P, 2, 2, NQ])
        rc = sb("rc", [P, 2, 2, NQ])
        coef = sb("coef", [P, 2, NQ])
        att_t = sb("att_t", [P, po[NQ]])
        yraw = sb("yraw", [P, HG * NQ, VD])
        ytail = sb("ytail", [1, H, VD])
        y = sb("y", [P, HG * NQ, VD])
        ysum = sb("ysum", [P, 2, HG * NQ])
        ysq = sb("ysq", [P, HG * NQ, VD])
        yrs = sb("yrs", [P, HG * NQ])
        yn = sb("yn", [P, NR, H * VD])
        yt = sb("yt", [P, 2, H * VD // P, P])
        o = sb("o", [P, NR, D])
        pt = sb("pt", [TC, T])
        pt2 = sb("pt2", [H, T])
        negt = sb("negt", [TC, 1])
        lt = sb("lt", [TC, 1])
        lt2 = sb("lt2", [H, 1])
        rt = sb("rt", [H, 2])
        ct = sb("ct", [H, 1])
        att_tail = sb("att_tail", [P, NR * H])
        tm = sb("tm", [H, H * VD])

        wtok_in = [sem(f"wtok_in{k}") for k in range(3)]
        names = """consts_in wattn_in x_in pool_const dve_const setup lam_exp wt_ps wt_even wt_odd
            x_ps x_sb gu_ps gate_sb hid_sb to_ps h_sb st_sb mv_sb veps_sb rs_sb xh_sb xht_ps xht_sb
            qk_ps hi_sb lo_sb qkt_ps qkt_hi qkt_lo qblk_sb v_ps v_sb rp_ps rpq_sb rpk_sb
            ts_ps tmax_sb texp_sb tcopy_sb tstep tatt_sb tt_ps tt_sb tv_ps tm_sb ty_ps ty_sb
            s_ps max_sb exp_sb coef_sb att_sb att_ps attt_even attt_odd pv_ps y_sb
            nstep yc_sb ysq_sb yvar_sb yrs_sb yrs_scaled yn_sb yt_ps yt_sb pc_ps pc_sb h_out o_out""".split()
        (consts_in, wattn_in, x_in, pool_const, dve_const, setup, lam_exp, wt_ps, wt_even, wt_odd,
         x_ps, x_sb, gu_ps, gate_sb, hid_sb, to_ps, h_sb, st_sb, mv_sb, veps_sb, rs_sb, xh_sb, xht_ps, xht_sb,
         qk_ps, hi_sb, lo_sb, qkt_ps, qkt_hi, qkt_lo, qblk_sb, v_ps, v_sb, rp_ps, rpq_sb, rpk_sb,
         ts_ps, tmax_sb, texp_sb, tcopy_sb, tstep, tatt_sb, tt_ps, tt_sb, tv_ps, tm_sb, ty_ps, ty_sb,
         s_ps, max_sb, exp_sb, coef_sb, att_sb, att_ps, attt_even, attt_odd, pv_ps, y_sb,
         nstep, yc_sb, ysq_sb, yvar_sb, yrs_sb, yrs_scaled, yn_sb, yt_ps, yt_sb, pc_ps, pc_sb, h_out, o_out
         ) = (sem(n) for n in names)

        TP = 4
        YB = 6
        BG = 7
        SLOTS = H * NQ
        GU = 2 * EC
        NN = NG + 1
        L_ATT, L_TURN, L_PV = NQ, NQ + 1, NQ + 3
        last_slot = SLOTS - 1 + L_PV
        TAIL_SLOT = SLOTS + NQ - 1
        PACE = 0.9
        NORM_Y = 3

        flat = pr[:, :, :, :].rearrange("p a b n -> p (a b n)")
        w0_raw = flat[:, 0:EC * D].rearrange("p (c d) -> p c d", c=EC)
        w1_raw = flat[:, EC * D:2 * EC * D].rearrange("p (c d) -> p c d", c=EC)
        wo_raw = flat[:, 2 * EC * D:2 * EC * D + DC * DE].rearrange("p (c d) -> p c d", c=DC)
        wt_jobs = []
        for raw, dst in ((w0_raw, w0t), (w1_raw, w1t)):
            for d in range(DC):
                for e in range(EC):
                    wt_jobs.append((raw[:, e, d * P:(d + 1) * P], dst[:, d, e * P:(e + 1) * P]))
        for e in range(EC):
            for d in range(DC):
                wt_jobs.append((wo_raw[:, d, e * P:(e + 1) * P], wot[:, e, d * P:(d + 1) * P]))

        def token_pieces():
            return ([("x", c) for c in range(DC)] + [("gu", k) for k in range(GU)] + [("to", i) for i in range(NR)]
                    + [("xh", i) for i in range(NR)] + [("qkt", 0)])

        projection_pieces = [("yt", 0)]
        for i in range(NR):
            projection_pieces += ([("yt", i + 1)] if i + 1 < NR else []) + [("pc", i)]

        def schedule(first, last):
            at = [[] for _ in range(2 * (last_slot + 1))]
            for n in range(1, H):
                at[2 * (NQ * n - 3) + 1].append(("rp", 2 * n, 0))
                at[2 * (NQ * n - 2)].append(("rp", 2 * n + 1, 0))
            free = [2 * sl + half for sl in range(TAIL_SLOT) for half in range(2)
                    if (sl % NQ, half) in ((0, 0), (0, 1), (1, 0), (2, 1)) and (sl < SLOTS or half == 1)]
            todo = [("v", i, 0, 4, 0) for i in range(NQ)]
            todo += [(kind, i, -1, {"yt": 1, "pc": 4}[kind], 2 * NORM_Y) for kind, i in projection_pieces]
            todo += [("v", NQ, 0, 4, 0), ("tt", 0, 0, 2, 0), ("tv", 0, 0, 10, 0), ("ty", 0, 0, 2, 0)]
            todo += [(kind, i, 1, {"x": 1, "gu": 4, "to": 4, "xh": 1, "qkt": 15}[kind], 0)
                     for kind, i in token_pieces()]
            todo += [("qk", j, 1, 4, 2 * (NQ * (HG * (j // 2 + 1) - 1) - 1)) for j in range(2 * NG)]
            total = sum(job[3] for job in todo)
            done = 0
            stats_from = 0
            for kind, i, t, share, first_half in todo:
                if kind == "xh":
                    first_half = stats_from + 2 * NQ
                pace = PACE * 2 * TAIL_SLOT * done / total
                k = min(f for f in free if f >= max(first_half, pace))
                free = [f for f in free if f > k]
                done += share
                if kind == "to":
                    stats_from = k
                if not (first and t < 0) and not (last and t > 0):
                    at[k].append((kind, i, t))
            if not last:
                at[2 * SLOTS].append(("rp", 0, 1))
                at[2 * SLOTS + 2].append(("rp", 1, 1))
            return at

        prologue = ([(k, i, 0) for k, i in token_pieces()] + [("qk", j, 0) for j in range(2 * NG)]
                    + [("rp", 0, 0), ("rp", 1, 0)])

        plan = schedule(False, False)
        slot_of = {piece: k // 2 for k, at_k in enumerate(plan) for piece in at_k}
        last_piece = [piece for at_k in plan for piece in at_k][-1]
        centre_slot = [0] + [NQ * HG * k + L_PV for k in range(1, NG)]
        centre_slot[0] = min(c for c in range(slot_of[("ty", 0, 0)] + 1, SLOTS)
                             if all(abs(c - other) >= NQ for other in centre_slot[1:]))
        turn_of = [sum(c < centre_slot[k] for c in centre_slot) for k in range(NG)] + [NG]
        norm_rows = [slot_of[("xh", i, 1)] - 1 for i in range(NR)]

        def bank_of(k):
            return {(0, 1): 1, (1, 1): 3}.get((k // 2 % NQ, k % 2), BG) if k < 2 * SLOTS else BG

        def score_view(i):
            nk, k = P * (i + 1), 2 * (i % 2)
            if 2 * nk <= 512:
                return ps[:, k, :].rearrange("p (m n) -> p m n", m=2)[:, :, 0:nk]
            return ps[:, k:k + 2, 0:nk]

        def left(kind, i, t):
            return {"x": (x_sb, t * DC + (i + 1)), "gu": (hid_sb, t * GU + (i + 1)), "to": (h_sb, t * NR + (i + 1)),
                    "xh": (xht_sb, t * NR + (i + 1)), "qk": (lo_sb, t * (2 * NG) + (i + 1)), "qkt": (qkt_lo, t + 1),
                    "v": (v_sb, t * NR + (i + 1)), "tt": (tt_sb, t + 1), "tv": (tm_sb, t + 1), "ty": (ty_sb, t + 1),
                    "rp": ((rpq_sb, rpk_sb)[i % 2], t * H + (i // 2 + 1)),
                    "yt": (yt_sb, t * NR + (i + 1)), "pc": (pc_sb, t * NR + (i + 1))}[kind]

        block = ctx.enter_context(nc.Block())

        def load_x(sp, b):
            sp.dma_start(xraw[:, :, :], x[b].rearrange("(t p) d e -> p t (d e)", p=P)).then_inc(x_in, 16)

        @block.sync
        def _(sp):
            for k, w in enumerate((lq1, lk1, lq2, lk2)):
                sp.dma_start(lam_in[:, k, :, :], w.partition_broadcast(P)).then_inc(consts_in, 16)
            sp.dma_start(cls_row[0:1, :], cls_tok.rearrange("a b d -> (a b) d")).then_inc(consts_in, 16)
            for w, raw, landed in zip((W0, W1, Wo), (w0_raw, w1_raw, wo_raw), wtok_in):
                sp.dma_start(raw, w.rearrange("(c p) d -> p c d", p=P)).then_inc(landed, 16)
            load_x(sp, 0)
            for w, dst in (((Wq1, Wq2), wq), ((Wk1, Wk2), wk)):
                for m in range(2):
                    for c in range(DC):
                        sp.dma_start(dst[:, c, :].rearrange("p (j m k) -> p j m k", m=2, k=HS)[:, :, m, :],
                                     w[m][c * P:(c + 1) * P, :].rearrange("p (j k) -> p j k", k=HS)
                                     ).then_inc(wattn_in, 16)
            sp.dma_start(wv[:, :, :], Wv.rearrange("(c p) d -> p c d", p=P)).then_inc(wattn_in, 16)
            sp.dma_start(wc[:, :, :], Wc.rearrange("(c p) d -> p c d", p=P)).then_inc(wattn_in, 16)

            def store(b, ready, src, dst, done):
                for i in range(NR):
                    sp.wait_ge(ready, b * NR + (i + 1))
                    sp.dma_start(dst[bass.ds(b * T + P * i, rn[i]), :], src[0:rn[i], i, :]).then_inc(done, 16)

            sp.wait_ge(x_ps, DC)
            load_x(sp, 1)
            store(0, h_sb, h, h_dram, h_out)
            sp.wait_ge(x_ps, 2 * DC)
            load_x(sp, 2)
            store(1, h_sb, h, h_dram, h_out)
            with sp.Fori(1, B - 2) as b:
                sp.wait_ge(x_ps, b * DC + 2 * DC)
                load_x(sp, b + 2)
                store(b - 1, pc_sb, o, o_dram, o_out)
                store(b + 1, h_sb, h, h_dram, h_out)
            store(B - 3, pc_sb, o, o_dram, o_out)
            store(B - 1, h_sb, h, h_dram, h_out)
            store(B - 2, pc_sb, o, o_dram, o_out)
            store(B - 1, pc_sb, o, o_dram, o_out)
            sp.wait_ge(h_out, 16 * NR * B)
            sp.wait_ge(o_out, 16 * NR * B)

        @block.gpsimd
        def _(pool):
            nc.gpsimd.memset(ident[:, :], 0.0).then_inc(pool_const, 1)
            nc.gpsimd.memset(causal[:, :], 0.0).then_inc(pool_const, 1)
            nc.gpsimd.memset(first_row[:, :], 0.0).then_inc(pool_const, 1)
            nc.gpsimd.memset(own_head[:, :], 1.0).then_inc(pool_const, 1)
            nc.gpsimd.memset(neg_half[:, :], -0.5).then_inc(pool_const, 1)
            nc.gpsimd.memset(eps[:, :], LN_EPS).then_inc(pool_const, 1)
            nc.gpsimd.memset(ones[:, :], 1.0).then_inc(pool_const, 1)
            pool.wait_ge(pool_const, 7)
            nc.gpsimd.affine_select(out=ident[:, :], in_=ident[:, :], compare_op=ALU.not_equal, fill=1.0,
                                    base=0, pattern=[[-1, P]], channel_multiplier=1).then_inc(pool_const, 1)
            nc.gpsimd.affine_select(out=causal[:, :], in_=causal[:, :], compare_op=ALU.is_ge, fill=MASKED,
                                    base=0, pattern=[[-1, P]], channel_multiplier=1).then_inc(pool_const, 1)
            nc.gpsimd.affine_select(out=own_head[:, :], in_=own_head[:, :], compare_op=ALU.is_ge, fill=0.0,
                                    base=0, pattern=[[1, H * VD]], channel_multiplier=-VD).then_inc(pool_const, 1)
            pool.wait_ge(pool_const, 10)
            nc.gpsimd.affine_select(out=own_head[:, :], in_=own_head[:, :], compare_op=ALU.is_ge, fill=0.0,
                                    base=VD - 1, pattern=[[-1, H * VD]], channel_multiplier=VD
                                    ).then_inc(pool_const, 1)
            nc.gpsimd.tensor_copy(identb[:, :], ident[:, :]).then_inc(pool_const, 1)
            nc.gpsimd.memset(first_row[0:1, 0:1], 1.0).then_inc(pool_const, 1)

            def norm_scale(t):
                wait(pool, mv_sb, t * NR + NR)
                nc.gpsimd.tensor_tensor(rs[:, :], mv[:, :, 1], eps[:, :], ALU.add).then_inc(veps_sb, 1)
                pool.wait_ge(veps_sb, t + 1)
                nc.gpsimd.tensor_tensor(rs[:, :], rs[:, :], neg_half[:, 0:NR], ALU.pow).then_inc(rs_sb, 1)

            def head_scale(b, k):
                m = 1 if k == 0 else P
                pool.wait_ge(yc_sb, b * NN + (turn_of[k] + 1))
                nc.gpsimd.tensor_tensor(ysq[0:m, :, :], y[0:m, :, :], y[0:m, :, :], ALU.mult).then_inc(ysq_sb, 1)
                pool.wait_ge(yvar_sb, b * NN + (turn_of[k] + 1))
                nc.gpsimd.tensor_tensor(yrs[0:m, :], ysum[0:m, 1, :], neg_half[0:m, :], ALU.pow).then_inc(yrs_sb, 1)

            def batch(b, first, last):
                if not first:
                    head_scale(b - 1, NG)
                todo = [(centre_slot[k], k) for k in range(NG)]
                if not last:
                    todo.append((slot_of[("to", NR - 1, 1)], None))
                for _, k in sorted(todo, key=lambda e: e[0]):
                    if k is None:
                        norm_scale(b + 1)
                    else:
                        head_scale(b, k)

            norm_scale(0)
            batch(0, True, False)
            with pool.Fori(1, B - 1) as b:
                batch(b, False, False)
            batch(B - 1, False, True)
            head_scale(B - 1, NG)

        @block.scalar
        def _(act):
            act.wait_ge(dve_const, 6)
            nc.scalar.activation(lam_s[:, :, :], lam_s[:, :, :], ACT.Exp).then_inc(lam_exp, 1)
            for n, (_, dst) in enumerate(wt_jobs):
                if n % 2 == 0:
                    act.wait_ge(wt_ps, n + 1)
                    nc.scalar.copy(dst, ps[:, n % 8, 0:P]).then_inc(wt_even, 1)

            def piece(kind, i, t, bank):
                src = ps[:, bank, :]
                if kind == "x":
                    act.wait_ge(x_ps, t * DC + (i + 1))
                    wait(act, gu_ps, t * GU)
                    nc.scalar.copy(xt_tok[:, i, :], src).then_inc(x_sb, 1)
                elif kind == "gu":
                    act.wait_ge(gu_ps, t * GU + (i + 1))
                    wait(act, hid_sb, t * GU + max(i - 1, 0))
                    nc.scalar.activation(gate[:, i % 2, :], src[:, 0:S // 2], ACT.Relu).then_inc(gate_sb, 1)
                elif kind == "xh":
                    act.wait_ge(xht_ps, t * NR + (i + 1))
                    wait(act, v_ps, t * NR)
                    nc.scalar.copy(xt[:, :, P * i:P * i + rn[i]],
                                   src[:, 0:DC * rn[i]].rearrange("p (c n) -> p c n", c=DC)).then_inc(xht_sb, 1)
                elif kind == "qk":
                    g = i // 2
                    act.wait_ge(qk_ps, t * (2 * NG) + (i + 1))
                    wait(act, rp_ps, t * (2 * H) - 2 * H + 2 * HG * (g + 1))
                    dst = (qs, ks)[i % 2]
                    nc.scalar.activation(dst[:, 0, g, 0:S], src, ACT.Copy, scale=(HS ** -0.5, 1.0)[i % 2]
                                         ).then_inc(hi_sb, 1)
                elif kind == "qkt":
                    act.wait_ge(qkt_ps, t + 1)
                    wait(act, ts_ps, t)
                    nc.scalar.activation(qs[:, 0, :, S:T].rearrange("p g n -> p (g n)"), src[:, 0:NG], ACT.Copy,
                                         scale=HS ** -0.5)
                    nc.scalar.activation(ks[:, 0, :, S:T].rearrange("p g n -> p (g n)"), src[:, NG:2 * NG], ACT.Copy
                                         ).then_inc(qkt_hi, 1)
                elif kind == "v":
                    m = rn[i]
                    act.wait_ge(v_ps, t * NR + (i + 1))
                    wait(act, pv_ps, t * SLOTS)
                    wait(act, tv_ps, t)
                    nc.scalar.copy(v[0:m, i, :], src[0:m, :]).then_inc(v_sb, 1)
                elif kind == "rp" and i % 2 == 0:
                    n = i // 2
                    act.wait_ge(rp_ps, t * (2 * H) + (i + 1))
                    wait(act, s_ps, t * SLOTS + NQ * (n - 1))
                    for m in range(2):
                        rows = slice(4 * HS * m, 4 * HS * (m + 1))
                        q = nc.scalar.copy(q4[rows, n % 2, m, :], src[rows, :])
                    q.then_inc(rpq_sb, 1)
                elif kind == "yt":
                    act.wait_ge(yt_ps, t * NR + (i + 1))
                    nc.scalar.copy(yt[:, i % 2, :, 0:rn[i]],
                                   src[:, 0:H * VD // P * rn[i]].rearrange("p (c n) -> p c n", n=rn[i])
                                   ).then_inc(yt_sb, 1)
                elif kind == "pc":
                    act.wait_ge(pc_ps, t * NR + (i + 1))
                    nc.scalar.copy(o[0:rn[i], i, :], src[0:rn[i], 0:D]).then_inc(pc_sb, 1)

            def tail_exp(b):
                act.wait_ge(tmax_sb, b + 1)
                wait(act, tatt_sb, b)
                nc.scalar.activation(pt[:, :], ps[0:TC, 0:2, :].rearrange("p k n -> p (k n)")[:, 0:T], ACT.Exp,
                                     bias=negt[:, 0:1], accum_out=lt[:, 0:1]).then_inc(texp_sb, 1)
                act.wait_ge(texp_sb, b + 1)
                wait(act, tt_ps, b)
                nc.scalar.copy(pt2[:, :], pt[2 * HS:3 * HS, :])
                nc.scalar.copy(lt2[:, :], lt[2 * HS:3 * HS, :]).then_inc(tcopy_sb, 1)

            def batch(b, first, last):
                at = schedule(first, last)
                for s in range(last_slot + 1):
                    c = s - L_TURN - 1
                    if c >= 0 and c < SLOTS and c % 2 == 1:
                        i = c % NQ
                        act.wait_ge(att_ps, b * SLOTS + (c + 1))
                        wait(act, pv_ps, b * SLOTS + max(c - NQ + 1, 0))
                        nc.scalar.copy(att_t[:, po[i]:po[i + 1]], ps[:, TP + 1, 0:P * (i + 1)]).then_inc(attt_odd, 1)
                    for kind, i, dt in at[2 * s]:
                        piece(kind, i, b + dt, bank_of(2 * s))
                    if s == SLOTS // 2 and not first:
                        act.wait_ge(o_out, b * (NR * 16))
                    if s < SLOTS:
                        n, i = divmod(s, NQ)
                        nk = P * (i + 1)
                        act.wait_ge(max_sb, b * SLOTS + (s + 1))
                        wait(act, att_ps, b * SLOTS + (s - 2 * NQ + 1 if n >= 2 else 0))
                        for m in range(2):
                            e = nc.scalar.activation(pr[:, n % 2, m, po[i]:po[i] + nk], score_view(i)[:, m, :],
                                                     ACT.Exp, bias=negm[:, n % 2, i, m:m + 1],
                                                     accum_out=lsum[:, n % 2, m, i:i + 1])
                        e.then_inc(exp_sb, 1)
                    if s == TAIL_SLOT + 1 and not last:
                        tail_exp(b + 1)
                    for kind, i, dt in at[2 * s + 1]:
                        piece(kind, i, b + dt, bank_of(2 * s + 1))

            for k, (kind, i, t) in enumerate(prologue):
                piece(kind, i, t, k % 4)
            tail_exp(0)
            batch(0, True, False)
            with act.Fori(1, B - 1) as b:
                batch(b, False, False)
            batch(B - 1, False, True)
            for k, (kind, i) in enumerate(projection_pieces):
                piece(kind, i, B - 1, k % 4)

        @block.vector
        def _(dve):
            nc.vector.memset(mv[:, :, :], 1.0).then_inc(dve_const, 1)
            nc.vector.memset(hid_tok[:, :, 0:1], 0.0).then_inc(dve_const, 1)
            nc.vector.memset(sel[:, :, :, :, :].bitcast(F32), 0.0).then_inc(setup, 1)
            nc.vector.memset(blk[:, :, :], 0.0).then_inc(setup, 1)
            nc.vector.memset(q4[:, :, :, :].bitcast(F32), 0.0).then_inc(dve_const, 1)
            nc.vector.memset(qblk[:, :, :].bitcast(F32), 0.0).then_inc(setup, 1)
            nc.vector.memset(qs[:, :, :, T:T + 1].bitcast(F32), 0.0).then_inc(dve_const, 1)
            nc.vector.memset(ks[:, :, :, T:T + 1].bitcast(F32), 0.0).then_inc(dve_const, 1)
            dve.wait_ge(consts_in, 5 * 16)
            nc.vector.tensor_tensor(lam_in[:, 0:2, :, :], lam_in[:, 0:4:2, :, :], lam_in[:, 1:4:2, :, :], ALU.mult
                                    ).then_inc(setup, 1)
            dve.wait_ge(setup, 4)
            nc.vector.tensor_reduce(lam_s[:, :, :], lam_in[:, 0:2, :, :], AX_X, ALU.add).then_inc(dve_const, 1)
            dve.wait_ge(pool_const, 13)
            nc.vector.tensor_reduce(which[:, :, :], ident[:, :].rearrange("p (j m d) -> p j m d", m=2, d=HS), AX_X,
                                    ALU.add).then_inc(setup, 1)
            for qk, places in enumerate((((0, 1), (2, 3)), ((0, 2), (1, 3)))):
                for part in range(2):
                    for j in range(HG):
                        for c in places[part]:
                            cp = nc.vector.tensor_copy(
                                sel[:, qk, part, j, :].rearrange("p (m c d) -> p m c d", m=2, d=HS)[:, :, c, :],
                                ident[:, 2 * HS * j:2 * HS * (j + 1)].rearrange("p (m d) -> p m d", m=2))
            cp.then_inc(setup, 1)
            dve.wait_ge(setup, 6)
            for g in range(NG):
                for m in range(2):
                    cp = nc.vector.tensor_copy(blk[:, g, 2 * HS * m + HG * g:2 * HS * m + HG * (g + 1)],
                                               which[:, :, m])
            cp.then_inc(setup, 1)
            dve.wait_ge(lam_exp, 1)
            nc.vector.tensor_tensor(neg_lam[:, :], lam_s[:, 1, :], lam_s[:, 0, :], ALU.subtract).then_inc(setup, 1)
            dve.wait_ge(setup, 8)
            nc.vector.tensor_scalar(neg_lam[:, :], neg_lam[:, :], -LAMBDA_INIT, None, ALU.add).then_inc(setup, 1)
            dve.wait_ge(setup, 9)
            nc.vector.tensor_tensor(lam_diag[:, :], neg_lam[0:H, :], ident[0:H, 0:H], ALU.mult).then_inc(setup, 1)
            dve.wait_ge(setup, 10)
            nc.vector.tensor_reduce(neg_lam_col[:, :], lam_diag[:, :], AX_X, ALU.add).then_inc(setup, 1)
            for n, (_, dst) in enumerate(wt_jobs):
                if n % 2 == 1:
                    dve.wait_ge(wt_ps, n + 1)
                    nc.vector.tensor_copy(dst, ps[:, n % 8, 0:P]).then_inc(wt_odd, 1)
            dve.wait_ge(setup, 11)

            def piece(kind, i, t, bank):
                src = ps[:, bank, :]
                if kind == "gu":
                    c, half = divmod(i, 2)
                    dve.wait_ge(gate_sb, t * GU + (i + 1))
                    wait(dve, to_ps, t * NR)
                    nc.vector.tensor_tensor(hid_tok[:, c, 1 + S // 2 * half:1 + S // 2 * (half + 1)], gate[:, i % 2, :],
                                            src[:, S // 2:S], ALU.mult).then_inc(hid_sb, 1)
                elif kind == "to":
                    m = rn[i]
                    dve.wait_ge(to_ps, t * NR + (i + 1))
                    wait(dve, h_out, t * (NR * 16))
                    nc.vector.tensor_copy(h[0:m, i, :], src[0:m, 0:D]).then_inc(h_sb, 1)
                    dve.wait_ge(h_sb, t * NR + (i + 1))
                    nc.vector.bn_stats(st6[0:m, i, :], h[0:m, i, :]).then_inc(st_sb, 1)
                    if i == NR - 1:
                        dve.wait_ge(st_sb, t * NR + NR)
                        nc.vector.memset(unused[:, :], 0.0)
                        for j in range(NR):
                            nc.vector.bn_aggr(mv[0:rn[j], j, :], st6[0:rn[j], j, :]).then_inc(mv_sb, 1)
                elif kind == "qk":
                    g = i // 2
                    dst = (qs, ks)[i % 2]
                    dve.wait_ge(hi_sb, t * (2 * NG) + (i + 1))
                    nc.vector.scalar_tensor_tensor(out=dst[:, 1, g, 0:S], in0=src, scalar=(HS ** -0.5, 1.0)[i % 2],
                                                   in1=dst[:, 0, g, 0:S].bitcast(F32), op0=ALU.mult,
                                                   op1=ALU.subtract).then_inc(lo_sb, 1)
                elif kind == "qkt":
                    dve.wait_ge(qkt_hi, t + 1)
                    for dst, a, sc in ((qs, 0, HS ** -0.5), (ks, NG, 1.0)):
                        lo = nc.vector.scalar_tensor_tensor(
                            out=dst[:, 1, :, S:T].rearrange("p g n -> p (g n)"), in0=src[:, a:a + NG], scalar=sc,
                            in1=dst[:, 0, :, S:T].bitcast(F32).rearrange("p g n -> p (g n)"), op0=ALU.mult,
                            op1=ALU.subtract)
                    lo.then_inc(qkt_lo, 1)
                    dve.wait_ge(qkt_lo, t + 1)
                    for part in range(2):
                        for g in range(NG):
                            q = nc.vector.tensor_scalar(qblk[:, part, TC * g:TC * (g + 1)], blk[:, g, :],
                                                        qs[:, part, g, S:T].bitcast(F32), None, ALU.mult)
                    q.then_inc(qblk_sb, 1)
                elif kind == "rp" and i % 2 == 1:
                    n = i // 2
                    dve.wait_ge(rp_ps, t * (2 * H) + (i + 1))
                    wait(dve, s_ps, t * SLOTS + NQ * (n - 1))
                    nc.vector.tensor_copy(k4[:, n % 2, :], src).then_inc(rpk_sb, 1)
                elif kind == "tt":
                    dve.wait_ge(tt_ps, t + 1)
                    nc.vector.tensor_copy(att_tail[:, 0:NQ * H], src[:, 0:NQ * H])
                    nc.vector.tensor_copy(att_tail[0:1, NQ * H:NR * H], src[0:1, NQ * H:NR * H]).then_inc(tt_sb, 1)
                elif kind == "tv":
                    dve.wait_ge(tv_ps, t + 1)
                    nc.vector.tensor_tensor(tm[:, :], own_head[:, :], src[0:H, :], ALU.mult).then_inc(tm_sb, 1)
                elif kind == "ty":
                    dve.wait_ge(ty_ps, t + 1)
                    nc.vector.tensor_copy(ytail[:, :, :].rearrange("p h d -> p (h d)"), src[0:1, :]
                                          ).then_inc(ty_sb, 1)

            def normalise(t, i):
                m = rn[i]
                dve.wait_ge(rs_sb, t + 1)
                wait(dve, xht_ps, t * NR + max(i - 1, 0))
                nc.vector.tensor_scalar(xh[0:m, i % 2, :], h[0:m, i, :], mv[0:m, i, 0:1], rs[0:m, i:i + 1],
                                        ALU.subtract, ALU.mult).then_inc(xh_sb, 1)

            def tail_max(b):
                dve.wait_ge(ts_ps, b + 1)
                nc.vector.tensor_reduce(negt[:, :], ps[0:TC, 0:2, :].rearrange("p k n -> p (k n)")[:, 0:T], AX_X,
                                        ALU.max, negate=True).then_inc(tmax_sb, 1)

            def tail_combine(b):
                dve.wait_ge(tcopy_sb, b + 1)
                nc.vector.reciprocal(rt[:, 0:1], lt[0:H, :]).then_inc(tstep, 1)
                nc.vector.reciprocal(rt[:, 1:2], lt2[:, :]).then_inc(tstep, 1)
                dve.wait_ge(tstep, b * 4 + 2)
                nc.vector.tensor_tensor(ct[:, :], rt[:, 1:2], neg_lam_col[:, :], ALU.mult).then_inc(tstep, 1)
                dve.wait_ge(tstep, b * 4 + 3)
                nc.vector.tensor_scalar(pt2[:, :], pt2[:, :], ct[:, 0:1], None, ALU.mult).then_inc(tstep, 1)
                dve.wait_ge(tstep, b * 4 + 4)
                nc.vector.scalar_tensor_tensor(out=pt2[:, :], in0=pt[0:H, :], scalar=rt[:, 0:1], in1=pt2[:, :],
                                               op0=ALU.mult, op1=ALU.add).then_inc(tatt_sb, 1)

            def coefs(b, n):
                dve.wait_ge(exp_sb, b * SLOTS + NQ * (n + 1))
                nc.vector.reciprocal(rc[:, n % 2, :, :], lsum[:, n % 2, :, :]).then_inc(coef_sb, 1)
                dve.wait_ge(coef_sb, b * (2 * H) + (2 * n + 1))
                nc.vector.scalar_tensor_tensor(out=coef[:, n % 2, :], in0=lsum[:, n % 2, 0, :],
                                               scalar=neg_lam[:, n:n + 1], in1=rc[:, n % 2, 1, :], op0=ALU.mult,
                                               op1=ALU.mult).then_inc(coef_sb, 1)
                dve.wait_ge(coef_sb, b * (2 * H) + (2 * n + 2))

            def take_y(b, n):
                dve.wait_ge(pv_ps, b * SLOTS + NQ * (n + 1))
                nc.vector.tensor_tensor(yraw[:, NQ * (n % HG):NQ * (n % HG + 1), :],
                                        ps[:, YB, 0:NQ * VD].rearrange("p (i d) -> p i d", d=VD),
                                        rc[:, n % 2, 0, :].unsqueeze(2).to_broadcast([P, NQ, VD]), ALU.mult
                                        ).then_inc(y_sb, 1)

            def centre(b, k):
                m = 1 if k == 0 else P
                c = b * (3 * NN) + 3 * turn_of[k]
                if k:
                    dve.wait_ge(y_sb, b * H + HG * k)
                else:
                    dve.wait_ge(ty_sb, b + 1)
                src = yraw if k else ytail
                nc.vector.tensor_reduce(ysum[0:m, 0, :], src[0:m, :, :], AX_X, ALU.add).then_inc(nstep, 1)
                dve.wait_ge(nstep, c + 1)
                nc.vector.tensor_scalar(ysum[0:m, 0, :], ysum[0:m, 0, :], 1.0 / VD, None, ALU.mult).then_inc(nstep, 1)
                dve.wait_ge(nstep, c + 2)
                nc.vector.tensor_tensor(y[0:m, :, :], src[0:m, :, :],
                                        ysum[0:m, 0, :].unsqueeze(2).to_broadcast([m, HG * NQ, VD]), ALU.subtract
                                        ).then_inc(yc_sb, 1)

            def spread(b, k):
                m = 1 if k == 0 else P
                c = b * (3 * NN) + 3 * turn_of[k]
                dve.wait_ge(ysq_sb, b * NN + (turn_of[k] + 1))
                nc.vector.tensor_reduce(ysum[0:m, 1, :], ysq[0:m, :, :], AX_X, ALU.add).then_inc(nstep, 1)
                dve.wait_ge(nstep, c + 3)
                nc.vector.tensor_scalar(ysum[0:m, 1, :], ysum[0:m, 1, :], 1.0 / VD, LN_EPS, ALU.mult, ALU.add
                                        ).then_inc(yvar_sb, 1)

            def scale_y(b, k):
                m = 1 if k == 0 else P
                dve.wait_ge(yrs_sb, b * NN + (turn_of[k] + 1))
                nc.vector.tensor_scalar(yrs[0:m, :], yrs[0:m, :], 1.0 - LAMBDA_INIT, None, ALU.mult
                                        ).then_inc(yrs_scaled, 1)
                dve.wait_ge(yrs_scaled, b * NN + (turn_of[k] + 1))
                if turn_of[k] == 0:
                    wait(dve, yt_ps, b * NR)
                if k == 0:
                    nc.vector.tensor_tensor(yn[0:1, NQ, :].rearrange("p (h d) -> p h d", d=VD), y[0:1, :, :],
                                            yrs[0:1, :].unsqueeze(2).to_broadcast([1, HG * NQ, VD]), ALU.mult
                                            ).then_inc(yn_sb, 1)
                    return
                for j in range(HG):
                    hd = HG * (k - 1) + j
                    last = nc.vector.tensor_tensor(
                        yn[:, 0:NQ, VD * hd:VD * (hd + 1)], y[:, NQ * j:NQ * (j + 1), :],
                        yrs[:, NQ * j:NQ * (j + 1)].unsqueeze(2).to_broadcast([P, NQ, VD]), ALU.mult)
                last.then_inc(yn_sb, 1)

            def batch(b, first, last):
                at = schedule(first, last)
                for s in range(last_slot + 1):
                    c = s - L_TURN - 1
                    if c >= 0 and c < SLOTS and c % 2 == 0:
                        i = c % NQ
                        dve.wait_ge(att_ps, b * SLOTS + (c + 1))
                        wait(dve, pv_ps, b * SLOTS + max(c - NQ + 1, 0))
                        nc.vector.tensor_copy(att_t[:, po[i]:po[i + 1]], ps[:, TP, 0:P * (i + 1)]
                                              ).then_inc(attt_even, 1)
                    if s < SLOTS:
                        n, i = divmod(s, NQ)
                        dve.wait_ge(s_ps, b * SLOTS + (s + 1))
                        nc.vector.tensor_reduce(negm[:, n % 2, i, :], score_view(i), AX_X, ALU.max, negate=True
                                                ).then_inc(max_sb, 1)
                    for kind, i, dt in at[2 * s]:
                        piece(kind, i, b + dt, bank_of(2 * s))
                    c = s - L_ATT
                    if c >= 0 and c < SLOTS:
                        n, i = divmod(c, NQ)
                        if i == 0:
                            coefs(b, n)
                        cut = slice(po[i], po[i + 1])
                        nc.vector.scalar_tensor_tensor(out=pr[:, n % 2, 0, cut], in0=pr[:, n % 2, 1, cut],
                                                       scalar=coef[:, n % 2, i:i + 1], in1=pr[:, n % 2, 0, cut],
                                                       op0=ALU.mult, op1=ALU.add).then_inc(att_sb, 1)
                    if not last:
                        if s == TAIL_SLOT:
                            tail_max(b + 1)
                        if s == TAIL_SLOT + 2:
                            tail_combine(b + 1)
                    for kind, i, dt in at[2 * s + 1]:
                        piece(kind, i, b + dt, bank_of(2 * s + 1))
                    if s >= L_PV + NQ - 1 and (s - L_PV) % NQ == NQ - 1:
                        take_y(b, (s - L_PV) // NQ)
                    if not last:
                        for i in range(NR):
                            if norm_rows[i] == s:
                                normalise(b + 1, i)
                    if not first:
                        if s == 0:
                            centre(b - 1, NG)
                        if s == 1:
                            spread(b - 1, NG)
                        if s == NORM_Y - 1:
                            scale_y(b - 1, NG)
                    for k in range(NG):
                        if s == centre_slot[k]:
                            centre(b, k)
                        if s == centre_slot[k] + 1:
                            spread(b, k)
                        if s == centre_slot[k] + 3:
                            scale_y(b, k)

            for k, (kind, i, t) in enumerate(prologue):
                if kind == "xh":
                    normalise(t, i)
                piece(kind, i, t, k % 4)
            tail_max(0)
            tail_combine(0)
            batch(0, True, False)
            with dve.Fori(1, B - 1) as b:
                batch(b, False, False)
            batch(B - 1, False, True)
            centre(B - 1, NG)
            spread(B - 1, NG)
            scale_y(B - 1, NG)

        @block.tensor
        def _(pe):
            pe.wait_ge(pool_const, 13)
            for n, (raw, _) in enumerate(wt_jobs):
                if n % (DC * EC) == 0:
                    pe.wait_ge(wtok_in[n // (DC * EC)], 16)
                if n >= 8:
                    pe.wait_ge(wt_even if n % 2 == 0 else wt_odd, n // 2 - 3)
                nc.tensor.transpose(ps[:, n % 8, 0:P], raw, ident[:, :]).then_inc(wt_ps, 1)
            pe.wait_ge(wt_even, len(wt_jobs) // 2)
            pe.wait_ge(wt_odd, len(wt_jobs) // 2)
            pe.wait_ge(dve_const, 6)
            pe.wait_ge(consts_in, 5 * 16)
            pe.wait_ge(setup, 7)

            def take_waits(dst):
                nc.tensor.matmul(dst[0:32, 0:2], ident[:, 0:32], ident[:, 0:2], start=True, stop=True)

            def piece(kind, i, t, bank):
                dst = ps[:, bank, :]
                if kind == "x":
                    pe.wait_ge(x_in, t * 16 + 16)
                    for q in range(XT):
                        xv = xraw[:, q, :].rearrange("p (d e) -> p d e", e=E)[:, i * P:(i + 1) * P, 0]
                        last = nc.tensor.transpose(dst[:, q * P:(q + 1) * P], xv, ident[:, :])
                    last.then_inc(x_ps, 1)
                elif kind == "gu":
                    c, half = divmod(i, 2)
                    cols = slice(S // 2 * half, S // 2 * (half + 1))
                    pe.wait_ge(x_sb, t * DC + DC)
                    for k, w in enumerate((w0t, w1t)):
                        for d in range(DC):
                            last = nc.tensor.matmul(dst[:, S // 2 * k:S // 2 * (k + 1)], w[:, d, c * P:(c + 1) * P],
                                                    xt_tok[:, d, cols], start=(d == 0), stop=(d == DC - 1))
                    last.then_inc(gu_ps, 1)
                elif kind == "to":
                    m = rn[i]
                    pe.wait_ge(hid_sb, t * GU + GU)
                    for c in range(EC):
                        last = nc.tensor.matmul(dst[0:m, 0:D], hid_tok[:, c, P * i:P * i + m], wot[:, c, :],
                                                start=(c == 0), stop=(c == EC - 1 and i > 0))
                    if i == 0:
                        last = nc.tensor.matmul(dst[0:m, 0:D], first_row[0:1, 0:m], cls_row[0:1, :], start=False,
                                                stop=True)
                    last.then_inc(to_ps, 1)
                elif kind == "xh":
                    m = rn[i]
                    pe.wait_ge(xh_sb, t * NR + (i + 1))
                    if m < P:
                        take_waits(dst)
                    for c in range(DC):
                        last = nc.tensor.transpose(dst[:, c * m:(c + 1) * m], xh[0:m, i % 2, c * P:(c + 1) * P],
                                                   ident[0:m, 0:m])
                    last.then_inc(xht_ps, 1)
                elif kind == "qk":
                    g = i // 2
                    w = (wq, wk)[i % 2]
                    pe.wait_ge(xht_sb, t * NR + NR)
                    for d in range(DC):
                        last = nc.tensor.matmul(dst, w[:, d, g * P:(g + 1) * P], xt[:, d, 0:S],
                                                start=(d == 0), stop=(d == DC - 1))
                    last.then_inc(qk_ps, 1)
                elif kind == "qkt":
                    pe.wait_ge(xht_sb, t * NR + NR)
                    for j in range(2 * NG):
                        w, g = ((wq, wk)[j // NG], j % NG)
                        for d in range(DC):
                            last = nc.tensor.matmul(dst[:, j:j + 1], w[:, d, g * P:(g + 1) * P], xt[:, d, S:T],
                                                    start=(d == 0), stop=(d == DC - 1))
                    last.then_inc(qkt_ps, 1)
                elif kind == "v":
                    m = rn[i]
                    for d in range(DC):
                        last = nc.tensor.matmul(dst[0:m, :], xt[:, d, P * i:P * i + m], wv[:, d, :],
                                                start=(d == 0), stop=(d == DC - 1))
                    last.then_inc(v_ps, 1)
                elif kind == "rp":
                    n, qk = divmod(i, 2)
                    g, j = divmod(n, HG)
                    src = (qs, ks)[qk]
                    pe.wait_ge(lo_sb, t * (2 * NG) + (2 * g + qk + 1))
                    for part in range(2):
                        last = nc.tensor.matmul(dst, sel[:, qk, part, j, :], src[:, part, g, 0:S],
                                                start=(part == 0), stop=(part == 1))
                    last.then_inc(rp_ps, 1)
                elif kind == "tt":
                    pe.wait_ge(tatt_sb, t + 1)
                    take_waits(dst)
                    for j in range(NR):
                        last = nc.tensor.transpose(dst[0:rn[j], H * j:H * (j + 1)], pt2[:, P * j:P * j + rn[j]],
                                                   ident[0:H, 0:H])
                    last.then_inc(tt_ps, 1)
                elif kind == "tv":
                    pe.wait_ge(tt_sb, t + 1)
                    pe.wait_ge(v_sb, t * NR + NR)
                    for j in range(NR):
                        last = nc.tensor.matmul(dst[0:H, :], att_tail[0:rn[j], H * j:H * (j + 1)], v[0:rn[j], j, :],
                                                start=(j == 0), stop=(j == NR - 1))
                    last.then_inc(tv_ps, 1)
                elif kind == "ty":
                    pe.wait_ge(tm_sb, t + 1)
                    take_waits(dst)
                    nc.tensor.matmul(dst[0:1, :], ones[0:H, :], tm[:, :], start=True, stop=True).then_inc(ty_ps, 1)
                elif kind == "yt":
                    m = rn[i]
                    pe.wait_ge(yn_sb, t * NN + NN)
                    if m < P:
                        take_waits(dst)
                    for c in range(H * VD // P):
                        last = nc.tensor.transpose(dst[:, c * m:(c + 1) * m], yn[0:m, i, c * P:(c + 1) * P],
                                                   ident[0:m, 0:m])
                    last.then_inc(yt_ps, 1)
                elif kind == "pc":
                    m = rn[i]
                    pe.wait_ge(yt_sb, t * NR + (i + 1))
                    for c in range(H * VD // P):
                        last = nc.tensor.matmul(dst[0:m, 0:D], yt[:, i % 2, c, 0:m], wc[:, c, :],
                                                start=(c == 0), stop=(c == H * VD // P - 1))
                    last.then_inc(pc_ps, 1)

            def tail_scores(b):
                wait(pe, exp_sb, b * SLOTS)
                pe.wait_ge(qblk_sb, b + 1)
                pe.wait_ge(lo_sb, b * (2 * NG) + 2 * NG)
                for a, z, bank in ((0, S, 0), (S, T + 1, 1)):
                    for g in range(NG):
                        for k in range(4):
                            last = nc.tensor.matmul(ps[:, bank, 0:z - a], qblk[:, k // 2, TC * g:TC * g + P],
                                                    ks[:, k % 2, g, a:z], start=(g == 0 and k == 0),
                                                    stop=(g == NG - 1 and k == 3))
                last.then_inc(ts_ps, 1)

            before = {}

            def bank_free(b, bank):
                if before.get(bank) is not None:
                    kind, i, dt = before[bank]
                    ready, value = left(kind, i, b + dt)
                    pe.wait_ge(ready, value)
                    before[bank] = None

            def scores(b, s):
                n, i = divmod(s, NQ)
                nk = P * (i + 1)
                if s >= 2:
                    pe.wait_ge(exp_sb, b * SLOTS + (s - 1))
                else:
                    pe.wait_ge(texp_sb, b + 1)
                if i == 0:
                    pe.wait_ge(rpq_sb, b * H + (n + 1))
                    pe.wait_ge(rpk_sb, b * H + (n + 1))
                bank_free(b, {2: 1, 3: 3}.get(i))
                dst = score_view(i)
                for m in range(2):
                    nc.tensor.matmul(dst[:, m, :], q4[:, n % 2, m, P * i:P * (i + 1)], k4[:, n % 2, 0:nk],
                                     start=True, stop=False)
                    last = nc.tensor.matmul(dst[:, m, P * i:nk], identb[:, :], causal[:, :], start=False, stop=True)
                last.then_inc(s_ps, 1)

            def turn(b, c):
                n, i = divmod(c, NQ)
                pe.wait_ge(att_sb, b * SLOTS + (c + 1))
                wait(pe, attt_even if c % 2 == 0 else attt_odd, b * (SLOTS // 2) + c // 2)
                for j in range(i + 1):
                    last = nc.tensor.transpose(ps[:, TP + c % 2, P * j:P * (j + 1)],
                                               pr[:, n % 2, 0, po[i] + P * j:po[i] + P * (j + 1)], ident[:, :])
                last.then_inc(att_ps, 1)

            def values(b, c):
                n, i = divmod(c, NQ)
                pe.wait_ge(attt_even if c % 2 == 0 else attt_odd, b * (SLOTS // 2) + (c // 2 + 1))
                if n == 0:
                    pe.wait_ge(v_sb, b * NR + (i + 1))
                if i == 0:
                    wait(pe, y_sb, b * H + n)
                for j in range(i + 1):
                    last = nc.tensor.matmul(ps[:, YB, VD * i:VD * (i + 1)], att_t[:, po[i] + P * j:po[i] + P * (j + 1)],
                                            v[:, j, VD * n:VD * (n + 1)], start=(j == 0), stop=(j == i))
                last.then_inc(pv_ps, 1)

            def run(kind, i, b, dt, bank):
                bank_free(b, bank)
                before[bank] = (kind, i, dt)
                piece(kind, i, b + dt, bank)

            def batch(b, first, last):
                at = schedule(first, last)
                for s in range(last_slot + 1):
                    if s < SLOTS:
                        scores(b, s)
                    if s == TAIL_SLOT and not last:
                        tail_scores(b + 1)
                    for kind, i, dt in at[2 * s]:
                        run(kind, i, b, dt, bank_of(2 * s))
                    if s >= L_PV:
                        values(b, s - L_PV)
                    if s >= L_TURN and s - L_TURN < SLOTS:
                        turn(b, s - L_TURN)
                    for kind, i, dt in at[2 * s + 1]:
                        run(kind, i, b, dt, bank_of(2 * s + 1))

            for k, (kind, i, t) in enumerate(prologue):
                if k >= 4:
                    k2, i2, t2 = prologue[k - 4]
                    s2, v2 = left(k2, i2, t2)
                    pe.wait_ge(s2, v2)
                if kind == "qkt" and k:
                    pe.wait_ge(wattn_in, (2 * 2 * DC + 2) * 16)
                piece(kind, i, t, k % 4)
            for k2, i2, t2 in prologue[-4:]:
                s2, v2 = left(k2, i2, t2)
                pe.wait_ge(s2, v2)
            tail_scores(0)
            batch(0, True, False)
            kind, i, dt = last_piece
            with pe.Fori(1, B - 1) as b:
                before[BG] = (kind, i, dt - 1)
                batch(b, False, False)
            before[BG] = (kind, i, dt - 1)
            batch(B - 1, False, True)
            for k, (kind, i) in enumerate(projection_pieces):
                run(kind, i, B - 1, 0, k % 4)

    with ExitStack() as ctx:
        def sb(name, shape, dt=F32):
            return ctx.enter_context(nc.sbuf_tensor(name, shape, dt))

        def sem(name):
            return ctx.enter_context(nc.semaphore(name))

        ps = ctx.enter_context(nc.psum_tensor("ps2", [P, 8, 512], F32))

        ident = sb("ident2", [P, P])
        half = sb("half", [P, NT])
        zeros = sb("zeros", [P, DC * I + D])
        lower = sb("lower", [P, G, G])
        bias = sb("bias", [P, NX])
        rw_raw = sb("rw_raw", [P, D])
        rw_t = sb("rw_t", [P, DC, NX])
        acc = sb("acc", [P, NT, D])
        oacc = sb("oacc", [P, NT, D])
        st6 = sb("st62", [P, NT, 6])
        mv = sb("mv2", [P, NT, 2])
        rs = sb("rs2", [P, NT])
        NX2 = 4
        x2 = sb("x2", [P, NX2, D])
        x2t = sb("x2t", [P, DC, N])
        score = sb("score", [P, NT, NX])
        sfc = sb("sfc", [P, NT, NX])
        eq = sb("eq", [P, NT, NX])
        rest = sb("rest", [P, NT, NX])
        g1 = sb("g1", [P, NT, G])
        g2 = sb("g2", [P, NT, G])
        gc = sb("gc", [P, NT, G])
        top8 = sb("top8", [P, NT, 8])
        wsum = sb("wsum", [P, NT])
        comb = sb("comb", [P, NX, NT])
        cur = sb("cur", [P, 2, NT])
        WC = DC * I + D
        UPW = slice(0, DC * I)
        DNW = slice(DC * I, WC)
        wr = sb("wr", [P, NS + 2, WC])
        wh = sb("wh", [P, NS + 2, WC], F32R)
        wl = sb("wl", [P, NS + 2, WC], F32R)
        x2h = sb("x2h", [P, DC, N], F32R)
        x2l = sb("x2l", [P, DC, N], F32R)
        r = sb("r", [P, 2, u0[NU] - u0[NU - 1]])
        hid = sb("hid", [P, 2, N])
        hid_h = sb("hid_h", [P, 2, P * NT], F32R)
        hid_l = sb("hid_l", [P, 2, P * NT], F32R)

        w_in = sem("w_in")
        h2_in = [sem(f"h2_in{k}") for k in range(-(-NT // 4))]
        shared_in = sem("shared_in")
        up_in = [sem(f"up_in{k}") for k in range(2)]
        down_in = [sem(f"down_in{k}") for k in range(2)]
        uph_sb = sem("uph_sb")
        upl_sb = sem("upl_sb")
        downh_sb = sem("downh_sb")
        downl_sb = sem("downl_sb")
        x2h_sb = sem("x2h_sb")
        x2l_sb = sem("x2l_sb")
        sq_sb = sem("sq_sb")
        hidh_sb = sem("hidh_sb")
        hidl_sb = sem("hidl_sb")
        shared_hidl_sb = sem("shared_hidl_sb")
        pad_sb = sem("pad_sb")
        pool_c2 = sem("pool_c2")
        clear_sb = sem("clear_sb")
        sum_sb = sem("sum_sb")
        st_sb = sem("st_sb2")
        mv_sb = sem("mv_sb2")
        veps_sb = sem("veps_sb2")
        rs_sb = sem("rs_sb2")
        x2_sb = sem("x2_sb")
        x2_ps = sem("x2_ps")
        rw_ps = sem("rw_ps")
        rw_sb = sem("rw_sb")
        logit_ps = sem("logit_ps")
        sig_sb = sem("sig_sb")
        route = sem("route")
        cur_sb = sem("cur_sb")
        up_ps = sem("up_ps")
        relu_sb = sem("relu_sb")
        down_ps = sem("down_ps")
        acc_sb = sem("acc_sb")
        out_done = sem("out_done")

        UP = 0
        DN = 5
        LG = 5
        SHARED_PAIRS = NS // 2
        full = N // P
        LB = 512 // NX
        logit_banks = [(a, min(a + LB, full)) for a in range(0, full, LB)] + ([(full, NT)] if full < NT else [])
        chunks = [(a, min(a + 4, full)) for a in range(0, full, 4)]
        pieces = [list(range(a, z)) for a, z in chunks] + ([[full]] if full < NT else [])

        block = ctx.enter_context(nc.Block())

        @block.sync
        def _(sp):
            for k, (a, z) in enumerate(chunks):
                for src, dst in ((h_dram, acc), (o_dram, oacc)):
                    sp.dma_start(dst[:, a:z, :], src[P * a:P * z, :].rearrange("(t p) d -> p t d", p=P)
                                 ).then_inc(h2_in[k], 16)
                if k == 0:
                    sp.dma_start(rw_raw[0:NX, :], router_w).then_inc(w_in, 16)
                    sp.dma_start(bias[:, :], correction_bias.partition_broadcast(P)).then_inc(w_in, 16)
            if full < NT:
                sp.wait_ge(clear_sb, 1)
                for src, dst in ((h_dram, acc), (o_dram, oacc)):
                    sp.dma_start(dst[0:tn[full], full, :], src[P * full:N, :]).then_inc(h2_in[-1], 16)
            for c in range(DC):
                sp.dma_start(wr[:, 0:NS, I * c:I * (c + 1)],
                             shared_up_w[P * c:P * (c + 1), :].rearrange("p (n i) -> p n i", i=I)
                             ).then_inc(shared_in, 16)
            sp.dma_start(wr[:, 0:NS, DC * I:WC], shared_down_w.rearrange("(n p) d -> p n d", p=P)
                         ).then_inc(shared_in, 16)

            def load_up(e, k):
                sp.dma_start(wr[:, NS + k, UPW].rearrange("p (c i) -> p c i", c=DC),
                             up_w[bass.ds(e, 1)].rearrange("a (c p) i -> p (a c) i", p=P)
                             ).then_inc(up_in[k], 16)

            def load_down(e, k):
                sp.dma_start(wr[:, NS + k, DNW], down_w[bass.ds(e, 1)].rearrange("a i d -> i (a d)")
                             ).then_inc(down_in[k], 16)

            for k in range(2):
                load_up(k, k)
                load_down(k, k)
            with sp.Fori(0, NX // 2 - 1) as j:
                e = j * 2
                for k in range(2):
                    sp.wait_ge(upl_sb, e + (NS + k + 1))
                    load_up(e + (2 + k), k)
                    sp.wait_ge(downl_sb, e + (NS + k + 1))
                    load_down(e + (2 + k), k)
            for k, (a, z) in enumerate(chunks):
                sp.wait_ge(acc_sb, (SHARED_PAIRS + NX - 1) * NP + -(-z // 2))
                sp.dma_start(out_rows[P * a:P * z, :].rearrange("(t p) d -> p t d", p=P), acc[:, a:z, :]
                             ).then_inc(out_done, 16)
            if full < NT:
                sp.wait_ge(acc_sb, (SHARED_PAIRS + NX) * NP)
                sp.dma_start(out_rows[P * full:N, :], acc[0:tn[full], full, :]).then_inc(out_done, 16)
            sp.wait_ge(out_done, 16 * (len(chunks) + (full < NT)))

        @block.gpsimd
        def _(pool):
            nc.gpsimd.memset(ident[:, :], 0.0).then_inc(pool_c2, 1)
            nc.gpsimd.memset(half[:, :], -0.5).then_inc(pool_c2, 1)
            nc.gpsimd.memset(lower[:, :, :], 0.0).then_inc(pool_c2, 1)
            nc.gpsimd.memset(zeros[:, :], 0.0).then_inc(pool_c2, 1)
            pool.wait_ge(pool_c2, 4)
            nc.gpsimd.affine_select(out=ident[:, :], in_=ident[:, :], compare_op=ALU.not_equal, fill=1.0,
                                    base=0, pattern=[[-1, P]], channel_multiplier=1).then_inc(pool_c2, 1)
            nc.gpsimd.affine_select(out=lower[:, :, :], in_=lower[:, :, :], compare_op=ALU.is_ge, fill=1.0,
                                    base=0, pattern=[[-1, G], [1, G]], channel_multiplier=0).then_inc(pool_c2, 1)
            for k in range(len(pieces)):
                a, z = pieces[k][0], pieces[k][-1] + 1
                pool.wait_ge(mv_sb, z)
                nc.gpsimd.tensor_scalar(rs[:, a:z], mv[:, a:z, 1], LN_EPS, None, ALU.add).then_inc(veps_sb, 1)
                pool.wait_ge(veps_sb, k + 1)
                nc.gpsimd.tensor_tensor(rs[:, a:z], rs[:, a:z], half[:, a:z], ALU.pow).then_inc(rs_sb, 1)

            def split_up(n, slot):
                nc.gpsimd.tensor_tensor(wh[:, slot, UPW], wr[:, slot, UPW], zeros[:, UPW], ALU.add
                                        ).then_inc(uph_sb, 1)
                pool.wait_ge(uph_sb, n + 1)
                nc.gpsimd.tensor_tensor(wl[:, slot, UPW], wr[:, slot, UPW], wh[:, slot, UPW].bitcast(F32),
                                        ALU.subtract).then_inc(upl_sb, 1)

            def split_down(n, slot):
                nc.gpsimd.tensor_tensor(wh[:, slot, DNW], wr[:, slot, DNW], zeros[:, 0:D], ALU.add
                                        ).then_inc(downh_sb, 1)
                pool.wait_ge(downh_sb, n + 1)
                nc.gpsimd.tensor_tensor(wl[:, slot, DNW], wr[:, slot, DNW], wh[:, slot, DNW].bitcast(F32),
                                        ALU.subtract).then_inc(downl_sb, 1)

            pool.wait_ge(shared_in, (DC + 1) * 16)
            split_up(0, 0)
            for t in range(NT):
                cols = slice(P * t, P * t + tn[t])
                pool.wait_ge(x2h_sb, t + 1)
                nc.gpsimd.tensor_tensor(x2l[:, :, cols], x2t[:, :, cols], x2h[:, :, cols].bitcast(F32), ALU.subtract
                                        ).then_inc(x2l_sb, 1)

            def low(n):
                for u in range(NU):
                    cols = slice(u0[u], u0[u + 1])
                    pool.wait_ge(hidh_sb, n * NU + (u + 1))
                    if n >= 2:
                        pool.wait_ge(down_ps, n // 2 * NP)
                    nc.gpsimd.tensor_tensor(hid_l[:, n % 2, cols], hid[:, n % 2, cols],
                                            hid_h[:, n % 2, cols].bitcast(F32), ALU.subtract
                                            ).then_inc(shared_hidl_sb, 1)

            pool.wait_ge(pad_sb, 2)
            split_down(0, 0)
            split_up(1, 1)
            for n in range(NS):
                if n + 2 < NS:
                    split_up(n + 2, n + 2)
                else:
                    k = n + 2 - NS
                    pool.wait_ge(up_in[k], 16)
                    split_up(NS + k, NS + k)
                low(n)
                if n + 1 < NS:
                    split_down(n + 1, n + 1)
            for k in range(2):
                pool.wait_ge(down_in[k], 16)
                split_down(NS + k, NS + k)
            with pool.Fori(0, NX // 2 - 1) as j:
                e = j * 2 + 2
                for k in range(2):
                    pool.wait_ge(up_in[k], e * 8 + 16)
                    pool.wait_ge(up_ps, (e + (NS - 1 + k)) * NU)
                    split_up(e + (NS + k), NS + k)
                    pool.wait_ge(down_in[k], e * 8 + 16)
                    pool.wait_ge(down_ps, (e + (SHARED_PAIRS - 1 + k)) * NP)
                    split_down(e + (NS + k), NS + k)

        @block.scalar
        def _(act):
            act.wait_ge(rw_ps, 1)
            nc.scalar.copy(rw_t[:, :, :], ps[:, 7, 0:DC * NX].rearrange("p (c n) -> p c n", c=DC)).then_inc(rw_sb, 1)
            for t in range(NT):
                n = tn[t]
                act.wait_ge(x2_ps, t + 1)
                nc.scalar.copy(x2t[:, :, P * t:P * t + n],
                               ps[:, UP + t % 2, 0:DC * n].rearrange("p (c n) -> p c n", c=DC))
                nc.scalar.copy(x2h[:, :, P * t:P * t + n],
                               ps[:, UP + t % 2, 0:DC * n].rearrange("p (c n) -> p c n", c=DC)).then_inc(x2h_sb, 1)
            act.wait_ge(clear_sb, 2)
            for a, z in logit_banks:
                act.wait_ge(logit_ps, z)
                m = tn[a]
                nc.scalar.activation(score[0:m, a:z, :].rearrange("p t e -> p (t e)"),
                                     ps[0:m, LG + a // LB, NX * (a % LB):NX * (a % LB) + NX * (z - a)], ACT.Exp,
                                     scale=-1.0).then_inc(sig_sb, 1)

            def expert(n, k):
                def square(u):
                    act.wait_ge(relu_sb, n * NU + (u + 1))
                    nc.scalar.activation(hid[:, k, u0[u]:u0[u + 1]], r[:, u % 2, 0:u0[u + 1] - u0[u]], ACT.Square
                                         ).then_inc(sq_sb, 1)

                def high(u):
                    act.wait_ge(sq_sb, n * NU + (u + 1))
                    nc.scalar.copy(hid_h[:, k, u0[u]:u0[u + 1]], hid[:, k, u0[u]:u0[u + 1]]).then_inc(hidh_sb, 1)

                for u in range(NU):
                    act.wait_ge(up_ps, n * NU + (u + 1))
                    wait(act, sq_sb, n * NU + max(u - 1, 0))
                    nc.scalar.activation(r[:, u % 2, 0:u0[u + 1] - u0[u]], ps[:, UP + u, 0:u0[u + 1] - u0[u]], ACT.Relu
                                         ).then_inc(relu_sb, 1)
                    if u >= 1:
                        square(u - 1)
                    if u >= 2:
                        high(u - 2)
                square(NU - 1)
                high(NU - 2)
                high(NU - 1)

            def free_hid(g):
                act.wait_ge(down_ps, g * NP)

            act.wait_ge(pad_sb, 2)
            for n in range(NS):
                if n >= 2:
                    free_hid(n // 2)
                expert(n, n % 2)
            for k in range(2):
                free_hid(SHARED_PAIRS)
                expert(NS + k, k)
            with act.Fori(1, NX // 2) as j:
                for k in range(2):
                    free_hid(j * 2 + (SHARED_PAIRS + k - 1))
                    expert(j * 2 + (NS + k), k)

        @block.vector
        def _(dve):
            nc.vector.memset(mv[:, :, :], 1.0)
            nc.vector.memset(acc[:, full:NT, :], 0.0).then_inc(clear_sb, 1)
            nc.vector.memset(score[:, :, :], 0.0).then_inc(clear_sb, 1)
            for part in (hid_h, hid_l):
                nc.vector.memset(part[:, :, N:P * NT].bitcast(F32), 0.0).then_inc(pad_sb, 1)
            def stats(k):
                dve.wait_ge(h2_in[k], 2 * 16)
                for t in pieces[k]:
                    nc.vector.tensor_tensor(acc[0:tn[t], t, :], acc[0:tn[t], t, :], oacc[0:tn[t], t, :], ALU.add
                                            ).then_inc(sum_sb, 1)
                for t in pieces[k]:
                    dve.wait_ge(sum_sb, t + 1)
                    nc.vector.bn_stats(st6[0:tn[t], t, :], acc[0:tn[t], t, :]).then_inc(st_sb, 1)
                for t in pieces[k]:
                    dve.wait_ge(st_sb, t + 1)
                    nc.vector.bn_aggr(mv[0:tn[t], t, :], st6[0:tn[t], t, :]).then_inc(mv_sb, 1)

            def normalise(k):
                dve.wait_ge(mv_sb, pieces[k][-1] + 1)
                dve.wait_ge(rs_sb, k + 1)
                for t in pieces[k]:
                    if t >= NX2:
                        dve.wait_ge(x2_ps, t - NX2 + 1)
                    n = tn[t]
                    nc.vector.tensor_scalar(x2[0:n, t % NX2, :], acc[0:n, t, :], mv[0:n, t, 0:1], rs[0:n, t:t + 1],
                                            ALU.subtract, ALU.mult).then_inc(x2_sb, 1)

            stats(0)
            for k in range(1, len(pieces)):
                stats(k)
                normalise(k - 1)
            normalise(len(pieces) - 1)

            step = [0]

            def link(ins):
                step[0] += 1
                ins.then_inc(route, 1)
                dve.wait_ge(route, step[0])

            def over(ap, n):
                return ap.unsqueeze(3).to_broadcast([P, NT, G, n])

            grp = sfc[:, :, :].rearrange("p t (g k) -> p t g k", g=G)
            eqg = eq[:, :, :].rearrange("p t (g k) -> p t g k", g=G)
            resg = rest[:, :, :].rearrange("p t (g k) -> p t g k", g=G)

            def group_scores():
                dve.wait_ge(sig_sb, len(logit_banks))
                dve.wait_ge(w_in, 2 * 16)
                dve.wait_ge(pool_c2, 6)
                link(nc.vector.tensor_scalar(score[:, :, :], score[:, :, :], 1.0, None, ALU.add))
                link(nc.vector.reciprocal(score[:, :, :], score[:, :, :]))
                link(nc.vector.tensor_tensor(sfc[:, :, :], score[:, :, :],
                                             bias[:, :].unsqueeze(1).to_broadcast([P, NT, NX]), ALU.add))
                link(nc.vector.tensor_reduce(g1[:, :, :], grp, AX_X, ALU.max))
                link(nc.vector.tensor_tensor(eqg, grp, over(g1[:, :, :], GE), ALU.is_equal))
                link(nc.vector.tensor_reduce(gc[:, :, :], eqg, AX_X, ALU.add))
                link(nc.vector.scalar_tensor_tensor(out=rest[:, :, :].rearrange("p t e -> p (t e)"),
                                                    in0=eq[:, :, :].rearrange("p t e -> p (t e)"), scalar=MASKED,
                                                    in1=sfc[:, :, :].rearrange("p t e -> p (t e)"),
                                                    op0=ALU.mult, op1=ALU.add))
                link(nc.vector.tensor_reduce(g2[:, :, :], resg, AX_X, ALU.max))
                link(nc.vector.tensor_scalar(gc[:, :, :], gc[:, :, :], 1.5, MASKED, ALU.is_lt, ALU.mult))
                link(nc.vector.tensor_tensor(gc[:, :, :], gc[:, :, :], g1[:, :, :], ALU.add))
                link(nc.vector.tensor_tensor(g2[:, :, :], g2[:, :, :], gc[:, :, :], ALU.max))
                link(nc.vector.tensor_tensor(g1[:, :, :], g1[:, :, :], g2[:, :, :], ALU.add))
            def pick_groups():
                ga = over(g1[:, :, :], G)
                gb = g1[:, :, :].unsqueeze(2).to_broadcast([P, NT, G, G])
                link(nc.vector.tensor_tensor(eqg, gb, ga, ALU.is_equal))
                link(nc.vector.tensor_tensor(eqg, eqg, lower[:, :, :].unsqueeze(1).to_broadcast([P, NT, G, G]),
                                             ALU.mult))
                link(nc.vector.tensor_tensor(resg, gb, ga, ALU.is_gt))
                link(nc.vector.tensor_tensor(eq[:, :, :], eq[:, :, :], rest[:, :, :], ALU.add))
                link(nc.vector.tensor_reduce(gc[:, :, :], eqg, AX_X, ALU.add))
                link(nc.vector.tensor_scalar(gc[:, :, :], gc[:, :, :], TOPG - 0.5, None, ALU.is_lt))
                link(nc.vector.tensor_tensor(grp, grp, over(gc[:, :, :], GE), ALU.mult))
                link(nc.vector.tensor_scalar(sfc[:, :, :], sfc[:, :, :], 0.0, None, ALU.add))

            def pick_experts():
                for t in range(NT):
                    top = nc.vector.max(top8[:, t, :], sfc[:, t, :])
                link(top)
                for t in range(NT):
                    rep = nc.vector.match_replace(rest[:, t, :], top8[:, t, :], sfc[:, t, :], MASKED)
                link(rep)
                link(nc.vector.tensor_tensor(eq[:, :, :], rest[:, :, :], sfc[:, :, :], ALU.not_equal))
                link(nc.vector.tensor_tensor(eq[:, :, :], eq[:, :, :], score[:, :, :], ALU.mult))
                link(nc.vector.tensor_reduce(wsum[:, :], eq[:, :, :], AX_X, ALU.add))
                link(nc.vector.tensor_scalar(wsum[:, :], wsum[:, :], 1e-20, None, ALU.add))
                link(nc.vector.reciprocal(wsum[:, :], wsum[:, :]))
                link(nc.vector.tensor_tensor(rest[:, :, :], eq[:, :, :],
                                             wsum[:, :].unsqueeze(2).to_broadcast([P, NT, NX]), ALU.mult))
                link(nc.vector.tensor_scalar(comb[:, :, :].rearrange("p e t -> p t e"), rest[:, :, :], ROUTE_SCALE,
                                             None, ALU.mult))

            def low(n, k):
                for u in range(NU):
                    cols = slice(u0[u], u0[u + 1])
                    dve.wait_ge(hidh_sb, n * NU + (u + 1))
                    nc.vector.tensor_tensor(hid_l[:, k, cols], hid[:, k, cols], hid_h[:, k, cols].bitcast(F32),
                                            ALU.subtract).then_inc(hidl_sb, 1)

            def add(g, k):
                for q in range(NP):
                    dve.wait_ge(down_ps, g * NP + (q + 1))
                    for t in range(2 * q, min(2 * q + 2, NT)):
                        m = tn[t]
                        w = 1.0 if k is None else cur[0:m, k, t:t + 1]
                        last = nc.vector.scalar_tensor_tensor(
                            out=acc[0:m, t, :], in0=ps[0:m, DN + q % 3, D * (t % 2):D * (t % 2 + 1)], scalar=w,
                            in1=acc[0:m, t, :], op0=ALU.mult, op1=ALU.add)
                    last.then_inc(acc_sb, 1)

            group_scores()
            add(0, None)
            pick_groups()
            pick_experts()
            for g in range(1, SHARED_PAIRS):
                dve.wait_ge(acc_sb, g * NP)
                add(g, None)
            low(NS, NS % 2)
            with dve.Fori(0, NX // 2 - 1) as j:
                e = j * 2
                for k in range(2):
                    nc.vector.tensor_copy(cur[:, k, :], comb[:, bass.ds(e + k, 1), :].rearrange("p a t -> p (a t)")
                                          ).then_inc(cur_sb, 1)
                    dve.wait_ge(cur_sb, e + (k + 1))
                    dve.wait_ge(acc_sb, (e + (SHARED_PAIRS + k)) * NP)
                    add(e + (SHARED_PAIRS + k), k)
                    low(e + (NS + k + 1), (NS + k + 1) % 2)
            for k in range(2):
                n = NE - 2 + k
                nc.vector.tensor_copy(cur[:, k, :], comb[:, NX - 2 + k, :]).then_inc(cur_sb, 1)
                dve.wait_ge(cur_sb, NX - 2 + (k + 1))
                g = SHARED_PAIRS + NX - 2 + k
                dve.wait_ge(acc_sb, g * NP)
                add(g, k)
                if k == 0:
                    low(n + 1, (n + 1) % 2)

        @block.tensor
        def _(pe):
            pe.wait_ge(pool_c2, 5)
            pe.wait_ge(w_in, 2 * 16)
            for c in range(DC):
                last = nc.tensor.transpose(ps[:, 7, c * NX:(c + 1) * NX], rw_raw[0:NX, c * P:(c + 1) * P],
                                           ident[0:NX, 0:NX])
            last.then_inc(rw_ps, 1)
            pe.wait_ge(rw_sb, 1)

            def logits(t):
                n = tn[t]
                pe.wait_ge(x2h_sb, t + 1)
                dst = ps[0:n, LG + t // LB, NX * (t % LB):NX * (t % LB + 1)]
                for c in range(DC):
                    last = nc.tensor.matmul(dst, x2t[:, c, P * t:P * t + n], rw_t[:, c, :], start=(c == 0),
                                            stop=(c == DC - 1))
                last.then_inc(logit_ps, 1)

            for t in range(NT):
                n = tn[t]
                pe.wait_ge(x2_sb, t + 1)
                if t >= 2:
                    pe.wait_ge(x2h_sb, t - 1)
                for c in range(DC):
                    last = nc.tensor.transpose(ps[:, UP + t % 2, c * n:(c + 1) * n],
                                               x2[0:n, t % NX2, c * P:(c + 1) * P], ident[0:n, 0:n])
                last.then_inc(x2_ps, 1)
                if t >= 1:
                    logits(t - 1)
            logits(NT - 1)

            def products(dst, pairs):
                for k, (w, x) in enumerate(pairs):
                    last = nc.tensor.matmul(dst, w, x, start=(k == 0), stop=(k == len(pairs) - 1))
                return last

            def up(n, slot):
                pe.wait_ge(upl_sb, n + 1)
                for u in range(NU):
                    cols = slice(u0[u], u0[u + 1])
                    if isinstance(n, int) and n == 0:
                        pe.wait_ge(x2l_sb, upto_x[u])
                    else:
                        pe.wait_ge(relu_sb, (n - 1) * NU + (u + 1))
                    pairs = []
                    for c in range(DC):
                        w = slice(I * c, I * (c + 1))
                        pairs += [(wh[:, slot, w], x2h[:, c, cols]), (wh[:, slot, w], x2l[:, c, cols]),
                                  (wl[:, slot, w], x2h[:, c, cols])]
                    products(ps[:, UP + u, 0:u0[u + 1] - u0[u]], pairs).then_inc(up_ps, 1)

            def down(g, experts, hid_low, value):
                if isinstance(g, int) and g == 0:
                    pe.wait_ge(sig_sb, len(logit_banks))
                for q in range(NP):
                    if isinstance(g, int) and g == 0:
                        if q >= 3:
                            pe.wait_ge(acc_sb, q - 2)
                    else:
                        pe.wait_ge(acc_sb, g * NP + (q - 2))
                    for t in range(2 * q, min(2 * q + 2, NT)):
                        rows = slice(P * t, P * (t + 1))
                        pe.wait_ge(hid_low, value + (upto[t] + 1))
                        pairs = []
                        for k, slot in experts:
                            pairs += [(hid_h[:, k, rows], wh[:, slot, DNW]), (hid_h[:, k, rows], wl[:, slot, DNW]),
                                      (hid_l[:, k, rows], wh[:, slot, DNW])]
                        last = products(ps[:, DN + q % 3, D * (t % 2):D * (t % 2 + 1)], pairs)
                    last.then_inc(down_ps, 1)

            def shared_down(g):
                pe.wait_ge(downl_sb, 2 * g + 2)
                down(g, ((0, 2 * g), (1, 2 * g + 1)), shared_hidl_sb, (2 * g + 1) * NU)

            def routed_down(e, k):
                pe.wait_ge(downl_sb, e + (NS + 1))
                down(e + SHARED_PAIRS, ((k, NS + k),), hidl_sb, e * NU)

            upto_x = [-(-u0[u + 1] // P) for u in range(NU)]
            pe.wait_ge(pad_sb, 2)
            up(0, 0)
            up(1, 1)
            for g in range(SHARED_PAIRS):
                up(2 * g + 2, 2 * g + 2)
                shared_down(g)
                if g + 1 < SHARED_PAIRS:
                    up(2 * g + 3, 2 * g + 3)
            with pe.Fori(0, NX // 2 - 1) as j:
                e = j * 2
                up(e + (NS + 1), NS + 1)
                routed_down(e, 0)
                up(e + (NS + 2), NS)
                routed_down(e + 1, 1)
            up(NE - 1, NS + 1)
            routed_down(NX - 2, 0)
            routed_down(NX - 1, 1)


_INS = ['x', 'cls_tok', 'L0_tok_W0', 'L0_tok_W1', 'L0_tok_Wo', 'L0_attn_Wq1', 'L0_attn_Wq2', 'L0_attn_Wk1',
        'L0_attn_Wk2', 'L0_attn_Wv', 'L0_attn_Wc', 'L0_attn_lq1', 'L0_attn_lk1', 'L0_attn_lq2', 'L0_attn_lk2',
        'L0_ffn_router_w', 'L0_ffn_correction_bias', 'L0_ffn_up_w', 'L0_ffn_down_w', 'L0_ffn_shared_up_w',
        'L0_ffn_shared_down_w']
_OUTS = [((4, 513, 256), 'float32')]


def kernel(**inputs):
    import numpy as _np
    import concourse.bacc as _bacc
    from concourse import mybir as _mybir
    from concourse.bass_utils import run_bass_kernel_spmd as _run

    nc = _bacc.Bacc("TRN2", target_bir_lowering=False, num_devices=1)
    arrays, args = {}, []
    for name in _INS:
        a = _np.ascontiguousarray(inputs[name])
        arrays[f"in_{name}_dram"] = a
        args.append(nc.dram_tensor(f"in_{name}_dram", a.shape, _mybir.dt.from_np(a.dtype), kind="ExternalInput").ap())
    for i, (shape, dtype) in enumerate(_OUTS):
        dt = _mybir.dt.from_np(_np.dtype(dtype))
        args.append(nc.dram_tensor(f"out_{i}_dram", shape, dt, kind="ExternalOutput").ap())
    vit_layer(nc, *args)
    r = _run(nc, [arrays], core_ids=[0])
    got = tuple(r.results[0][f"out_{i}_dram"] for i in range(len(_OUTS)))
    return got[0]
```
